# Optimizing a Trainium2 kernel written in Bass

```python
import numpy as np
import jax
import jax.numpy as jnp

def _softmax(x, axis=-1):
    return jax.nn.softmax(x, axis=axis)

def _gelu(x):
    return jax.nn.gelu(x, approximate=True)

def _silu(x):
    return jax.nn.silu(x)

def _sigmoid(x):
    return jax.nn.sigmoid(x)

def _layernorm(x, axis=-1, eps=1e-05):
    m = jnp.mean(x, axis=axis, keepdims=True)
    v = jnp.var(x, axis=axis, keepdims=True)
    return (x - m) / jnp.sqrt(v + eps)

def _scatter_add(tgt, idx, src, axis=0):
    return tgt.at[idx].add(src)

def _segment_sum(src, seg, n):
    return jax.ops.segment_sum(src, seg, n)
kernel_name = 'mk_metaformer_d2_conv_nchw256_r2_ea43e9'

def setup_inputs(seed: int=0):
    np.random.seed(seed)
    _w = jnp.asarray

    def _rec_inputs():
        import jax
        import jax.numpy as jnp
        _gk = jax.random.key(seed)
        x = -0.000125 + 0.9999 * jax.random.normal(jax.random.fold_in(_gk, 1), (8, 128, 64, 64), jnp.float32)
        return x
    x = _rec_inputs()

    def _L0_conv_setup():
        import jax, jax.numpy as jnp
        import numpy as np
        C = 128
        K = 7
        GC = 32
        G = C // GC
        RED = 4
        EPS = 1e-05
        key = jax.random.key(seed)
        ks = jax.random.split(key, 8)
        B, H, W = (8, 64, 64)
        Cr = C // RED
        x = jax.random.normal(ks[0], (B, C, H, W), jnp.float32)
        w1 = jax.random.normal(ks[1], (Cr, C), jnp.float32) * 0.05
        b1 = jax.random.normal(ks[2], (Cr,), jnp.float32) * 0.01
        bn_gamma = jnp.ones((Cr,), jnp.float32)
        bn_beta = jnp.zeros((Cr,), jnp.float32)
        bn_mean = jax.random.normal(ks[3], (Cr,), jnp.float32) * 0.1
        bn_var = jax.random.uniform(ks[4], (Cr,), jnp.float32, 0.5, 1.5)
        w2 = jax.random.normal(ks[5], (G * K * K, Cr), jnp.float32) * 0.05
        b2 = jax.random.normal(ks[6], (G * K * K,), jnp.float32) * 0.01
        return {'x': x, 'w1': w1, 'b1': b1, 'bn_gamma': bn_gamma, 'bn_beta': bn_beta, 'bn_mean': bn_mean, 'bn_var': bn_var, 'w2': w2, 'b2': b2}
    _L0_conv_all = _L0_conv_setup()
    _L0_conv_in = {k: v for k, v in _L0_conv_all.items() if k in ('w1', 'b1', 'bn_gamma', 'bn_beta', 'bn_mean', 'bn_var', 'w2', 'b2')}
    del _L0_conv_all

    def _L0_ffn_setup():
        import math
        import jax, jax.numpy as jnp
        import numpy as np
        CAPACITY_FACTOR = 1.25
        key = jax.random.key(seed)
        ks = jax.random.split(key, 5)
        B, L, D, F, E = (8, 4096, 128, 512, 8)
        h = jax.random.normal(ks[0], (B, L, D), dtype=jnp.float32)
        gate_w = jax.random.normal(ks[1], (D, E), dtype=jnp.float32) * 0.02
        gate_b = jnp.zeros((E,), dtype=jnp.float32)
        w1 = jax.random.normal(ks[2], (E, D, F), dtype=jnp.float32) * (1.0 / math.sqrt(D))
        b1 = jnp.zeros((E, F), dtype=jnp.float32)
        w2 = jax.random.normal(ks[3], (E, F, D), dtype=jnp.float32) * (1.0 / math.sqrt(F))
        b2 = jnp.zeros((E, D), dtype=jnp.float32)
        return {'h': h, 'gate_w': gate_w, 'gate_b': gate_b, 'w1': w1, 'b1': b1, 'w2': w2, 'b2': b2}
    _L0_ffn_all = _L0_ffn_setup()
    _L0_ffn_in = {k: v for k, v in _L0_ffn_all.items() if k in ('gate_w', 'gate_b', 'w1', 'b1', 'w2', 'b2')}
    del _L0_ffn_all

    def _L1_conv_setup():
        import jax, jax.numpy as jnp
        import numpy as np
        N, CIN, COUT, H, W = (32, 128, 128, 56, 56)
        key = jax.random.key(seed)
        k1, k2, k3 = jax.random.split(key, 3)
        x = jax.random.normal(k1, (N, CIN, H, W), dtype=jnp.float32)
        weight = jax.random.normal(k2, (COUT, CIN, 3, 3), dtype=jnp.float32) * 0.05
        bias = jax.random.normal(k3, (COUT,), dtype=jnp.float32)
        return {'x': x, 'weight': weight, 'bias': bias}
    _L1_conv_all = _L1_conv_setup()
    _L1_conv_in = {k: v for k, v in _L1_conv_all.items() if k in ('weight', 'bias')}
    del _L1_conv_all

    def _L1_ffn_setup():
        import jax, jax.numpy as jnp
        import numpy as np
        B, N, D = (16, 2048, 128)
        NUM_EXPERTS, TOP_K, HEADS = (4, 2, 4)
        N_EDGES = 524288
        LN_EPS = 1e-05

        def _layernorm(x, g, b):
            mu = x.mean(-1, keepdims=True)
            var = ((x - mu) ** 2).mean(-1, keepdims=True)
            return (x - mu) * jax.lax.rsqrt(var + LN_EPS) * g + b

        def _forward(x, edge_index, W_gat, att_src, att_dst, b_gat, ln_gamma, ln_beta, W1, b1, W2, b2):
            Bc, Nc, Dc = x.shape
            M = Bc * Nc
            x_flat = x.reshape(M, Dc)
            h = (x_flat @ W_gat).reshape(M, HEADS, NUM_EXPERTS)
            loops = jnp.arange(M, dtype=edge_index.dtype)
            src = jnp.concatenate([edge_index[0], loops])
            dst = jnp.concatenate([edge_index[1], loops])
            a_src = (h * att_src).sum(-1)
            a_dst = (h * att_dst).sum(-1)
            e = jax.nn.leaky_relu(a_src[src] + a_dst[dst], negative_slope=0.2)
            e_max = jax.ops.segment_max(e, dst, num_segments=M)
            ee = jnp.exp(e - e_max[dst])
            denom = jax.ops.segment_sum(ee, dst, num_segments=M)
            alpha = ee / (denom[dst] + 1e-16)
            msg = h[src] * alpha[:, :, None]
            agg = jax.ops.segment_sum(msg, dst, num_segments=M).reshape(M, HEADS * NUM_EXPERTS) + b_gat
            scores = _layernorm(agg, ln_gamma, ln_beta).reshape(M, HEADS, NUM_EXPERTS).mean(1)
            scores = scores.reshape(Bc, Nc, NUM_EXPERTS)
            topk_s, topk_i = jax.lax.top_k(scores, TOP_K)
            w = jax.nn.softmax(topk_s, axis=-1)
            out = jnp.zeros_like(x)
            for ei in range(NUM_EXPERTS):
                g = jnp.where(topk_i == ei, w, 0.0).sum(-1)
                hh = jax.nn.gelu(x @ W1[ei] + b1[ei], approximate=False)
                out = out + g[..., None] * (hh @ W2[ei] + b2[ei])
            return out
        key = jax.random.key(seed)
        ks = jax.random.split(key, 8)
        s = 0.05
        return {'x': jax.random.normal(ks[0], (B, N, D), jnp.float32), 'W_gat': jax.random.normal(ks[1], (D, HEADS * NUM_EXPERTS), jnp.float32) * s, 'att_src': jax.random.normal(ks[2], (HEADS, NUM_EXPERTS), jnp.float32) * s, 'att_dst': jax.random.normal(ks[3], (HEADS, NUM_EXPERTS), jnp.float32) * s, 'b_gat': jnp.zeros((HEADS * NUM_EXPERTS,), jnp.float32), 'ln_gamma': jnp.ones((HEADS * NUM_EXPERTS,), jnp.float32), 'ln_beta': jnp.zeros((HEADS * NUM_EXPERTS,), jnp.float32), 'W1': jax.random.normal(ks[4], (NUM_EXPERTS, D, 2 * D), jnp.float32) * s, 'b1': jnp.zeros((NUM_EXPERTS, 2 * D), jnp.float32), 'W2': jax.random.normal(ks[5], (NUM_EXPERTS, 2 * D, D), jnp.float32) * s, 'b2': jnp.zeros((NUM_EXPERTS, D), jnp.float32), 'edge_index': jax.random.randint(ks[6], (2, N_EDGES), 0, B * N, jnp.int32)}
    _L1_ffn_all = _L1_ffn_setup()
    _L1_ffn_in = {k: v for k, v in _L1_ffn_all.items() if k in ('W_gat', 'att_src', 'att_dst', 'b_gat', 'ln_gamma', 'ln_beta', 'W1', 'b1', 'W2', 'b2', 'edge_index')}
    del _L1_ffn_all
    return {'x': x, 'L0_conv_w1': _L0_conv_in['w1'], 'L0_conv_b1': _L0_conv_in['b1'], 'L0_conv_bn_gamma': _L0_conv_in['bn_gamma'], 'L0_conv_bn_beta': _L0_conv_in['bn_beta'], 'L0_conv_bn_mean': _L0_conv_in['bn_mean'], 'L0_conv_bn_var': _L0_conv_in['bn_var'], 'L0_conv_w2': _L0_conv_in['w2'], 'L0_conv_b2': _L0_conv_in['b2'], 'L0_ffn_gate_w': _L0_ffn_in['gate_w'], 'L0_ffn_gate_b': _L0_ffn_in['gate_b'], 'L0_ffn_w1': _L0_ffn_in['w1'], 'L0_ffn_b1': _L0_ffn_in['b1'], 'L0_ffn_w2': _L0_ffn_in['w2'], 'L0_ffn_b2': _L0_ffn_in['b2'], 'L1_conv_weight': _L1_conv_in['weight'], 'L1_conv_bias': _L1_conv_in['bias'], 'L1_ffn_W_gat': _L1_ffn_in['W_gat'], 'L1_ffn_att_src': _L1_ffn_in['att_src'], 'L1_ffn_att_dst': _L1_ffn_in['att_dst'], 'L1_ffn_b_gat': _L1_ffn_in['b_gat'], 'L1_ffn_ln_gamma': _L1_ffn_in['ln_gamma'], 'L1_ffn_ln_beta': _L1_ffn_in['ln_beta'], 'L1_ffn_W1': _L1_ffn_in['W1'], 'L1_ffn_b1': _L1_ffn_in['b1'], 'L1_ffn_W2': _L1_ffn_in['W2'], 'L1_ffn_b2': _L1_ffn_in['b2'], 'L1_ffn_edge_index': _L1_ffn_in['edge_index']}

def reference(x, L0_conv_w1, L0_conv_b1, L0_conv_bn_gamma, L0_conv_bn_beta, L0_conv_bn_mean, L0_conv_bn_var, L0_conv_w2, L0_conv_b2, L0_ffn_gate_w, L0_ffn_gate_b, L0_ffn_w1, L0_ffn_b1, L0_ffn_w2, L0_ffn_b2, L1_conv_weight, L1_conv_bias, L1_ffn_W_gat, L1_ffn_att_src, L1_ffn_att_dst, L1_ffn_b_gat, L1_ffn_ln_gamma, L1_ffn_ln_beta, L1_ffn_W1, L1_ffn_b1, L1_ffn_W2, L1_ffn_b2, L1_ffn_edge_index):
    import jax
    import jax.numpy as jnp

    def _L0_conv_ref(x, w1, b1, bn_gamma, bn_beta, bn_mean, bn_var, w2, b2):
        import jax, jax.numpy as jnp
        import numpy as np
        C = 128
        K = 7
        GC = 32
        G = C // GC
        RED = 4
        EPS = 1e-05
        B, Cc, H, W = x.shape
        t = jnp.einsum('bchw,oc->bohw', x, w1) + b1[None, :, None, None]
        scale = (bn_gamma / jnp.sqrt(bn_var + EPS))[None, :, None, None]
        t = (t - bn_mean[None, :, None, None]) * scale + bn_beta[None, :, None, None]
        t = jax.nn.relu(t)
        wt = jnp.einsum('bchw,oc->bohw', t, w2) + b2[None, :, None, None]
        wt = wt.reshape(B, G, K * K, H, W)
        pad = (K - 1) // 2
        xp = jnp.pad(x, ((0, 0), (0, 0), (pad, pad), (pad, pad)))
        xg = xp.reshape(B, G, GC, H + 2 * pad, W + 2 * pad)
        s = jnp.zeros((B, G, GC, H, W), x.dtype)
        for i in range(K):
            for j in range(K):
                s = s + wt[:, :, i * K + j][:, :, None] * xg[:, :, :, i:i + H, j:j + W]
        out = s * wt.sum(axis=2)[:, :, None]
        return out.reshape(B, Cc, H, W)

    def _L0_ffn_ref(h, gate_w, gate_b, w1, b1, w2, b2):
        import math
        import jax, jax.numpy as jnp
        import numpy as np
        CAPACITY_FACTOR = 1.25
        B, L, D = h.shape
        E = gate_w.shape[1]
        T = B * L
        C = max(1, math.ceil(CAPACITY_FACTOR * T / E))
        x = h.reshape(T, D)
        logits = x @ gate_w + gate_b
        probs = jax.nn.softmax(logits, axis=-1)
        idx = jnp.argmax(probs, axis=-1)
        prb = jnp.take_along_axis(probs, idx[:, None], axis=1)[:, 0]
        one_hot = jax.nn.one_hot(idx, E, dtype=jnp.float32)
        pos = (jnp.cumsum(one_hot, axis=0) * one_hot).sum(-1).astype(jnp.int32) - 1
        kept = pos < C
        pos_safe = jnp.where(kept, pos, C)
        buf = jnp.zeros((E, C, D), dtype=h.dtype).at[idx, pos_safe].set(x, mode='drop')
        hmid = jax.nn.relu(jnp.einsum('ecd,edf->ecf', buf, w1) + b1[:, None, :])
        ybuf = jnp.einsum('ecf,efd->ecd', hmid, w2) + b2[:, None, :]
        pos_g = jnp.minimum(pos, C - 1)
        y_tok = ybuf[idx, pos_g] * (prb * kept)[:, None]
        y = y_tok.reshape(B, L, D)
        y = jnp.nan_to_num(y, nan=0.0, posinf=10000.0, neginf=-10000.0)
        return y

    def _L1_conv_ref(x, weight, bias):
        import jax, jax.numpy as jnp
        import numpy as np
        N, CIN, COUT, H, W = (32, 128, 128, 56, 56)
        y = jax.lax.conv_general_dilated(x, weight, window_strides=(1, 1), padding=((1, 1), (1, 1)), dimension_numbers=('NCHW', 'OIHW', 'NCHW'))
        return jax.nn.relu(y + bias[None, :, None, None])

    def _L1_ffn_ref(x, W_gat, att_src, att_dst, b_gat, ln_gamma, ln_beta, W1, b1, W2, b2, edge_index):
        import jax, jax.numpy as jnp
        import numpy as np
        B, N, D = (16, 2048, 128)
        NUM_EXPERTS, TOP_K, HEADS = (4, 2, 4)
        N_EDGES = 524288
        LN_EPS = 1e-05

        def _layernorm(x, g, b):
            mu = x.mean(-1, keepdims=True)
            var = ((x - mu) ** 2).mean(-1, keepdims=True)
            return (x - mu) * jax.lax.rsqrt(var + LN_EPS) * g + b

        def _forward(x, edge_index, W_gat, att_src, att_dst, b_gat, ln_gamma, ln_beta, W1, b1, W2, b2):
            Bc, Nc, Dc = x.shape
            M = Bc * Nc
            x_flat = x.reshape(M, Dc)
            h = (x_flat @ W_gat).reshape(M, HEADS, NUM_EXPERTS)
            loops = jnp.arange(M, dtype=edge_index.dtype)
            src = jnp.concatenate([edge_index[0], loops])
            dst = jnp.concatenate([edge_index[1], loops])
            a_src = (h * att_src).sum(-1)
            a_dst = (h * att_dst).sum(-1)
            e = jax.nn.leaky_relu(a_src[src] + a_dst[dst], negative_slope=0.2)
            e_max = jax.ops.segment_max(e, dst, num_segments=M)
            ee = jnp.exp(e - e_max[dst])
            denom = jax.ops.segment_sum(ee, dst, num_segments=M)
            alpha = ee / (denom[dst] + 1e-16)
            msg = h[src] * alpha[:, :, None]
            agg = jax.ops.segment_sum(msg, dst, num_segments=M).reshape(M, HEADS * NUM_EXPERTS) + b_gat
            scores = _layernorm(agg, ln_gamma, ln_beta).reshape(M, HEADS, NUM_EXPERTS).mean(1)
            scores = scores.reshape(Bc, Nc, NUM_EXPERTS)
            topk_s, topk_i = jax.lax.top_k(scores, TOP_K)
            w = jax.nn.softmax(topk_s, axis=-1)
            out = jnp.zeros_like(x)
            for ei in range(NUM_EXPERTS):
                g = jnp.where(topk_i == ei, w, 0.0).sum(-1)
                hh = jax.nn.gelu(x @ W1[ei] + b1[ei], approximate=False)
                out = out + g[..., None] * (hh @ W2[ei] + b2[ei])
            return out
        return _forward(x, edge_index, W_gat, att_src, att_dst, b_gat, ln_gamma, ln_beta, W1, b1, W2, b2)

    def _gn(v, G=32, eps=1e-05):
        B_, C_, H_, W_ = v.shape
        g = v.reshape(B_, G, C_ // G, H_, W_)
        m = jnp.mean(g, axis=(2, 3, 4), keepdims=True)
        s = jnp.var(g, axis=(2, 3, 4), keepdims=True)
        return ((g - m) / jnp.sqrt(s + eps)).reshape(v.shape)

    def _ln_c(v, eps=1e-06):
        m = jnp.mean(v, axis=1, keepdims=True)
        s = jnp.var(v, axis=1, keepdims=True)
        return (v - m) / jnp.sqrt(s + eps)

    def _ln_t(v, eps=1e-05):
        m = jnp.mean(v, axis=-1, keepdims=True)
        s = jnp.var(v, axis=-1, keepdims=True)
        return (v - m) / jnp.sqrt(s + eps)

    def _to_tokens(v):
        B_, C_, H_, W_ = v.shape
        return v.reshape(B_, C_, H_ * W_).transpose(0, 2, 1)

    def _from_tokens(t, like):
        B_, C_, H_, W_ = like.shape
        return t.transpose(0, 2, 1).reshape(B_, C_, H_, W_)
    x = x + _L0_conv_ref(_ln_c(x), L0_conv_w1, L0_conv_b1, L0_conv_bn_gamma, L0_conv_bn_beta, L0_conv_bn_mean, L0_conv_bn_var, L0_conv_w2, L0_conv_b2)
    t = _to_tokens(x)
    t = t + _L0_ffn_ref(_ln_t(t), L0_ffn_gate_w, L0_ffn_gate_b, L0_ffn_w1, L0_ffn_b1, L0_ffn_w2, L0_ffn_b2)
    x = _from_tokens(t, x)
    x = x + _L1_conv_ref(_ln_c(x), L1_conv_weight, L1_conv_bias)
    t = _to_tokens(x)
    t = t + _L1_ffn_ref(_ln_t(t), L1_ffn_W_gat, L1_ffn_att_src, L1_ffn_att_dst, L1_ffn_b_gat, L1_ffn_ln_gamma, L1_ffn_ln_beta, L1_ffn_W1, L1_ffn_b1, L1_ffn_W2, L1_ffn_b2, L1_ffn_edge_index)
    x = _from_tokens(t, x)
    return x

_drawn_inputs = setup_inputs


def setup_inputs(seed=0):
    import zlib

    import numpy as np

    out = dict(_drawn_inputs(seed))
    spreads = {'L0_conv_bn_gamma': (1.0, 0.2),
     'L0_conv_bn_beta': (0.0, 0.1),
     'L0_ffn_gate_b': (0.0, 0.1),
     'L0_ffn_b1': (0.0, 0.8),
     'L0_ffn_b2': (0.0, 0.712),
     'L1_ffn_b_gat': (0.0, 0.1),
     'L1_ffn_ln_gamma': (1.0, 0.6),
     'L1_ffn_ln_beta': (0.0, 0.602),
     'L1_ffn_b1': (0.0, 0.464),
     'L1_ffn_b2': (0.0, 0.1)}
    factors = {'L0_conv_b1': 3.172, 'L1_ffn_att_src': 8.0, 'L1_ffn_att_dst': 8.0}
    for name, (base, spread) in spreads.items():
        noise = np.random.default_rng([zlib.crc32(name.encode()), seed]).standard_normal(out[name].shape)
        drawn = base * np.exp(spread * noise) if base else spread * noise
        out[name] = jnp.asarray(drawn.astype(out[name].dtype))
    for name, factor in factors.items():
        out[name] = (out[name] * factor).astype(out[name].dtype)
    return out
```

```python
from contextlib import ExitStack

import numpy as np
import concourse.bass as bass
from concourse import mybir

ALU = mybir.AluOpType
ACT = mybir.ActivationFunctionType
AX = mybir.AxisListType
F32 = mybir.dt.float32
BF16 = mybir.dt.bfloat16
I32 = mybir.dt.int32

P = 128
B, H, W = 8, 64, 64
HW = H * W
M = B * HW
TILES = HW // P
NT = 512
LT = HW // NT

KS, G, CR = 7, 4, 32
TAPS = KS * KS
GC = P // G
OUT = 5
IN = OUT + KS - 1
PR = -(-H // OUT)
NP = PR * PR
PO = PR * OUT
PI = PO + KS - 1
KIN = IN * IN
NOUT = OUT * OUT
LEAD = (OUT - 1) * (IN + 1)
CAN = LEAD + KIN

E0, F0 = 8, 512
CAP = -(-5 * M // (4 * E0))
SLOTS = E0 * CAP


class LayerNorm:

    def __init__(self, nc, sb, sem, ones, psum_mean, psum_var, tag):
        self.nc, self.ones, self.pm, self.pv = nc, ones, psum_mean, psum_var
        self.sq = sb(f"{tag}_sq", [P, 2, NT], F32)
        self.sd = sb(f"{tag}_sd", [P, 2, NT], F32)
        self.mean_ready = sem(f"{tag}_mean_ready")
        self.centred = sem(f"{tag}_centred")
        self.squared = sem(f"{tag}_squared")
        self.var_ready = sem(f"{tag}_var_ready")
        self.dev_ready = sem(f"{tag}_dev_ready")
        self.rstd_ready = sem(f"{tag}_rstd_ready")
        self.normed = sem(f"{tag}_normed")

    def tensor(self, pe, x, base):
        def var(t):
            pe.wait_ge(self.squared, base + (t + 1))
            if t >= 2:
                pe.wait_ge(self.dev_ready, base + (t - 1))
            self.nc.tensor.matmul(self.pv[t % 2], self.ones, self.sq[:, t % 2], start=True,
                                  stop=True).then_inc(self.var_ready, 1)

        for t in range(LT):
            if t >= 2:
                pe.wait_ge(self.centred, base + (t - 1))
            self.nc.tensor.matmul(self.pm[t % 2], self.ones, x[:, t * NT:(t + 1) * NT], start=True,
                                  stop=True).then_inc(self.mean_ready, 1)
            if t >= 1:
                var(t - 1)
        var(LT - 1)

    def scalar(self, act, xc, eps, base):
        def dev(t):
            act.wait_ge(self.var_ready, base + (t + 1))
            if t >= 2:
                act.wait_ge(self.normed, base + (t - 1))
            self.nc.scalar.activation(self.sd[:, t % 2], self.pv[t % 2], ACT.Sqrt,
                                      bias=eps).then_inc(self.dev_ready, 1)

        for t in range(LT):
            act.wait_ge(self.centred, base + (t + 1))
            if t >= 2:
                act.wait_ge(self.var_ready, base + (t - 1))
            self.nc.scalar.activation(self.sq[:, t % 2], xc[:, t * NT:(t + 1) * NT],
                                      ACT.Square).then_inc(self.squared, 1)
            if t >= 1:
                dev(t - 1)
        dev(LT - 1)

    def vector(self, dve, x, xc, base):
        def rstd(t):
            dve.wait_ge(self.dev_ready, base + (t + 1))
            self.nc.vector.reciprocal(self.sd[:, t % 2], self.sd[:, t % 2]).then_inc(self.rstd_ready, 1)

        for t in range(LT):
            dve.wait_ge(self.mean_ready, base + (t + 1))
            c = slice(t * NT, (t + 1) * NT)
            self.nc.vector.tensor_tensor(xc[:, c], x[:, c], self.pm[t % 2],
                                         ALU.subtract).then_inc(self.centred, 1)
            if t >= 1:
                rstd(t - 1)
        rstd(LT - 1)

    def gpsimd(self, pool, xc, out, base):
        for t in range(LT):
            pool.wait_ge(self.rstd_ready, base + (t + 1))
            self.nc.gpsimd.tensor_tensor(out(t), xc[:, t * NT:(t + 1) * NT].rearrange("p (r w) -> p r w", w=W),
                                         self.sd[:, t % 2].rearrange("p (r w) -> p r w", w=W),
                                         ALU.mult).then_inc(self.normed, 1)


def involution_and_routing(nc, passed, x, x1, xb, keep, w):
    slots_all, gates_all = keep
    with ExitStack() as ctx:
        sb = lambda n, s, d: ctx.enter_context(nc.sbuf_tensor(f"a_{n}", s, d))
        sem = lambda n: ctx.enter_context(nc.semaphore(n))
        bank = [ctx.enter_context(nc.psum_tensor(f"a_bank{i}", [P, NT], F32)) for i in range(8)]

        xs = sb("xs", [P, HW], F32)
        xc = sb("xc", [P, HW], F32)
        xp = sb("xp", [P, PI, PI], F32)
        hid = sb("hid", [CR + 1, PO, PO], F32)
        taps = sb("taps", [P, G * NOUT, NP], F32)
        ws = sb("ws", [P, PO, PO], F32)
        so = sb("so", [P, PO, PO], F32)
        ht = so[:].rearrange("p a b -> p (a b)")[:, 0:HW].rearrange("p (t c) -> p t c", c=P)
        xq = [xc[:, z * PR * KIN:(z + 1) * PR * KIN] for z in range(2)]
        xt = sb("xt", [P, 3, 4, P], F32)
        ident = sb("ident", [P, P], F32)
        ones = sb("ones_p", [P, P], F32)
        upper = sb("upper", [P, P], BF16)
        onesb = sb("onesb", [P, P], BF16)
        w1t = sb("w1t", [P, CR], F32)
        w2t = sb("w2t", [CR + 1, G, TAPS], F32)
        canvas = sb("canvas", [CR + 1, G, CAN], F32)
        wsum = sb("wsum", [CR + 1, G], F32)
        wsumt = sb("wsumt", [CR + 1, G, GC], F32)
        bn = sb("bn", [CR, 8], F32)
        eps6 = sb("eps6", [P, 1], F32)
        eps5 = sb("eps5", [P, 1], F32)
        gw = sb("gw", [P, E0], F32)
        gb = sb("gb", [P, E0], F32)
        em8 = sb("em8", [P, E0], F32)
        carry = sb("carry", [P, E0], F32)
        R = lambda n, d=F32: sb(n, [P, TILES, E0], d)
        lg, ex, eq, oh, cum, pos = R("lg"), R("ex"), R("eq"), R("oh"), R("cum"), R("pos")
        ohb = R("ohb", BF16)
        T1 = lambda n, d=F32: sb(n, [P, TILES], d)
        mx, se, prb, ix, pt, kept, sl, sg = [T1(n) for n in ("mx", "se", "prb", "ix", "pt", "kept", "sl", "sg")]
        sidx = T1("sidx", I32)
        sgi = T1("sgi", I32)

        ln = LayerNorm(nc, sb, sem, ones[:], [bank[0][:], bank[1][:]], [bank[2][:], bank[3][:]], "lna")

        loaded = sem("a_loaded")
        consts = sem("a_consts")
        setup = sem("a_setup")
        setup_v = sem("a_setup_v")
        bn_root = sem("a_bn_root")
        bn_chain = sem("a_bn_chain")
        zeroed = sem("a_zeroed")
        hid_psum = sem("a_hid_psum")
        hid_ready = sem("a_hid_ready")
        ws_psum = sem("a_ws_psum")
        ws_ready = sem("a_ws_ready")
        taps_psum = sem("a_taps_psum")
        taps_act = sem("a_taps_act")
        taps_dve = sem("a_taps_dve")
        patch_rows = sem("a_patch_rows")
        patch_psum = sem("a_patch_psum")
        patch_act = sem("a_patch_act")
        patch_dve = sem("a_patch_dve")
        sum_psum = sem("a_sum_psum")
        sum_act = sem("a_sum_act")
        sum_dve = sem("a_sum_dve")
        x1_ready = sem("a_x1_ready")
        x1_stored = sem("a_x1_stored")
        tok_psum = sem("a_tok_psum")
        tok_act = sem("a_tok_act")
        logit_psum = sem("a_logit_psum")
        shifted = sem("a_shifted")
        exps = sem("a_exps")
        chosen = sem("a_chosen")
        rank_psum = sem("a_rank_psum")
        chain = sem("a_chain")
        slots_ready = sem("a_slots_ready")
        scattered = sem("a_scattered")
        ht_free = sem("a_ht_free")

        NB3 = -(-G * NOUT // 3)
        NX4 = -(-NP // 4)
        cols = [(0, 5), (5, 10), (10, 13)]
        NS = PR * len(cols)

        def bank_of(z):
            return (z // PR) * 3 + (0 if z % PR < 5 else 1 if z % PR < 10 else 2)

        def group_end(u):
            return bank_of(min(4 * u + 3, NP - 1)) + 1

        order = []
        done = 0
        for u in range(NX4):
            while done < NS and u >= 3 and done < group_end(u - 3):
                order.append(("sum", done))
                done += 1
            order.append(("patch", u))
        order += [("sum", v) for v in range(done, NS)]

        def sums(eng, copy, i, v, groups, s):
            a, (b0, b1) = v // 3, cols[v % 3]
            eng.wait_ge(sum_psum, NS * i + (v + 1))
            for g in groups:
                src = bank[6 + v % 2][GC * g:GC * (g + 1), 0:(b1 - b0) * G * NOUT].rearrange(
                    "p (b g r c) -> p b g r c", g=G, r=OUT, c=OUT)[:, :, g]
                dst = so[GC * g:GC * (g + 1), OUT * a:OUT * (a + 1), OUT * b0:OUT * b1].rearrange(
                    "p r (b c) -> p b r c", c=OUT)
                last = copy(dst, src)
            last.then_inc(s, 1)

        block = ctx.enter_context(nc.Block())

        @block.sync
        def _(sp):
            for dst, src in ((w1t[:], w["w1t"]), (w2t[0:CR].rearrange("k g t -> k (g t)"), w["w2t"]),
                             (w2t[CR:CR + 1].rearrange("k g t -> k (g t)"), w["b2"]),
                             (bn[:, 0:5], w["bn"]), (gw[:], w["gate_w"]),
                             (gb[:], w["gate_b"].broadcast_to([P, E0]))):
                sp.dma_start(dst, src).then_inc(consts, 16)
            sp.wait_ge(setup_v, 1)
            xbz = xb.rearrange("(p r) d -> p (r d)", p=P)
            step = SLOTS // 4
            for q in range(4):
                sp.dma_start(xbz[:, q * step:(q + 1) * step],
                             taps[:].rearrange("p a b -> p (a b)")[:, 0:step]).then_inc(zeroed, 16)
            with sp.Fori(0, B) as i:
                sp.dma_start(xs[:], x[i]).then_inc(loaded, 16)
                sp.wait_ge(x1_ready, i + 1)
                sp.dma_start(x1[i], xs[:]).then_inc(x1_stored, 16)
                sp.wait_ge(ln.centred, 2 * LT * i + 2 * LT)
                sp.wait_ge(x1_stored, 16 * i + 16)
                sp.sem_inc(passed, 1)

        @block.gpsimd
        def _(pool):
            pool.sem_inc(ht_free, 1)
            nc.gpsimd.memset(xp[:], 0.0).then_inc(setup, 1)
            nc.gpsimd.memset(ident[:], 0.0).then_inc(setup, 1)
            nc.gpsimd.memset(ones[:], 1.0 / P).then_inc(setup, 1)
            nc.gpsimd.memset(onesb[:], 1.0).then_inc(setup, 1)
            nc.gpsimd.memset(upper[:], 1.0).then_inc(setup, 1)
            nc.gpsimd.memset(eps6[:], 1e-6).then_inc(setup, 1)
            nc.gpsimd.memset(eps5[:], 1e-5).then_inc(setup, 1)
            nc.gpsimd.iota(em8[:], pattern=[[1, E0]], base=-E0, channel_multiplier=0,
                           allow_small_or_imprecise_dtypes=True).then_inc(setup, 1)
            pool.wait_ge(setup, 8)
            nc.gpsimd.affine_select(out=ident[:], in_=ident[:], compare_op=ALU.not_equal, fill=1.0, base=0,
                                    pattern=[[-1, P]], channel_multiplier=1).then_inc(setup, 1)
            nc.gpsimd.affine_select(out=upper[:], in_=upper[:], compare_op=ALU.is_gt, fill=0.0, base=0,
                                    pattern=[[1, P]], channel_multiplier=-1).then_inc(setup, 1)
            pool.wait_ge(setup, 10)
            with pool.Fori(0, B) as i:
                ln.gpsimd(pool, xc, lambda t: xp[:, 3 + 8 * t:11 + 8 * t, 3:3 + W], 2 * LT * i)
                pool.wait_ge(ln.normed, 2 * LT * i + LT)
                for a in range(PR):
                    if a >= 2:
                        pool.wait_ge(patch_psum, NX4 * i + (PR * (a - 1) - 1) // 4 + 1)
                    pool.sem_inc(passed, 1)
                    rows = xp[:, OUT * a:OUT * a + IN]
                    nc.gpsimd.tensor_copy(
                        xq[a % 2].rearrange("p (b r c) -> p b r c", r=IN, c=IN),
                        bass.AP(tensor=rows.tensor, offset=rows.offset,
                                ap=[list(rows.ap[0]), [OUT, PR], [PI, IN], [1, IN]])).then_inc(patch_rows, 1)
                ln.gpsimd(pool, xc, lambda t: xc[:, t * NT:(t + 1) * NT].rearrange("p (r w) -> p r w", w=W),
                          2 * LT * i + LT)
                pool.wait_ge(slots_ready, i + 1)
                pool.wait_ge(tok_act, LT * i + LT)
                pool.wait_ge(zeroed, 64)
                pool.sem_inc(passed, 1)
                for t in range(TILES):
                    nc.gpsimd.indirect_dma_start(
                        xb, bass.IndirectOffsetOnAxis(ap=sidx[:, t:t + 1], axis=0), ht[:, t], None,
                        bounds_check=SLOTS - 1, oob_is_err=False).then_inc(scattered, 16)
                pool.wait_ge(scattered, 16 * TILES * i + 16 * TILES)
                pool.sem_inc(ht_free, 1)

        @block.tensor
        def _(pe):
            pe.wait_ge(setup, 10)
            pe.wait_ge(setup_v, 5)
            pe.wait_ge(consts, 96)
            with pe.Fori(0, B) as i:
                pe.wait_ge(loaded, 16 * i + 16)
                ln.tensor(pe, xs, 2 * LT * i)
                for t in range(LT):
                    pe.wait_ge(ln.normed, 2 * LT * i + (t + 1))
                    if t >= 2:
                        pe.wait_ge(hid_ready, LT * i + (t - 1))
                    nc.tensor.matmul(bank[t % 2][0:CR, :], w1t[:], xp[:, 3 + 8 * t:11 + 8 * t, 3:3 + W],
                                     start=True, stop=True).then_inc(hid_psum, 1)
                for t in range(LT):
                    pe.wait_ge(hid_ready, LT * i + (t + 1))
                    if t >= 2:
                        pe.wait_ge(ws_ready, LT * i + (t - 1))
                    nc.tensor.matmul(bank[2 + t % 2][:], wsumt[:].rearrange("k g c -> k (g c)"),
                                     hid[:, 8 * t:8 * t + 8, 0:W], start=True, stop=True).then_inc(ws_psum, 1)
                pe.wait_ge(ws_ready, LT * i + LT)
                for q in range(NB3):
                    if q >= 4:
                        s, o = (taps_act, q - 4) if q % 2 == 0 else (taps_dve, q - 4)
                        pe.wait_ge(s, (NB3 // 2) * i + (o // 2 + 1))
                    for z in range(3 * q, min(3 * q + 3, G * NOUT)):
                        g, n = z // NOUT, z % NOUT
                        r, c = n // OUT, n % OUT
                        at = LEAD - (IN * r + c)
                        nc_mm = nc.tensor.matmul(
                            bank[q % 4][0:KIN, (z % 3) * NP:(z % 3 + 1) * NP], canvas[:, g, at:at + KIN],
                            hid[:, r::OUT, c::OUT], start=True, stop=True)
                    nc_mm.then_inc(taps_psum, 1)

                def transposed(u):
                    if u >= 2:
                        s = (patch_act, patch_dve)[u % 2]
                        n = (NX4 + 1) // 2 if u % 2 == 0 else NX4 // 2
                        pe.wait_ge(s, n * i + ((u - 2) // 2 + 1))
                    last_row = min(4 * u + 3, NP - 1) // PR
                    pe.wait_ge(patch_rows, PR * i + last_row + 1)
                    for z in range(4 * u, min(4 * u + 4, NP)):
                        a, b = z // PR, z % PR
                        mm = nc.tensor.transpose(bank[4 + u % 2][0:KIN, (z % 4) * P:(z % 4 + 1) * P],
                                                 xq[a % 2][:, b * KIN:(b + 1) * KIN], ident[:])
                    mm.then_inc(patch_psum, 1)

                transposed(0)
                transposed(1)
                u_next = 2
                pe.wait_ge(taps_act, (NB3 // 2) * i + NB3 // 2)
                pe.wait_ge(taps_dve, (NB3 // 2) * i + NB3 // 2)
                for v in range(NS):
                    a, (b0, b1) = v // 3, cols[v % 3]
                    if v >= 2:
                        pe.wait_ge(sum_act, NS * i + (v - 1))
                        pe.wait_ge(sum_dve, NS * i + (v - 1))
                    for b in range(b0, b1):
                        z = a * PR + b
                        u = z // 4
                        if z % 4 == 0:
                            s = (patch_act, patch_dve)[u % 2]
                            n = (NX4 + 1) // 2 if u % 2 == 0 else NX4 // 2
                            pe.wait_ge(s, n * i + (u // 2 + 1))
                        mm = nc.tensor.matmul(bank[6 + v % 2][:, (b - b0) * G * NOUT:(b - b0 + 1) * G * NOUT],
                                              xt[0:KIN, u % 3, z % 4, :], taps[0:KIN, :, z], start=True, stop=True)
                        if z % 4 == 3 and u_next < NX4:
                            transposed(u_next)
                            u_next += 1
                    mm.then_inc(sum_psum, 1)
                pe.wait_ge(x1_ready, i + 1)
                ln.tensor(pe, xs, 2 * LT * i + LT)
                pe.wait_ge(ln.normed, 2 * LT * i + 2 * LT)
                for t in range(LT):
                    if t >= 4:
                        pe.wait_ge(tok_act, LT * i + (t - 3))
                    for k in range(4):
                        mm = nc.tensor.transpose(bank[t % 4][:, k * P:(k + 1) * P],
                                                 xc[:, t * NT + k * P:t * NT + (k + 1) * P], ident[:])
                    mm.then_inc(tok_psum, 1)
                for t in range(TILES):
                    mm = nc.tensor.matmul(bank[4][:, t * E0:(t + 1) * E0], xc[:, t * P:(t + 1) * P], gw[:],
                                          start=True, stop=True)
                mm.then_inc(logit_psum, 1)
                pe.wait_ge(chosen, i + 1)
                o2 = ohb[:].rearrange("p t e -> p (t e)")
                nc.tensor.matmul(bank[5][:, 0:256], upper[:], o2, start=True, stop=True)
                nc.tensor.matmul(bank[5][:, 256:512], onesb[:], o2, start=True, stop=True).then_inc(rank_psum, 1)
                pe.wait_ge(tok_act, LT * i + LT)

        @block.scalar
        def _(act):
            act.wait_ge(setup, 10)
            act.wait_ge(setup_v, 4)
            nc.scalar.activation(bn[:, 7:8], bn[:, 7:8], ACT.Sqrt).then_inc(bn_root, 1)
            act.wait_ge(setup_v, 5)
            with act.Fori(0, B) as i:
                act.wait_ge(loaded, 16 * i + 16)
                ln.scalar(act, xc, eps6[:], 2 * LT * i)
                for t in range(LT):
                    act.wait_ge(hid_psum, LT * i + (t + 1))
                    nc.scalar.activation(hid[0:CR, 8 * t:8 * t + 8, 0:W],
                                         bank[t % 2][0:CR, :].rearrange("p (r w) -> p r w", w=W), ACT.Relu,
                                         bias=bn[:, 6:7], scale=bn[:, 5:6]).then_inc(hid_ready, 1)
                for t in range(LT):
                    act.wait_ge(ws_psum, LT * i + (t + 1))
                    nc.scalar.activation(ws[:, 8 * t:8 * t + 8, 0:W],
                                         bank[2 + t % 2][:].rearrange("p (r w) -> p r w", w=W),
                                         ACT.Copy).then_inc(ws_ready, 1)
                for q in range(0, NB3, 2):
                    act.wait_ge(taps_psum, NB3 * i + (q + 1))
                    n = min(3, G * NOUT - 3 * q)
                    nc.scalar.activation(taps[0:KIN, 3 * q:3 * q + n].rearrange("p a b -> p (a b)"),
                                         bank[q % 4][0:KIN, 0:n * NP], ACT.Copy).then_inc(taps_act, 1)

                def patches(u):
                    act.wait_ge(patch_psum, NX4 * i + (u + 1))
                    if u >= 3:
                        act.wait_ge(sum_psum, NS * i + group_end(u - 3))
                    n = min(4, NP - 4 * u)
                    nc.scalar.activation(xt[0:KIN, u % 3, 0:n].rearrange("p a b -> p (a b)"),
                                         bank[4 + u % 2][0:KIN, 0:n * P], ACT.Copy).then_inc(patch_act, 1)

                for kind, n in order:
                    if kind == "patch":
                        if n % 2 == 0:
                            patches(n)
                    else:
                        sums(act, nc.scalar.copy, i, n, (0, 1), sum_act)
                ln.scalar(act, xc, eps5[:], 2 * LT * i + LT)
                act.wait_ge(ht_free, i + 1)
                for t in range(LT):
                    act.wait_ge(tok_psum, LT * i + (t + 1))
                    nc.scalar.activation(ht[:, 4 * t:4 * t + 4].rearrange("p a b -> p (a b)"), bank[t % 4][:],
                                         ACT.Copy).then_inc(tok_act, 1)
                act.wait_ge(shifted, i + 1)
                nc.scalar.activation(ex[:], lg[:], ACT.Exp).then_inc(exps, 1)

        @block.vector
        def _(dve):
            nc.vector.memset(taps[:].rearrange("p a b -> p (a b)"), 0.0).then_inc(setup_v, 1)
            nc.vector.memset(hid[:], 0.0)
            nc.vector.memset(canvas[:], 0.0)
            nc.vector.memset(carry[:], 0.0)
            nc.vector.memset(ws[:], 0.0).then_inc(setup_v, 1)
            dve.wait_ge(setup_v, 2)
            nc.vector.memset(hid[CR:CR + 1], 1.0)
            dve.wait_ge(consts, 96)
            for g in range(G):
                nc.vector.tensor_copy(canvas[:, g, LEAD:LEAD + KS * IN].rearrange("k (a b) -> k a b", b=IN)[:, :, 0:KS],
                                      w2t[:, g].rearrange("k (a b) -> k a b", b=KS))
            nc.vector.tensor_reduce(wsum[:], w2t[:], AX.X, ALU.add).then_inc(setup_v, 1)
            dve.wait_ge(setup_v, 3)
            nc.vector.tensor_copy(wsumt[:], wsum[:].unsqueeze(2).broadcast_to([CR + 1, G, GC]))
            nc.vector.tensor_scalar(bn[:, 7:8], bn[:, 4:5], 1e-5, None, ALU.add).then_inc(setup_v, 1)
            dve.wait_ge(bn_root, 1)
            nc.vector.reciprocal(bn[:, 5:6], bn[:, 7:8]).then_inc(bn_chain, 1)
            dve.wait_ge(bn_chain, 1)
            nc.vector.tensor_tensor(bn[:, 5:6], bn[:, 5:6], bn[:, 1:2], ALU.mult).then_inc(bn_chain, 1)
            nc.vector.tensor_tensor(bn[:, 6:7], bn[:, 0:1], bn[:, 3:4], ALU.subtract).then_inc(bn_chain, 1)
            dve.wait_ge(bn_chain, 3)
            nc.vector.scalar_tensor_tensor(out=bn[:, 6:7], in0=bn[:, 6:7], scalar=bn[:, 5:6], in1=bn[:, 2:3],
                                           op0=ALU.mult, op1=ALU.add).then_inc(setup_v, 1)
            with dve.Fori(0, B) as i:
                dve.wait_ge(loaded, 16 * i + 16)
                ln.vector(dve, xs, xc, 2 * LT * i)
                for q in range(1, NB3, 2):
                    dve.wait_ge(taps_psum, NB3 * i + (q + 1))
                    n = min(3, G * NOUT - 3 * q)
                    nc.vector.tensor_copy(taps[0:KIN, 3 * q:3 * q + n].rearrange("p a b -> p (a b)"),
                                          bank[q % 4][0:KIN, 0:n * NP]).then_inc(taps_dve, 1)
                dve.wait_ge(ht_free, i + 1)
                for kind, n in order:
                    if kind == "patch":
                        if n % 2 == 1:
                            u = n
                            dve.wait_ge(patch_psum, NX4 * i + (u + 1))
                            if u >= 3:
                                dve.wait_ge(sum_psum, NS * i + group_end(u - 3))
                            m = min(4, NP - 4 * u)
                            nc.vector.tensor_copy(xt[0:KIN, u % 3, 0:m].rearrange("p a b -> p (a b)"),
                                                  bank[4 + u % 2][0:KIN, 0:m * P]).then_inc(patch_dve, 1)
                    else:
                        sums(dve, nc.vector.tensor_copy, i, n, (2, 3), sum_dve)
                K = 22
                n = [0]

                def link(ins):
                    n[0] += 1
                    ins.then_inc(chain, 1)
                    dve.wait_ge(chain, K * i + n[0])

                dve.wait_ge(sum_act, NS * i + NS)
                dve.wait_ge(sum_dve, NS * i + NS)
                dve.wait_ge(ws_ready, LT * i + LT)
                link(nc.vector.tensor_tensor(so[:, 0:H, 0:W], so[:, 0:H, 0:W], ws[:, 0:H, 0:W], ALU.mult))
                xv = xs[:].rearrange("p (r w) -> p r w", w=W)
                nc.vector.tensor_tensor(xv, xv, so[:, 0:H, 0:W], ALU.add).then_inc(x1_ready, 1)
                dve.wait_ge(x1_ready, i + 1)
                ln.vector(dve, xs, xc, 2 * LT * i + LT)
                dve.wait_ge(logit_psum, i + 1)
                full = [P, TILES, E0]
                link(nc.vector.tensor_tensor(lg[:], bank[4][:, 0:256].rearrange("p (t e) -> p t e", e=E0),
                                             gb[:].unsqueeze(1).broadcast_to(full), ALU.add))
                link(nc.vector.tensor_reduce(mx[:], lg[:], AX.X, ALU.max))
                nc.vector.tensor_tensor(lg[:], lg[:], mx[:].unsqueeze(2).broadcast_to(full),
                                        ALU.subtract).then_inc(shifted, 1)
                dve.wait_ge(shifted, i + 1)
                link(nc.vector.tensor_scalar(eq[:], lg[:], 0.0, None, ALU.is_equal))
                link(nc.vector.tensor_tensor(eq[:], eq[:], em8[:].unsqueeze(1).broadcast_to(full), ALU.mult))
                link(nc.vector.tensor_reduce(ix[:], eq[:], AX.X, ALU.min))
                link(nc.vector.tensor_tensor(oh[:], em8[:].unsqueeze(1).broadcast_to(full),
                                             ix[:].unsqueeze(2).broadcast_to(full), ALU.is_equal))
                nc.vector.tensor_copy(ohb[:], oh[:]).then_inc(chosen, 1)
                dve.wait_ge(exps, i + 1)
                link(nc.vector.tensor_reduce(se[:], ex[:], AX.X, ALU.add))
                link(nc.vector.reciprocal(prb[:], se[:]))
                dve.wait_ge(rank_psum, i + 1)
                rank = bank[5][:, 0:256].rearrange("p (t e) -> p t e", e=E0)
                link(nc.vector.tensor_copy(ex[:], bank[5][:, 256:512].rearrange("p (t e) -> p t e", e=E0)))
                for e in range(E0):
                    last = nc.vector.tensor_tensor_scan(cum[:, :, e], ex[:, :, e], ex[:, :, e],
                                                        carry[:, e:e + 1], ALU.add, ALU.bypass)
                link(last)
                link(nc.vector.tensor_copy(carry[:], cum[:, TILES - 1]))
                link(nc.vector.tensor_tensor(cum[:], cum[:], ex[:], ALU.subtract))
                link(nc.vector.tensor_tensor(cum[:], cum[:], rank, ALU.add))
                link(nc.vector.tensor_tensor(pos[:], cum[:], oh[:], ALU.mult))
                link(nc.vector.tensor_reduce(pt[:], pos[:], AX.X, ALU.add))
                link(nc.vector.tensor_scalar(kept[:], pt[:], float(CAP), None, ALU.is_lt))
                link(nc.vector.tensor_scalar(sl[:], ix[:], float(E0), float(CAP), ALU.add, ALU.mult))
                link(nc.vector.tensor_tensor(sl[:], sl[:], pt[:], ALU.add))
                link(nc.vector.tensor_tensor(sg[:], sl[:], kept[:], ALU.mult))
                nc.vector.tensor_copy(slots_all[:, bass.ts(i, TILES)], sg[:])
                nc.vector.tensor_tensor(gates_all[:, bass.ts(i, TILES)], prb[:], kept[:], ALU.mult)
                link(nc.vector.tensor_scalar(pt[:], kept[:], -float(2 * SLOTS), float(2 * SLOTS), ALU.mult,
                                             ALU.add))
                link(nc.vector.tensor_tensor(sl[:], sl[:], pt[:], ALU.add))
                dve.wait_ge(ht_free, i + 1)
                nc.vector.tensor_copy(sidx[:], sl[:]).then_inc(slots_ready, 1)
                assert n[0] == K, n[0]


def experts(nc, passed, xb, yb, w):
    NF = F0 // P
    STEPS = CAP // NT
    TURN = 2 * STEPS
    with ExitStack() as ctx:
        sb = lambda n, s, d=F32: ctx.enter_context(nc.sbuf_tensor(f"b_{n}", s, d))
        sem = lambda n: ctx.enter_context(nc.semaphore(f"b_{n}"))
        bank = [ctx.enter_context(nc.psum_tensor(f"b_bank{i}", [P, NT], F32)) for i in range(8)]
        tok = sb("tok", [P, 4, 4, P])
        xt = sb("xt", [P, 2, NT])
        hid = sb("hid", [P, 2, NF, NT])
        y = sb("y", [P, 2, 4, P])
        w1 = sb("w1", [P, 2, F0])
        w2 = sb("w2", [P, 2, NF, P])
        b1 = sb("b1", [P, 2, NF])
        b2 = sb("b2", [P, 2, P])
        ident = sb("ident", [P, P])

        setup = sem("setup")
        wload = [sem(f"weights_loaded_{s}") for s in range(2)]
        xload = [sem(f"slots_loaded_{s}") for s in range(4)]
        turned = sem("turned")
        xt_ready = sem("xt_ready")
        up_psum = sem("up_psum")
        up_ready = sem("up_ready")
        down_psum = sem("down_psum")
        y_ready = sem("y_ready")
        y_stored = [sem(f"y_stored_{s}") for s in range(2)]

        xn = xb.rearrange("(n p k) d -> n p k d", p=P, k=4)
        yn = yb.rearrange("(n p k) d -> n p k d", p=P, k=4)
        def store(act, i, t):
            act.wait_ge(y_ready, TURN * i + (t + 1))
            act.dma_start(yn[TURN * i + t], y[:, t % 2]).then_inc(y_stored[t % 2], 16)

        block = ctx.enter_context(nc.Block())

        @block.sync
        def _(sp):
            with sp.Fori(0, E0 // 2) as i:
                for s in range(2):
                    e = 2 * i + s
                    for dst, src in ((w1[:, s], w["w1"][e]),
                                     (w2[:, s], w["w2"][e].rearrange("(f p) d -> p f d", p=P)),
                                     (b1[:, s], w["b1"][e]), (b2[:, s], w["b2"][e].broadcast_to([P, P]))):
                        sp.dma_start(dst, src).then_inc(wload[s], 16)
                for t in range(TURN):
                    if t >= 4:
                        sp.wait_ge(turned, TURN * i + (t - 3))
                    sp.dma_start(tok[:, t % 4], xn[TURN * i + t]).then_inc(xload[t % 4], 16)
                sp.wait_ge(y_ready, TURN * i + TURN)
                sp.sem_inc(passed, 1)

        @block.gpsimd
        def _(pool):
            nc.gpsimd.memset(ident[:], 0.0).then_inc(setup, 1)
            pool.wait_ge(setup, 1)
            nc.gpsimd.affine_select(out=ident[:], in_=ident[:], compare_op=ALU.not_equal, fill=1.0, base=0,
                                    pattern=[[-1, P]], channel_multiplier=1).then_inc(setup, 1)

        @block.tensor
        def _(pe):
            pe.wait_ge(setup, 2)
            with pe.Fori(0, E0 // 2) as i:
                def turn(t):
                    pe.wait_ge(xload[t % 4], (TURN // 4) * 16 * i + 16 * (t // 4 + 1))
                    if t >= 2:
                        pe.wait_ge(xt_ready, TURN * i + (t - 1))
                    for k in range(4):
                        mm = nc.tensor.transpose(bank[t % 2][:, k * P:(k + 1) * P], tok[:, t % 4, k], ident[:])
                    mm.then_inc(turned, 1)

                def up(t):
                    s = t // STEPS
                    if t % STEPS == 0:
                        pe.wait_ge(wload[s], 64 * i + 64)
                    pe.wait_ge(xt_ready, TURN * i + (t + 1))
                    for f in range(NF):
                        n = NF * t + f
                        if n >= 3:
                            pe.wait_ge(up_ready, NF * TURN * i + (n - 2))
                        nc.tensor.matmul(bank[2 + n % 3][:], w1[:, s, f * P:(f + 1) * P], xt[:, t % 2],
                                         start=True, stop=True).then_inc(up_psum, 1)

                def down(t):
                    s = t // STEPS
                    pe.wait_ge(up_ready, NF * TURN * i + NF * (t + 1))
                    if t >= 2:
                        pe.wait_ge(y_ready, TURN * i + (t - 1))
                    for k in range(4):
                        for f in range(NF):
                            mm = nc.tensor.matmul(bank[5 + t % 2][:, k * P:(k + 1) * P],
                                                  hid[:, t % 2, f, k * P:(k + 1) * P], w2[:, s, f],
                                                  start=(f == 0), stop=(f == NF - 1))
                    mm.then_inc(down_psum, 1)

                turn(0)
                for t in range(TURN + 1):
                    if t + 1 < TURN:
                        turn(t + 1)
                    if t < TURN:
                        up(t)
                    if t >= 1:
                        down(t - 1)
                pe.wait_ge(y_ready, TURN * i + TURN)

        @block.scalar
        def _(act):
            with act.Fori(0, E0 // 2) as i:
                for t in range(TURN):
                    for f in range(NF):
                        n = NF * t + f
                        act.wait_ge(up_psum, NF * TURN * i + (n + 1))
                        if t >= 2 and f == 0:
                            act.wait_ge(down_psum, TURN * i + (t - 1))
                        nc.scalar.activation(hid[:, t % 2, f], bank[2 + n % 3][:], ACT.Relu,
                                             bias=b1[:, t // STEPS, f:f + 1]).then_inc(up_ready, 1)
                    if t >= 1:
                        store(act, i, t - 1)
                store(act, i, TURN - 1)
                for s in range(2):
                    act.wait_ge(y_stored[s], 16 * (TURN // 2) * i + 16 * (TURN // 2))
                    act.sem_inc(passed, 1)

        @block.vector
        def _(dve):
            with dve.Fori(0, E0 // 2) as i:
                def cols(t):
                    dve.wait_ge(turned, TURN * i + (t + 1))
                    if t >= 2:
                        dve.wait_ge(up_psum, NF * TURN * i + NF * (t - 1))
                    nc.vector.tensor_copy(xt[:, t % 2], bank[t % 2][:]).then_inc(xt_ready, 1)

                cols(0)
                for t in range(TURN):
                    if t + 1 < TURN:
                        cols(t + 1)
                    if t % STEPS == 0:
                        dve.wait_ge(wload[t // STEPS], 64 * i + 64)
                    dve.wait_ge(down_psum, TURN * i + (t + 1))
                    if t >= 2:
                        dve.wait_ge(y_stored[t % 2], 16 * (TURN // 2) * i + 16 * (t // 2))
                    nc.vector.tensor_tensor(y[:, t % 2], bank[5 + t % 2][:].rearrange("p (k d) -> p k d", d=P),
                                            b2[:, t // STEPS].unsqueeze(1).broadcast_to([P, 4, P]),
                                            ALU.add).then_inc(y_ready, 1)
                for s in range(2):
                    dve.wait_ge(y_stored[s], 16 * (TURN // 2) * i + 16 * (TURN // 2))


NTL = M // P
K3 = 3
PC = W + K3 - 1
NH, NE = 4, 4
HF = NH * NE
ROW = HF + NH


def combine_and_conv(nc, passed, x1, yb, x3, hn, rows, adst, keep, w):
    slots_all, gates_all = keep
    with ExitStack() as ctx:
        sb = lambda n, s, d=F32: ctx.enter_context(nc.sbuf_tensor(f"c_{n}", s, d))
        sem = lambda n: ctx.enter_context(nc.semaphore(f"c_{n}"))
        bank = [ctx.enter_context(nc.psum_tensor(f"c_bank{i}", [P, NT], F32)) for i in range(8)]
        xs = sb("xs", [P, HW])
        xc = sb("xc", [P, HW])
        xp = sb("xp", [P, PC, PC])
        yt = sb("yt", [P, TILES, P])
        yg = sb("yg", [P, TILES, P])
        yc = sb("yc", [P, TILES, P])
        mask = sb("mask", [P, TILES, P], I32)
        rl = sb("rl", [P, 2, NT])
        w9 = sb("w9", [P, K3 * K3, P])
        bias = sb("bias", [P, 1])
        wg = sb("wg", [P, HF + 2 * NH])
        att = sb("att", [P, 2, HF])
        prod = sb("prod", [P, 2, HF])
        zero = sb("zero", [P, 1])
        tr = sb("tr", [P, TILES, ROW])
        td = sb("td", [P, TILES, NH])
        sidx = sb("sidx", [P, TILES], I32)
        gate = sb("gate", [P, TILES])
        ident = sb("ident", [P, P])
        ones = sb("ones", [P, P])
        eps6 = sb("eps6", [P, 1])
        eps5 = sb("eps5", [P, 1])
        ln = LayerNorm(nc, sb, sem, ones[:], [bank[0][:], bank[1][:]], [bank[2][:], bank[3][:]], "ln")

        consts, setup, setup_v = sem("consts"), sem("setup"), sem("setup_v")
        loaded = sem("loaded")
        slots_copied = sem("slots_copied")
        gathered = sem("gathered")
        y_taken = sem("y_taken")
        clean = sem("clean")
        y_psum = sem("y_psum")
        x2_ready = sem("x2_ready")
        conv_psum = sem("conv_psum")
        conv_act = sem("conv_act")
        x3_ready = sem("x3_ready")
        table_psum = sem("table_psum")
        table_ready = sem("table_ready")
        stored = sem("stored")
        NSTORE = 4

        block = ctx.enter_context(nc.Block())
        rows_d = rows.rearrange("(i t p) c -> i p t c", p=P, t=TILES)
        adst_d = adst.rearrange("(i t p) c -> i p t c", p=P, t=TILES)

        @block.sync
        def _(sp):
            for dst, src in ((w9[:], w["conv"]), (bias[:], w["conv_b"]), (wg[:, 0:HF], w["gat"]),
                             (att[:, 0], w["att_src"].broadcast_to([P, HF])),
                             (att[:, 1], w["att_dst"].broadcast_to([P, HF]))):
                sp.dma_start(dst, src).then_inc(consts, 16)
            with sp.Fori(0, B) as i:
                sp.dma_start(xs[:], x1[i]).then_inc(loaded, 16)
                sp.wait_ge(x3_ready, LT * i + LT)
                sp.dma_start(x3[i], xs[:]).then_inc(stored, 16)
                sp.wait_ge(ln.normed, 2 * LT * i + 2 * LT)
                sp.dma_start(hn[i], xc[:]).then_inc(stored, 16)
                sp.wait_ge(table_ready, 4 * i + 4)
                sp.dma_start(rows_d[i], tr[:]).then_inc(stored, 16)
                sp.dma_start(adst_d[i], td[:]).then_inc(stored, 16)
                sp.wait_ge(stored, 16 * NSTORE * i + 16 * NSTORE)
                sp.sem_inc(passed, 1)

        @block.gpsimd
        def _(pool):
            for k, (t, v) in enumerate(((ident, 0.0), (xp, 0.0), (ones, 1.0 / P), (eps6, 1e-6), (eps5, 1e-5),
                                        (zero, 0.0))):
                nc.gpsimd.memset(t[:], v).then_inc(setup, 1)
            pool.wait_ge(setup, 6)
            nc.gpsimd.affine_select(out=ident[:], in_=ident[:], compare_op=ALU.not_equal, fill=1.0, base=0,
                                    pattern=[[-1, P]], channel_multiplier=1).then_inc(setup, 1)

            def gather():
                for t in range(TILES):
                    nc.gpsimd.indirect_dma_start(yt[:, t], None, yb,
                                                 bass.IndirectOffsetOnAxis(ap=sidx[:, t:t + 1], axis=0)
                                                 ).then_inc(gathered, 16)

            pool.wait_ge(slots_copied, 1)
            gather()
            with pool.Fori(0, B) as i:
                pool.wait_ge(y_taken, i + 1)
                pool.wait_ge(slots_copied, i + 2)
                pool.sem_inc(passed, 1)
                gather()
                ln.gpsimd(pool, xc, lambda t: xp[:, 1 + 8 * t:9 + 8 * t, 1:1 + W], 2 * LT * i)
                ln.gpsimd(pool, xc, lambda t: xc[:, t * NT:(t + 1) * NT].rearrange("p (r w) -> p r w", w=W),
                          2 * LT * i + LT)
            pool.wait_ge(gathered, 16 * TILES * (B + 1))

        @block.tensor
        def _(pe):
            pe.wait_ge(setup, 7)
            pe.wait_ge(consts, 80)
            pe.wait_ge(setup_v, 5)
            with pe.Fori(0, B) as i:
                pe.wait_ge(clean, 6 * i + 6)
                for t in range(LT):
                    if t >= 4:
                        pe.wait_ge(x2_ready, LT * i + (t - 3))
                    for k in range(4):
                        mm = nc.tensor.transpose(bank[t % 4][:, k * P:(k + 1) * P], yc[:, 4 * t + k], ident[:])
                    mm.then_inc(y_psum, 1)
                pe.wait_ge(x2_ready, LT * i + LT)
                ln.tensor(pe, xs, 2 * LT * i)
                for t in range(LT):
                    pe.wait_ge(ln.normed, 2 * LT * i + min(t + 2, LT))
                    if t >= 2:
                        pe.wait_ge(conv_act, LT * i + (t - 1))
                    for k in range(K3 * K3):
                        a, b = k // K3, k % K3
                        mm = nc.tensor.matmul(bank[4 + t % 2][:], w9[:, k], xp[:, 8 * t + a:8 * t + a + 8, b:b + W],
                                              start=(k == 0), stop=(k == K3 * K3 - 1))
                    mm.then_inc(conv_psum, 1)
                pe.wait_ge(x3_ready, LT * i + LT)
                ln.tensor(pe, xs, 2 * LT * i + LT)
                pe.wait_ge(ln.normed, 2 * LT * i + 2 * LT)
                C = HF + 2 * NH
                for q in range(2):
                    for t in range(TILES // 2):
                        z = q * TILES // 2 + t
                        mm = nc.tensor.matmul(bank[6 + q][:, t * C:(t + 1) * C], xc[:, z * P:(z + 1) * P], wg[:],
                                              start=True, stop=True)
                    mm.then_inc(table_psum, 1)
                pe.wait_ge(table_ready, 4 * i + 4)

        @block.scalar
        def _(act):
            act.wait_ge(setup, 7)
            act.wait_ge(consts, 80)
            with act.Fori(0, B) as i:
                ln.scalar(act, xc, eps6[:], 2 * LT * i)
                for t in range(LT):
                    act.wait_ge(conv_psum, LT * i + (t + 1))
                    if t >= 2:
                        act.wait_ge(x3_ready, LT * i + (t - 1))
                    nc.scalar.activation(rl[:, t % 2], bank[4 + t % 2][:], ACT.Relu,
                                         bias=bias[:]).then_inc(conv_act, 1)
                ln.scalar(act, xc, eps5[:], 2 * LT * i + LT)

        @block.vector
        def _(dve):
            nc.vector.memset(slots_all[:, NTL:], 0).then_inc(setup_v, 1)
            dve.wait_ge(consts, 80)
            for k in range(2):
                nc.vector.tensor_tensor(prod[:, k], wg[:, 0:HF], att[:, k], ALU.mult).then_inc(setup_v, 1)
            dve.wait_ge(setup_v, 3)
            for k in range(2):
                nc.vector.tensor_reduce(wg[:, HF + NH * k:HF + NH * (k + 1)],
                                        prod[:, k].rearrange("p (h e) -> p h e", e=NE), AX.X,
                                        ALU.add).then_inc(setup_v, 1)
            nc.vector.tensor_copy(sidx[:], slots_all[:, 0:TILES]).then_inc(slots_copied, 1)
            with dve.Fori(0, B) as i:
                dve.wait_ge(gathered, 16 * TILES * i + 16 * TILES)
                nc.vector.tensor_copy(sidx[:], slots_all[:, bass.ts(i + 1, TILES)]).then_inc(slots_copied, 1)
                nc.vector.tensor_copy(gate[:], gates_all[:, bass.ts(i, TILES)]).then_inc(clean, 1)
                dve.wait_ge(clean, 6 * i + 1)
                nc.vector.tensor_tensor(yg[:], yt[:], gate[:].unsqueeze(2).broadcast_to([P, TILES, P]),
                                        ALU.mult).then_inc(y_taken, 1)
                dve.wait_ge(y_taken, i + 1)
                nc.vector.tensor_scalar(yc[:], yg[:], 1e4, -1e4, ALU.min, ALU.max).then_inc(clean, 1)
                nc.vector.tensor_scalar(mask[:], yg[:], 0.0, 0.0, ALU.mult, ALU.is_equal).then_inc(clean, 1)
                dve.wait_ge(clean, 6 * i + 3)
                dve.sem_inc(passed, 1)
                nc.vector.copy_predicated(yc[:], mask[:], yg[:]).then_inc(clean, 1)
                dve.wait_ge(clean, 6 * i + 4)
                nc.vector.tensor_tensor(mask[:], yg[:], yg[:], ALU.not_equal).then_inc(clean, 1)
                dve.wait_ge(clean, 6 * i + 5)
                dve.sem_inc(passed, 1)
                nc.vector.copy_predicated(yc[:].rearrange("p a b -> p (a b)"), mask[:].rearrange("p a b -> p (a b)"),
                                          zero[:].broadcast_to([P, TILES * P])).then_inc(clean, 1)
                dve.wait_ge(loaded, 16 * i + 16)
                for t in range(LT):
                    dve.wait_ge(y_psum, LT * i + (t + 1))
                    c = slice(t * NT, (t + 1) * NT)
                    nc.vector.tensor_tensor(xs[:, c], xs[:, c], bank[t % 4][:], ALU.add).then_inc(x2_ready, 1)
                ln.vector(dve, xs, xc, 2 * LT * i)
                for t in range(LT):
                    dve.wait_ge(conv_act, LT * i + (t + 1))
                    c = slice(t * NT, (t + 1) * NT)
                    nc.vector.tensor_tensor(xs[:, c], xs[:, c], rl[:, t % 2], ALU.add).then_inc(x3_ready, 1)
                ln.vector(dve, xs, xc, 2 * LT * i + LT)
                for q in range(2):
                    dve.wait_ge(table_psum, 2 * i + (q + 1))
                    src = bank[6 + q][:, 0:TILES // 2 * (HF + 2 * NH)].rearrange("p (t c) -> p t c", c=HF + 2 * NH)
                    h = slice(q * TILES // 2, (q + 1) * TILES // 2)
                    nc.vector.tensor_copy(tr[:, h], src[:, :, 0:ROW]).then_inc(table_ready, 1)
                    nc.vector.tensor_copy(td[:, h], src[:, :, ROW:]).then_inc(table_ready, 1)
                dve.wait_ge(stored, 16 * NSTORE * i + 16 * NSTORE)


N = M
NEDGE = 16 * N
FE = NEDGE // P
LF = FE.bit_length() - 1
LP = P.bit_length() - 1
RES = HF + 2 * NH
BIG = 1e30


def sort_edges(nc, src, dst, srcs, dsts, cont):
    with ExitStack() as ctx:
        sb = lambda n, s, d=F32: ctx.enter_context(nc.sbuf_tensor(f"s_{n}", s, d))
        sem = lambda n: ctx.enter_context(nc.semaphore(f"s_{n}"))
        bank = [ctx.enter_context(nc.psum_tensor(f"s_bank{i}", [P, NT], F32)) for i in range(8)]
        buf = [sb("keys0", [P, FE]), sb("keys1", [P, FE])]
        part = sb("part", [P, 1], I32)
        bit = sb("bit", [P, LP], I32)
        sign = sb("sign", [P, LP + 1])
        ident = sb("ident", [P, P])
        loaded, made, stage = sem("loaded"), sem("made"), sem("stage")
        turn_in, turn_psum, turn_act, turn_dve = sem("turn_in"), sem("turn_psum"), sem("turn_act"), sem("turn_dve")
        done, stored = sem("done"), sem("stored")

        steps = []
        for k in range(1, LF + LP + 1):
            if k >= LF:
                steps.append(("sign", k, 0))
            if k > LF:
                steps.append(("turn", 0, 0))
                steps += [("rows", k, j - LF) for j in range(k - 1, LF - 1, -1)]
                steps.append(("turn", 1, 0))
            steps += [("both" if k < LF else "rows", k, j) for j in range(min(k, LF) - 1, -1, -1)]
        NTURN = 8
        turns, at = [], 0
        for kind, back, _ in steps:
            if kind == "turn":
                turns.append((back, at))
            at ^= 1
        fin, other = buf[at], buf[1 - at]

        def bank_dst(t, q):
            back, a = turns[t]
            out = buf[1 - a][:]
            if back:
                return out.rearrange("p (q b) -> p b q", b=FE // P)[:, 4 * q:4 * q + 4]
            return out.rearrange("q (b p) -> q b p", p=P)[:, 4 * q:4 * q + 4]

        block = ctx.enter_context(nc.Block())

        @block.sync
        def _(sp):
            sp.dma_start(buf[0][:].bitcast(I32), dst).then_inc(loaded, 16)
            sp.dma_start(buf[1][:].bitcast(I32), src).then_inc(loaded, 16)
            sp.wait_ge(done, 1)
            sp.dma_start(srcs, other[:].bitcast(I32)).then_inc(stored, 16)
            sp.wait_ge(done, 2)
            sp.dma_start(dsts, fin[:].bitcast(I32)).then_inc(stored, 16)
            sp.wait_ge(done, 3)
            sp.dma_start(cont, other[:]).then_inc(stored, 16)
            sp.wait_ge(stored, 48)

        @block.gpsimd
        def _(pool):
            nc.gpsimd.iota(part[:], pattern=[[0, 1]], base=0, channel_multiplier=1).then_inc(made, 1)
            nc.gpsimd.memset(ident[:], 0.0).then_inc(made, 1)
            pool.wait_ge(made, 2)
            nc.gpsimd.affine_select(out=ident[:], in_=ident[:], compare_op=ALU.not_equal, fill=1.0, base=0,
                                    pattern=[[-1, P]], channel_multiplier=1).then_inc(made, 1)

        @block.tensor
        def _(pe):
            pe.wait_ge(made, 3)
            for t, (back, a) in enumerate(turns):
                pe.wait_ge(turn_in, t + 1)
                for q in range(NTURN):
                    if t:
                        pe.wait_ge((turn_act, turn_dve)[q % 2], (NTURN // 2) * (t - 1) + q // 2 + 1)
                    for z in range(4):
                        b = 4 * q + z
                        blk = (buf[a][:, b * P:(b + 1) * P] if back else
                               buf[a][:].rearrange("p (q b) -> p b q", b=FE // P)[:, b])
                        mm = nc.tensor.transpose(bank[q][:, z * P:(z + 1) * P], blk, ident[:])
                    mm.then_inc(turn_psum, 1)

        @block.scalar
        def _(act):
            for t in range(len(turns)):
                for q in range(0, NTURN, 2):
                    act.wait_ge(turn_psum, NTURN * t + q + 1)
                    nc.scalar.copy(bank_dst(t, q), bank[q][:].rearrange("p (b q) -> p b q", b=4)
                                   ).then_inc(turn_act, 1)

        @block.vector
        def _(dve):
            key = buf[0][:].bitcast(I32)
            dve.wait_ge(loaded, 32)
            nc.vector.tensor_scalar(key, key, 256.0, None, ALU.add).then_inc(stage, 1)
            dve.wait_ge(stage, 1)
            nc.vector.tensor_scalar(key, key, 15, None, ALU.logical_shift_left).then_inc(stage, 1)
            dve.wait_ge(stage, 2)
            nc.vector.tensor_tensor(key, key, buf[1][:].bitcast(I32), ALU.bitwise_or).then_inc(stage, 1)
            dve.wait_ge(made, 1)
            for c in range(LP):
                nc.vector.tensor_scalar(bit[:, c:c + 1], part[:], c, 1, ALU.logical_shift_right,
                                        ALU.bitwise_and).then_inc(stage, 1)
            dve.wait_ge(stage, 3 + LP)
            nc.vector.tensor_scalar(sign[:, 0:LP], bit[:], -2.0, 1.0, ALU.mult, ALU.add)
            nc.vector.memset(sign[:, LP:LP + 1], 1.0).then_inc(stage, 1)
            n, t, a = 4 + LP, 0, 0
            dve.wait_ge(stage, n)
            for kind, k, j in steps:
                x, y = buf[a][:], buf[1 - a][:]
                d = 1 << j
                if kind == "turn":
                    dve.sem_inc(turn_in, 1)
                    for q in range(1, NTURN, 2):
                        dve.wait_ge(turn_psum, NTURN * t + q + 1)
                        nc.vector.tensor_copy(bank_dst(t, q), bank[q][:].rearrange("p (b q) -> p b q", b=4)
                                              ).then_inc(turn_dve, 1)
                    t += 1
                    dve.wait_ge(turn_act, (NTURN // 2) * t)
                    dve.wait_ge(turn_dve, (NTURN // 2) * t)
                    a ^= 1
                    continue
                if kind == "sign":
                    m = k - LF
                    if m == 0:
                        ins = nc.vector.tensor_scalar(y, x, sign[:, 0:1], None, ALU.mult)
                    else:
                        ins = nc.vector.tensor_scalar(y, x, sign[:, m - 1:m], sign[:, m:m + 1], ALU.mult, ALU.mult)
                elif kind == "rows":
                    vx, vy = (v.rearrange("p (m two d) -> p m two d", two=2, d=d) for v in (x, y))
                    nc.vector.tensor_tensor(vy[:, :, 0], vx[:, :, 0], vx[:, :, 1], ALU.min)
                    ins = nc.vector.tensor_tensor(vy[:, :, 1], vx[:, :, 0], vx[:, :, 1], ALU.max)
                else:
                    vx, vy = (v.rearrange("p (n e m two d) -> p n e m two d", e=2, two=2, d=d, m=1 << (k - j - 1))
                              for v in (x, y))
                    for e in range(2):
                        nc.vector.tensor_tensor(vy[:, :, e, :, e], vx[:, :, e, :, 0], vx[:, :, e, :, 1], ALU.min)
                        ins = nc.vector.tensor_tensor(vy[:, :, e, :, 1 - e], vx[:, :, e, :, 0], vx[:, :, e, :, 1],
                                                      ALU.max)
                ins.then_inc(stage, 1)
                n += 1
                dve.wait_ge(stage, n)
                a ^= 1
            key = fin[:].bitcast(I32)
            nc.vector.tensor_scalar(other[:].bitcast(I32), key, (1 << 15) - 1, None, ALU.bitwise_and).then_inc(done, 1)
            dve.wait_ge(done, 1)
            nc.vector.tensor_scalar(key, key, 15, None, ALU.logical_shift_right).then_inc(stage, 1)
            dve.wait_ge(stage, n + 1)
            nc.vector.tensor_scalar(key, key, -256.0, None, ALU.add).then_inc(done, 1)
            dve.wait_ge(done, 2)
            dve.wait_ge(stored, 32)
            nc.vector.memset(other[:, 0:1], 0.0)
            nc.vector.tensor_tensor(other[:, 1:FE], key[:, 1:FE], key[:, 0:FE - 1], ALU.is_equal).then_inc(done, 1)


def count_edges(nc, passed, dst, ends, endtab):
    last_i, first_i, has = ends
    U = 16
    with ExitStack() as ctx:
        sb = lambda n, s, d=F32: ctx.enter_context(nc.sbuf_tensor(f"h_{n}", s, d))
        sem = lambda n: ctx.enter_context(nc.semaphore(f"h_{n}"))
        ps = [ctx.enter_context(nc.psum_tensor(f"h_ps{i}", [P, NT], F32)) for i in range(3)]
        raw = sb("raw", [P, 2, U], I32)
        bits = sb("bits", [P, 2, 2, U], I32)
        part = sb("part", [P, 2, 2, U])
        iota = sb("iota", [P, NTL], BF16)
        ioti = sb("ioti", [P, NTL], I32)
        lo = sb("lo", [P, 4, P], BF16)
        hi = sb("hi", [P, 4, NTL], BF16)
        zero = sb("zero", [P, NTL], BF16)
        cnt, cum, tot = sb("cnt", [P, NTL]), sb("cum", [P, NTL]), sb("tot", [P, NTL])
        endc, tmp = sb("endc", [P, NTL]), sb("tmp", [P, NTL])
        endt = sb("endt", [P, 2, P], I32)
        lower, ones, ident = sb("lower", [P, P]), sb("ones", [P, P]), sb("ident", [P, P])
        made, made_v = sem("made"), sem("made_v")
        loaded = [sem(f"loaded{s}") for s in range(2)]
        split = sem("split")
        taken = sem("taken")
        hot, counted, total = sem("hot"), sem("counted"), sem("total")
        chain, sums, turned, out = sem("chain"), sem("sums"), sem("turned"), sem("out")
        TURNS = FE // (2 * U)
        dchunk = dst.rearrange("p (n u) -> n p u", u=U)
        block = ctx.enter_context(nc.Block())

        @block.sync
        def _(sp):
            with sp.Fori(0, TURNS) as i:
                for s in range(2):
                    sp.wait_ge(taken, 2 * i + s + 1)
                    sp.dma_start(raw[:, s], dchunk[2 * i + s]).then_inc(loaded[s], 16)
            sp.wait_ge(chain, 20)
            sp.dma_start(endtab.rearrange("(q h l) c -> h q (l c)", q=2, l=P), endt[:]).then_inc(out, 16)
            sp.wait_ge(out, 16)

        @block.gpsimd
        def _(pool):
            nc.gpsimd.iota(ioti[:], pattern=[[1, NTL]], base=0, channel_multiplier=0).then_inc(made, 1)
            nc.gpsimd.memset(zero[:], 0.0).then_inc(made, 1)
            nc.gpsimd.memset(ones[:], 1.0).then_inc(made, 1)
            nc.gpsimd.memset(lower[:], 1.0).then_inc(made, 1)
            nc.gpsimd.memset(ident[:], 0.0).then_inc(made, 1)
            pool.wait_ge(made, 5)
            nc.gpsimd.affine_select(out=ident[:], in_=ident[:], compare_op=ALU.not_equal, fill=1.0, base=0,
                                    pattern=[[-1, P]], channel_multiplier=1).then_inc(made, 1)
            nc.gpsimd.affine_select(out=lower[:], in_=lower[:], compare_op=ALU.is_ge, fill=0.0, base=0,
                                    pattern=[[1, P]], channel_multiplier=-1).then_inc(made, 1)

        @block.tensor
        def _(pe):
            pe.wait_ge(made, 7)
            count = ps[0][:, 0:NTL]
            nc.tensor.matmul(count, zero[:, 0:P], zero[:], start=True, stop=False, skip_group_check=True)
            with pe.Fori(0, TURNS) as i:
                for c in range(2 * U):
                    pe.wait_ge(hot, 2 * U * i + (c + 1))
                    nc.tensor.matmul(count, lo[:, c % 4], hi[:, c % 4], start=False, stop=False,
                                     skip_group_check=True).then_inc(counted, 1)
            nc.tensor.matmul(count, zero[:, 0:P], zero[:], start=False, stop=True,
                             skip_group_check=True).then_inc(total, 1)
            pe.wait_ge(chain, 1)
            nc.tensor.matmul(ps[1][:, 0:NTL], lower[:], cnt[:], start=True, stop=True)
            nc.tensor.matmul(ps[1][:, NTL:2 * NTL], ones[:], cnt[:], start=True, stop=True).then_inc(sums, 1)
            pe.wait_ge(chain, 5)
            for q in range(2):
                mm = nc.tensor.transpose(ps[2][:, q * P:(q + 1) * P], endc[:, q * P:(q + 1) * P], ident[:])
            mm.then_inc(turned, 1)

        @block.vector
        def _(dve):
            dve.sem_inc(taken, 1)
            dve.wait_ge(made, 7)
            nc.vector.tensor_copy(iota[:], ioti[:]).then_inc(made_v, 1)
            dve.wait_ge(made_v, 1)
            dve.sem_inc(taken, 1)
            with dve.Fori(0, TURNS) as i:
                for s in range(2):
                    dve.wait_ge(loaded[s], 16 * i + 16)
                    nc.vector.tensor_scalar(bits[:, s, 0], raw[:, s], P - 1, None, ALU.bitwise_and)
                    nc.vector.tensor_scalar(bits[:, s, 1], raw[:, s], LP, None,
                                            ALU.logical_shift_right).then_inc(taken, 1)
                    dve.wait_ge(taken, 2 * i + s + 3)
                    nc.vector.tensor_copy(part[:, s], bits[:, s]).then_inc(split, 1)
                    dve.wait_ge(split, 2 * i + s + 1)
                    for u in range(U):
                        c = s * U + u
                        if c >= 4:
                            dve.wait_ge(counted, 2 * U * i + (c - 3))
                        nc.vector.tensor_scalar(lo[:, c % 4], iota[:, 0:P], part[:, s, 0, u:u + 1], None,
                                                ALU.is_equal)
                        nc.vector.tensor_scalar(hi[:, c % 4], iota[:], part[:, s, 1, u:u + 1], None,
                                                ALU.is_equal).then_inc(hot, 1)
                dve.wait_ge(counted, 2 * U * i + 2 * U)
            n = [0]

            def link(ins):
                n[0] += 1
                ins.then_inc(chain, 1)
                dve.wait_ge(chain, n[0])

            dve.wait_ge(total, 1)
            link(nc.vector.tensor_copy(cnt[:], ps[0][:, 0:NTL]))
            dve.wait_ge(sums, 1)
            link(nc.vector.tensor_copy(tot[:], ps[1][:, NTL:2 * NTL]))
            link(nc.vector.tensor_tensor_scan(cum[:], tot[:], tot[:], 0.0, ALU.add, ALU.bypass))
            link(nc.vector.tensor_tensor(cum[:], cum[:], tot[:], ALU.subtract))
            link(nc.vector.tensor_tensor(endc[:], cum[:], ps[1][:, 0:NTL], ALU.add))
            link(nc.vector.tensor_scalar(has[:], cnt[:], 1.0, None, ALU.min))
            link(nc.vector.tensor_scalar(tmp[:], endc[:], -1.0, 0.0, ALU.add, ALU.max))
            link(nc.vector.tensor_copy(last_i[:], tmp[:]))
            link(nc.vector.tensor_tensor(cum[:], endc[:], cnt[:], ALU.subtract))
            link(nc.vector.tensor_scalar(tmp[:], has[:], -2.0 * NEDGE, 2.0 * NEDGE, ALU.mult, ALU.add))
            link(nc.vector.tensor_tensor(cum[:], cum[:], tmp[:], ALU.add))
            link(nc.vector.tensor_copy(first_i[:], cum[:]))
            dve.wait_ge(turned, 1)
            nc.vector.tensor_copy(endt[:], ps[2][:, 0:2 * P].rearrange("p (q l) -> p q l", q=2)
                                  ).then_inc(chain, 8)


def spread_destinations(nc, adst, dsts, first_i, v):
    with ExitStack() as ctx:
        sb = lambda n, s, d=F32: ctx.enter_context(nc.sbuf_tensor(f"v_{n}", s, d))
        sem = lambda n: ctx.enter_context(nc.semaphore(f"v_{n}"))
        zeros = sb("zeros", [P, FE])
        td = sb("td", [P, NTL, NH])
        d0 = sb("d0", [P, 1], I32)
        a0 = sb("a0", [P, NH])
        made, zeroed, loaded, spread, got, fixed = (sem(n) for n in ("made", "zeroed", "loaded", "spread", "got",
                                                                     "fixed"))
        block = ctx.enter_context(nc.Block())

        @block.vector
        def _(dve):
            nc.vector.memset(zeros[:], 0.0).then_inc(made, 1)

        @block.sync
        def _(sp):
            sp.dma_start(td[:], adst.rearrange("(t p) c -> p t c", p=P)).then_inc(loaded, 16)
            sp.dma_start(d0[:], dsts[:, 0:1], allow_slow_non_contiguous=True).then_inc(loaded, 16)
            sp.wait_ge(made, 1)
            vz = v.rearrange("(q p f) c -> q p (f c)", q=4, p=P)
            for q in range(4):
                sp.dma_start(vz[q], zeros[:]).then_inc(zeroed, 16)
            sp.wait_ge(spread, 16 * NTL)
            sp.wait_ge(got, 16)
            sp.dma_start(v.rearrange("(p f) c -> p f c", p=P)[:, 0], a0[:]).then_inc(fixed, 16)
            sp.wait_ge(fixed, 16)

        @block.gpsimd
        def _(pool):
            pool.wait_ge(loaded, 32)
            nc.gpsimd.indirect_dma_start(a0[:], None, adst, bass.IndirectOffsetOnAxis(ap=d0[:], axis=0)
                                         ).then_inc(got, 16)
            pool.wait_ge(zeroed, 64)
            for t in range(NTL):
                nc.gpsimd.indirect_dma_start(v, bass.IndirectOffsetOnAxis(ap=first_i[:, t:t + 1], axis=0),
                                             td[:, t], None, bounds_check=NEDGE - 1, oob_is_err=False
                                             ).then_inc(spread, 16)
            pool.wait_ge(spread, 16 * NTL)


COMP = HF + NH


class Chain:

    def __init__(self, eng, sem, base=0):
        self.eng, self.sem, self.base, self.n = eng, sem, base, 0

    def __call__(self, ins):
        self.n += 1
        ins.then_inc(self.sem, 1)
        self.eng.wait_ge(self.sem, self.base + self.n)


def edge_states(nc, passed, rows, srcs, cont, v, res):
    U = 64
    TURNS = FE // (2 * U)
    with ExitStack() as ctx:
        sb = lambda n, s, d=F32: ctx.enter_context(nc.sbuf_tensor(f"e_{n}", s, d))
        sem = lambda n: ctx.enter_context(nc.semaphore(f"e_{n}"))
        allidx = sb("allidx", [P, FE + 2 * U], I32)
        idx = sb("idx", [P, 2, U], I32)
        same = sb("same", [P, 2, U])
        vd = sb("vd", [P, 2, U, NH])
        row = sb("row", [P, 2, U, ROW])
        neg = sb("neg", [P, U])
        dst = sb("dst", [P, 1 + U, NH])
        mx = sb("mx", [P, 1 + U, NH])
        score = sb("score", [P, U, NH])
        lrel = sb("lrel", [P, U, NH])
        dx = sb("dx", [P, 2, U, NH])
        ex = sb("ex", [P, 2, U, NH])
        msg = sb("msg", [P, U, NH, NE])
        st = sb("st", [P, 2, U, RES])
        loaded, init = sem("loaded"), sem("init")
        fload = [sem(f"flags_loaded{s}") for s in range(2)]
        gath = [sem(f"gathered{s}") for s in range(2)]
        idx_ready, slot_free, rows_free = sem("idx_ready"), sem("slot_free"), sem("rows_free")
        chain, dx_ready, ex_ready, st_ready = sem("chain"), sem("dx_ready"), sem("ex_ready"), sem("states_ready")
        stored = [sem(f"stored{s}") for s in range(2)]
        same_c = cont.rearrange("p (n u) -> n p u", u=U)
        v_c = v.rearrange("(p n u) c -> n p u c", p=P, u=U)
        res_c = res.rearrange("(p n u) c -> n p u c", p=P, u=U)
        block = ctx.enter_context(nc.Block())

        @block.sync
        def _(sp):
            sp.dma_start(allidx[:, 0:FE], srcs).then_inc(loaded, 16)
            with sp.Fori(0, TURNS) as i:
                for s in range(2):
                    sp.wait_ge(slot_free, 2 * i + s + 1)
                    sp.dma_start(same[:, s], same_c[2 * i + s]).then_inc(fload[s], 16)
                    sp.dma_start(vd[:, s], v_c[2 * i + s]).then_inc(fload[s], 16)

        @block.scalar
        def _(act):
            with act.Fori(0, TURNS) as i:
                for s in range(2):
                    act.wait_ge(dx_ready, 2 * i + s + 1)
                    nc.scalar.activation(ex[:], dx[:], ACT.Exp).then_inc(ex_ready, 1)
                    act.wait_ge(st_ready, 2 * i + s + 1)
                    act.dma_start(res_c[2 * i + s], st[:, s]).then_inc(stored[s], 16)
            for s in range(2):
                act.wait_ge(stored[s], 16 * TURNS)

        @block.gpsimd
        def _(pool):
            pool.sem_inc(rows_free, 2)
            with pool.Fori(0, TURNS) as i:
                for s in range(2):
                    pool.wait_ge(rows_free, 2 * i + s + 1)
                    pool.wait_ge(idx_ready, 2 * i + s + 1)
                    pool.sem_inc(passed, 1)
                    for u in range(U):
                        nc.gpsimd.indirect_dma_start(row[:, s, u], None, rows,
                                                     bass.IndirectOffsetOnAxis(ap=idx[:, s, u:u + 1], axis=0)
                                                     ).then_inc(gath[s], 16)
            for s in range(2):
                pool.wait_ge(gath[s], 16 * U * TURNS)

        @block.vector
        def _(dve):
            nc.vector.memset(allidx[:, FE:], 0)
            nc.vector.memset(st[:, 1], 0.0)
            nc.vector.memset(dst[:, U], 0.0)
            nc.vector.memset(mx[:, U], -BIG).then_inc(init, 1)
            dve.sem_inc(slot_free, 2)
            dve.wait_ge(loaded, 16)
            for s in range(2):
                nc.vector.tensor_copy(idx[:, s], allidx[:, s * U:(s + 1) * U]).then_inc(idx_ready, 1)
            dve.wait_ge(init, 1)
            K = 13
            with dve.Fori(0, TURNS) as i:
                for s in range(2):
                    n = 2 * i + s
                    link = Chain(dve, chain, K * n)
                    link(nc.vector.tensor_copy(mx[:, 0], mx[:, U]))
                    link(nc.vector.tensor_copy(dst[:, 0], dst[:, U]))
                    dve.wait_ge(fload[s], 32 * i + 32)
                    link(nc.vector.tensor_scalar(neg[:], same[:, s], BIG, -BIG, ALU.mult, ALU.add))
                    for h in range(NH):
                        last = nc.vector.tensor_tensor_scan(dst[:, 1:, h], same[:, s], vd[:, s, :, h],
                                                            dst[:, 0, h:h + 1], ALU.mult, ALU.add)
                    link(last)
                    dve.sem_inc(slot_free, 1)
                    dve.wait_ge(gath[s], 16 * U * i + 16 * U)
                    nc.vector.tensor_copy(idx[:, s], allidx[:, bass.ds((2 * i + s + 2) * U, U)]
                                          ).then_inc(idx_ready, 1)
                    link(nc.vector.tensor_tensor(score[:], row[:, s, :, HF:], dst[:, 1:], ALU.add))
                    link(nc.vector.scalar_tensor_tensor(out=lrel[:], in0=score[:], scalar=0.2, in1=score[:],
                                                        op0=ALU.mult, op1=ALU.max))
                    for h in range(NH):
                        last = nc.vector.tensor_tensor_scan(mx[:, 1:, h], neg[:], lrel[:, :, h], mx[:, 0, h:h + 1],
                                                            ALU.add, ALU.max)
                    link(last)
                    link(nc.vector.tensor_tensor(dx[:, 0], mx[:, 0:U], neg[:].unsqueeze(2).broadcast_to([P, U, NH]),
                                                 ALU.add))
                    link(nc.vector.tensor_tensor(dx[:, 0], dx[:, 0], mx[:, 1:], ALU.subtract))
                    link(nc.vector.tensor_tensor(dx[:, 1], lrel[:], mx[:, 1:], ALU.subtract))
                    dve.sem_inc(dx_ready, 1)
                    link(nc.vector.tensor_copy(st[:, s, :, COMP:], mx[:, 1:]))
                    dve.wait_ge(ex_ready, n + 1)
                    link(nc.vector.tensor_tensor(msg[:], row[:, s, :, 0:HF].rearrange("p u (h e) -> p u h e", e=NE),
                                                 ex[:, 1].unsqueeze(3).broadcast_to([P, U, NH, NE]), ALU.mult))
                    dve.sem_inc(rows_free, 1)
                    for c in range(COMP):
                        h = c // NE if c < HF else c - HF
                        add = msg[:, :, c // NE, c % NE] if c < HF else ex[:, 1, :, h]
                        last = nc.vector.tensor_tensor_scan(st[:, s, :, c], ex[:, 0, :, h], add,
                                                            st[:, 1 - s, U - 1, c:c + 1], ALU.mult, ALU.add)
                    link(last)
                    dve.sem_inc(st_ready, 1)
                    assert link.n == K, link.n
                for s in range(2):
                    dve.wait_ge(stored[s], 16 * i + 16)


def join_partitions(nc, res, dsts, endtab):
    with ExitStack() as ctx:
        sb = lambda n, s, d=F32: ctx.enter_context(nc.sbuf_tensor(f"j_{n}", s, d))
        sem = lambda n: ctx.enter_context(nc.semaphore(f"j_{n}"))
        ps = ctx.enter_context(nc.psum_tensor("j_ps", [P, NT], F32))
        pb = ctx.enter_context(nc.psum_tensor("j_pb", [P, NT], F32))
        ends = sb("ends", [P, RES])
        di = sb("di", [P, 3], I32)
        df = sb("df", [P, 3])
        place = sb("place", [P, 1], I32)
        pf = sb("pf", [P, 4])
        first = sb("first", [P, 1], I32)
        x3 = sb("x3", [P, 3, COMP])
        t3 = sb("t3", [COMP, 3, P])
        neg = sb("neg", [COMP, P])
        mc = sb("mc", [COMP, 1 + P])
        xc = sb("xc", [COMP, 1 + P])
        dx = sb("dx", [COMP, 2, P])
        fr = sb("fr", [P, 2, COMP])
        rr = sb("rr", [P, RES])
        gi = sb("gi", [P, 2], I32)
        d2 = sb("d2", [P, 2, COMP])
        new = sb("new", [P, RES])
        mn = sb("mn", [P, COMP])
        ident = sb("ident", [P, P])
        made, loaded, chain, asked, got = sem("made"), sem("loaded"), sem("chain"), sem("asked"), sem("got")
        turned, back, exps, exped, ready, put = (sem(n) for n in ("turned", "back", "exps", "exped", "ready", "put"))
        block = ctx.enter_context(nc.Block())

        @block.sync
        def _(sp):
            slow = dict(allow_slow_non_contiguous=True)
            sp.dma_start(ends[:], res.rearrange("(p f) c -> p f c", p=P)[:, FE - 1]).then_inc(loaded, 16)
            sp.dma_start(di[:, 0:1], dsts[:, FE - 1:FE], **slow).then_inc(loaded, 16)
            sp.dma_start(di[:, 2:3], dsts[:, 0:1], **slow).then_inc(loaded, 16)
            sp.wait_ge(made, 1)
            sp.dma_start(di[1:P, 1:2], dsts[0:P - 1, FE - 1:FE], **slow).then_inc(loaded, 16)

        @block.gpsimd
        def _(pool):
            nc.gpsimd.memset(di[:, 1:2], -1).then_inc(made, 1)
            nc.gpsimd.iota(first[:], pattern=[[0, 1]], base=0, channel_multiplier=FE).then_inc(made, 1)
            nc.gpsimd.memset(ident[:], 0.0).then_inc(made, 1)
            pool.wait_ge(made, 3)
            nc.gpsimd.affine_select(out=ident[:], in_=ident[:], compare_op=ALU.not_equal, fill=1.0, base=0,
                                    pattern=[[-1, P]], channel_multiplier=1).then_inc(made, 1)
            pool.wait_ge(asked, 1)
            nc.gpsimd.indirect_dma_start(place[:], None, endtab, bass.IndirectOffsetOnAxis(ap=gi[:, 0:1], axis=0)
                                         ).then_inc(got, 16)
            pool.wait_ge(asked, 2)
            nc.gpsimd.indirect_dma_start(rr[:], None, res, bass.IndirectOffsetOnAxis(ap=gi[:, 0:1], axis=0)
                                         ).then_inc(got, 16)
            pool.wait_ge(ready, 1)
            nc.gpsimd.indirect_dma_start(res, bass.IndirectOffsetOnAxis(ap=gi[:, 1:2], axis=0), new[:], None,
                                         bounds_check=NEDGE - 1, oob_is_err=False).then_inc(put, 16)
            pool.wait_ge(put, 16)

        @block.tensor
        def _(pe):
            pe.wait_ge(made, 4)
            pe.wait_ge(exps, 1)
            for k in range(3):
                mm = nc.tensor.transpose(ps[0:COMP, k * P:(k + 1) * P], x3[:, k], ident[:])
            mm.then_inc(turned, 1)
            pe.wait_ge(exps, 3)
            nc.tensor.transpose(pb[:, 0:COMP], xc[:, 0:P], ident[0:COMP, 0:COMP])
            nc.tensor.transpose(pb[:, COMP:2 * COMP], mc[:, 0:P], ident[0:COMP, 0:COMP]).then_inc(back, 1)

        @block.scalar
        def _(act):
            act.wait_ge(exps, 2)
            nc.scalar.activation(dx[:], dx[:], ACT.Exp).then_inc(exped, 1)
            act.wait_ge(exps, 4)
            nc.scalar.activation(d2[:], d2[:], ACT.Exp).then_inc(exped, 1)

        @block.vector
        def _(dve):
            link = Chain(dve, chain)
            by_head = lambda a: a.rearrange("p (h e) -> p h e", e=NE)
            dve.wait_ge(made, 4)
            dve.wait_ge(loaded, 64)
            nc.vector.tensor_copy(gi[:, 0:1], di[:, 2:3]).then_inc(asked, 1)
            link(nc.vector.tensor_copy(df[:], di[:]))
            nc.vector.tensor_copy(x3[:, 0], ends[:, 0:COMP])
            nc.vector.tensor_copy(by_head(x3[:, 1, 0:HF]), ends[:, COMP:].unsqueeze(2).broadcast_to([P, NH, NE]))
            nc.vector.tensor_copy(x3[:, 1, HF:], ends[:, COMP:])
            nc.vector.tensor_copy(x3[:, 2], df[:, 0:1].broadcast_to([P, COMP])).then_inc(exps, 1)
            dve.wait_ge(turned, 1)
            nc.vector.memset(mc[:, 0:1], -BIG)
            nc.vector.memset(xc[:, 0:1], 0.0)
            nc.vector.memset(neg[:, 0:1], 0.0)
            link(nc.vector.tensor_copy(t3[:], ps[0:COMP, 0:3 * P].rearrange("c (k p) -> c k p", k=3)))
            link(nc.vector.tensor_tensor(neg[:, 1:], t3[:, 2, 1:], t3[:, 2, 0:P - 1], ALU.is_equal))
            link(nc.vector.tensor_scalar(neg[:], neg[:], BIG, -BIG, ALU.mult, ALU.add))
            link(nc.vector.tensor_tensor_scan(mc[:, 1:], neg[:], t3[:, 1], -BIG, ALU.add, ALU.max))
            link(nc.vector.tensor_tensor(dx[:, 0], mc[:, 0:P], neg[:], ALU.add))
            link(nc.vector.tensor_tensor(dx[:, 0], dx[:, 0], mc[:, 1:], ALU.subtract))
            nc.vector.tensor_tensor(dx[:, 1], t3[:, 1], mc[:, 1:], ALU.subtract).then_inc(exps, 1)
            dve.wait_ge(exped, 1)
            link(nc.vector.tensor_tensor(dx[:, 1], dx[:, 1], t3[:, 0], ALU.mult))
            nc.vector.tensor_tensor_scan(xc[:, 1:], dx[:, 0], dx[:, 1], 0.0, ALU.mult, ALU.add).then_inc(exps, 1)
            dve.wait_ge(got, 16)
            link(nc.vector.tensor_copy(pf[:, 0:1], place[:]))
            link(nc.vector.tensor_copy(pf[:, 1:2], first[:]))
            link(nc.vector.tensor_scalar(pf[:, 0:1], pf[:, 0:1], -1.0, None, ALU.add))
            nc.vector.tensor_copy(gi[:, 0:1], pf[:, 0:1]).then_inc(asked, 1)
            link(nc.vector.tensor_tensor(pf[:, 1:2], pf[:, 0:1], pf[:, 1:2], ALU.subtract))
            link(nc.vector.tensor_scalar(pf[:, 1:2], pf[:, 1:2], float(FE), None, ALU.is_lt))
            link(nc.vector.tensor_tensor(pf[:, 2:3], df[:, 1:2], df[:, 2:3], ALU.is_equal))
            link(nc.vector.tensor_tensor(pf[:, 1:2], pf[:, 1:2], pf[:, 2:3], ALU.mult))
            link(nc.vector.tensor_scalar(pf[:, 1:2], pf[:, 1:2], -2.0 * NEDGE, 2.0 * NEDGE, ALU.mult, ALU.add))
            link(nc.vector.tensor_tensor(pf[:, 0:1], pf[:, 0:1], pf[:, 1:2], ALU.add))
            nc.vector.tensor_copy(gi[:, 1:2], pf[:, 0:1])
            dve.wait_ge(back, 1)
            link(nc.vector.tensor_copy(fr[:], pb[:, 0:2 * COMP].rearrange("p (k c) -> p k c", k=2)))
            dve.wait_ge(got, 32)
            nc.vector.tensor_copy(by_head(d2[:, 0, 0:HF]), rr[:, COMP:].unsqueeze(2).broadcast_to([P, NH, NE]))
            link(nc.vector.tensor_copy(d2[:, 0, HF:], rr[:, COMP:]))
            link(nc.vector.tensor_tensor(mn[:], d2[:, 0], fr[:, 1], ALU.max))
            link(nc.vector.tensor_tensor(d2[:, 0], d2[:, 0], mn[:], ALU.subtract))
            nc.vector.tensor_tensor(d2[:, 1], fr[:, 1], mn[:], ALU.subtract).then_inc(exps, 1)
            dve.wait_ge(exped, 2)
            link(nc.vector.tensor_tensor(new[:, 0:COMP], rr[:, 0:COMP], d2[:, 0], ALU.mult))
            link(nc.vector.tensor_tensor(d2[:, 1], d2[:, 1], fr[:, 0], ALU.mult))
            link(nc.vector.tensor_tensor(new[:, 0:COMP], new[:, 0:COMP], d2[:, 1], ALU.add))
            nc.vector.tensor_copy(new[:, COMP:], mn[:, HF:COMP]).then_inc(ready, 1)


def node_gates(nc, res, rows, adst, ends, gates, w):
    last_i, _, has = ends
    with ExitStack() as ctx:
        sb = lambda n, s, d=F32: ctx.enter_context(nc.sbuf_tensor(f"n_{n}", s, d))
        sem = lambda n: ctx.enter_context(nc.semaphore(f"n_{n}"))
        st = sb("st", [P, NTL, RES])
        tr = sb("tr", [P, NTL, ROW])
        td = sb("td", [P, NTL, NH])
        par = sb("par", [P, 3, HF])
        e4 = sb("e4", [P, NE])
        F4 = lambda n: sb(n, [P, NTL, NH])
        es, mh, mn, d0, d1, den = (F4(n) for n in ("es", "mh", "mn", "d0", "d1", "den"))
        agg = sb("agg", [P, NTL, HF])
        tmp = sb("tmp", [P, NTL, HF])
        hb = sb("hb", [P, NTL])
        mean = sb("mean", [P, NTL])
        var = sb("var", [P, NTL])
        m1, m2, i1 = (sb(n, [P, NTL]) for n in ("m1", "m2", "i1"))
        made, loaded, got, chain, asks, exped = (sem(n) for n in ("made", "loaded", "got", "chain", "asks", "exped"))
        block = ctx.enter_context(nc.Block())

        @block.sync
        def _(sp):
            sp.dma_start(tr[:], rows.rearrange("(t p) c -> p t c", p=P)).then_inc(loaded, 16)
            sp.dma_start(td[:], adst.rearrange("(t p) c -> p t c", p=P)).then_inc(loaded, 16)
            for k, n in enumerate(("b_gat", "ln_gamma", "ln_beta")):
                sp.dma_start(par[:, k], w[n].broadcast_to([P, HF])).then_inc(loaded, 16)

        @block.gpsimd
        def _(pool):
            nc.gpsimd.iota(e4[:], pattern=[[1, NE]], base=-NE, channel_multiplier=0,
                           allow_small_or_imprecise_dtypes=True).then_inc(made, 1)
            for t in range(NTL):
                nc.gpsimd.indirect_dma_start(st[:, t], None, res,
                                             bass.IndirectOffsetOnAxis(ap=last_i[:, t:t + 1], axis=0)
                                             ).then_inc(got, 16)

        @block.scalar
        def _(act):
            act.wait_ge(asks, 1)
            nc.scalar.activation(d0[:], d0[:], ACT.Exp)
            nc.scalar.activation(d1[:], d1[:], ACT.Exp).then_inc(exped, 1)
            act.wait_ge(asks, 2)
            nc.scalar.activation(var[:], var[:], ACT.Sqrt).then_inc(exped, 1)
            act.wait_ge(asks, 3)
            nc.scalar.activation(m2[:], m2[:], ACT.Exp).then_inc(exped, 1)

        @block.vector
        def _(dve):
            link = Chain(dve, chain)
            tt, ts = nc.vector.tensor_tensor, nc.vector.tensor_scalar
            A4 = [P, NTL, NH]
            A16 = [P, NTL, HF]
            per_node = lambda a, s=A4: a[:].unsqueeze(2).broadcast_to(s)
            heads = lambda a: a.rearrange("p t (h e) -> p t h e", e=NE)
            bh = lambda a: a[:].unsqueeze(3).broadcast_to([P, NTL, NH, NE])
            by_feature = lambda k: par[:, k].unsqueeze(1).broadcast_to(A16)
            dve.wait_ge(made, 1)
            dve.wait_ge(loaded, 80)
            link(tt(es[:], tr[:, :, HF:], td[:], ALU.add))
            link(nc.vector.scalar_tensor_tensor(out=es[:], in0=es[:], scalar=0.2, in1=es[:], op0=ALU.mult,
                                                op1=ALU.max))
            link(ts(hb[:], has[:], BIG, -BIG, ALU.mult, ALU.add))
            dve.wait_ge(got, 16 * NTL)
            link(tt(mh[:], st[:, :, COMP:], per_node(has), ALU.mult))
            link(tt(mh[:], mh[:], per_node(hb), ALU.add))
            link(tt(mn[:], mh[:], es[:], ALU.max))
            link(tt(d0[:], mh[:], mn[:], ALU.subtract))
            tt(d1[:], es[:], mn[:], ALU.subtract).then_inc(asks, 1)
            dve.wait_ge(exped, 1)
            link(tt(den[:], st[:, :, HF:COMP], d0[:], ALU.mult))
            link(tt(den[:], den[:], d1[:], ALU.add))
            link(ts(den[:], den[:], 1e-16, None, ALU.add))
            link(nc.vector.reciprocal(den[:], den[:]))
            link(tt(heads(agg[:]), heads(st[:, :, 0:HF]), bh(d0), ALU.mult))
            link(tt(heads(tmp[:]), heads(tr[:, :, 0:HF]), bh(d1), ALU.mult))
            link(tt(agg[:], agg[:], tmp[:], ALU.add))
            link(tt(heads(agg[:]), heads(agg[:]), bh(den), ALU.mult))
            link(tt(agg[:], agg[:], by_feature(0), ALU.add))
            link(nc.vector.tensor_reduce(mean[:], agg[:], AX.X, ALU.add))
            link(ts(mean[:], mean[:], 1.0 / HF, None, ALU.mult))
            link(tt(agg[:], agg[:], per_node(mean, A16), ALU.subtract))
            link(tt(tmp[:], agg[:], agg[:], ALU.mult))
            link(nc.vector.tensor_reduce(var[:], tmp[:], AX.X, ALU.add))
            ts(var[:], var[:], 1.0 / HF, 1e-5, ALU.mult, ALU.add).then_inc(asks, 1)
            dve.wait_ge(exped, 2)
            link(nc.vector.reciprocal(var[:], var[:]))
            link(tt(agg[:], agg[:], per_node(var, A16), ALU.mult))
            link(tt(agg[:], agg[:], by_feature(1), ALU.mult))
            link(tt(agg[:], agg[:], by_feature(2), ALU.add))
            link(nc.vector.tensor_reduce(es[:], agg[:].rearrange("p t (h e) -> p t e h", e=NE), AX.X, ALU.add))
            link(ts(es[:], es[:], 1.0 / NH, None, ALU.mult))
            be = e4[:].unsqueeze(1).broadcast_to(A4)

            def pick(scores, top, hot):
                link(nc.vector.tensor_reduce(top[:], scores[:], AX.X, ALU.max))
                link(tt(hot[:], scores[:], per_node(top), ALU.is_equal))
                link(tt(hot[:], hot[:], be, ALU.mult))
                link(nc.vector.tensor_reduce(i1[:], hot[:], AX.X, ALU.min))
                link(tt(hot[:], be, per_node(i1), ALU.is_equal))

            pick(es, m1, d0)
            link(nc.vector.scalar_tensor_tensor(out=mh[:], in0=d0[:], scalar=-BIG, in1=es[:], op0=ALU.mult,
                                                op1=ALU.add))
            pick(mh, m2, d1)
            tt(m2[:], m2[:], m1[:], ALU.subtract).then_inc(asks, 1)
            dve.wait_ge(exped, 3)
            link(ts(m1[:], m2[:], 1.0, None, ALU.add))
            link(nc.vector.reciprocal(m1[:], m1[:]))
            link(tt(m2[:], m2[:], m1[:], ALU.mult))
            link(tt(d0[:], d0[:], per_node(m1), ALU.mult))
            link(tt(d1[:], d1[:], per_node(m2), ALU.mult))
            link(tt(gates[:], d0[:], d1[:], ALU.add))


def gelu_experts(nc, passed, hn, x3, y, gates, w):
    F1 = 2 * P
    NF = F1 // P
    K = NT // P
    with ExitStack() as ctx:
        sb = lambda n, s, d=F32: ctx.enter_context(nc.sbuf_tensor(f"f_{n}", s, d))
        sem = lambda n: ctx.enter_context(nc.semaphore(f"f_{n}"))
        bank = [ctx.enter_context(nc.psum_tensor(f"f_bank{i}", [P, NT], F32)) for i in range(8)]
        h = sb("h", [P, 2, HW])
        xo = sb("xo", [P, 2, HW])
        hid = sb("hid", [P, 2, NF, NT])
        acc = sb("acc", [P, 2, K, P])
        g = sb("g", [P, 2, TILES, NE])
        yb2 = sb("yb2", [P, 2, K, P])
        w1 = sb("w1", [P, NE, F1])
        w2 = sb("w2", [P, NE, NF, P])
        b1 = sb("b1", [P, NE, NF])
        b2 = sb("b2", [P, NE, P])
        ident = sb("ident", [P, P])
        consts, setup = sem("consts"), sem("setup")
        loaded = [sem(f"image_loaded{s}") for s in range(2)]
        g_ready = sem("gates_ready")
        up_psum, up_ready, down_psum = sem("up_psum"), sem("up_ready"), sem("down_psum")
        biased = sem("biased")
        added = sem("added")
        turned = sem("turned")
        out_ready = sem("out_ready")
        stored = [sem(f"stored{s}") for s in range(2)]
        IMG = NE * LT
        block = ctx.enter_context(nc.Block())

        @block.sync
        def _(sp):
            for dst, src in ((w1[:], w["w1"].rearrange("e d f -> d e f")),
                             (w2[:], w["w2"].rearrange("e (f p) d -> p e f d", p=P)),
                             (b1[:], w["b1"]),
                             (b2[:].rearrange("p e d -> p (e d)"), w["b2"].broadcast_to([P, NE * P]))):
                sp.dma_start(dst, src).then_inc(consts, 16)
            with sp.Fori(0, B // 2) as i:
                for s in range(2):
                    sp.dma_start(h[:, s], hn[2 * i + s]).then_inc(loaded[s], 16)
                    sp.dma_start(xo[:, s], x3[2 * i + s]).then_inc(loaded[s], 16)
                for s in range(2):
                    sp.wait_ge(out_ready, 2 * LT * i + LT * (s + 1))
                    sp.dma_start(y[2 * i + s], xo[:, s]).then_inc(stored[s], 16)
                for s in range(2):
                    sp.wait_ge(stored[s], 16 * i + 16)
                    sp.sem_inc(passed, 1)

        @block.gpsimd
        def _(pool):
            nc.gpsimd.memset(ident[:], 0.0).then_inc(setup, 1)
            pool.wait_ge(setup, 1)
            nc.gpsimd.affine_select(out=ident[:], in_=ident[:], compare_op=ALU.not_equal, fill=1.0, base=0,
                                    pattern=[[-1, P]], channel_multiplier=1).then_inc(setup, 1)

        @block.tensor
        def _(pe):
            pe.wait_ge(setup, 2)
            pe.wait_ge(consts, 64)
            with pe.Fori(0, B // 2) as i:
                def up(n):
                    s, t, e = n // IMG, n % IMG // NE, n % NE
                    if n % IMG == 0:
                        pe.wait_ge(loaded[s], 32 * i + 32)
                    for f in range(NF):
                        m = NF * n + f
                        if m >= 3:
                            pe.wait_ge(up_ready, 2 * NF * IMG * i + (m - 2))
                        nc.tensor.matmul(bank[m % 3][:], w1[:, e, f * P:(f + 1) * P], h[:, s, t * NT:(t + 1) * NT],
                                         start=True, stop=True).then_inc(up_psum, 1)

                def down(n):
                    e = n % NE
                    pe.wait_ge(up_ready, 2 * NF * IMG * i + NF * (n + 1))
                    if n >= 3:
                        pe.wait_ge(added, 2 * IMG * i + (n - 2))
                    for k in range(K):
                        for f in range(NF):
                            mm = nc.tensor.matmul(bank[3 + n % 3][:, k * P:(k + 1) * P],
                                                  hid[:, n % 2, f, k * P:(k + 1) * P], w2[:, e, f],
                                                  start=(f == 0), stop=(f == NF - 1))
                    mm.then_inc(down_psum, 1)

                def turn(r):
                    pe.wait_ge(added, 2 * IMG * i + NE * (r + 1))
                    if r >= 2:
                        pe.wait_ge(out_ready, 2 * LT * i + (r - 1))
                    for k in range(K):
                        mm = nc.tensor.transpose(bank[6 + r % 2][:, k * P:(k + 1) * P], acc[:, r % 2, k], ident[:])
                    mm.then_inc(turned, 1)

                for n in range(2 * IMG):
                    up(n)
                    if n >= 1:
                        down(n - 1)
                    if n % NE == 1 and n > NE:
                        turn(n // NE - 1)
                down(2 * IMG - 1)
                turn(2 * LT - 1)
                pe.wait_ge(out_ready, 2 * LT * i + 2 * LT)

        @block.scalar
        def _(act):
            act.wait_ge(consts, 64)
            with act.Fori(0, B // 2) as i:
                for n in range(2 * IMG):
                    if n >= 2:
                        act.wait_ge(down_psum, 2 * IMG * i + (n - 1))
                    for f in range(NF):
                        m = NF * n + f
                        act.wait_ge(up_psum, 2 * NF * IMG * i + (m + 1))
                        nc.scalar.activation(hid[:, n % 2, f], bank[m % 3][:], ACT.Gelu,
                                             bias=b1[:, n % NE, f:f + 1]).then_inc(up_ready, 1)
                act.wait_ge(down_psum, 2 * IMG * i + 2 * IMG)

        @block.vector
        def _(dve):
            dve.wait_ge(consts, 64)
            with dve.Fori(0, B // 2) as i:
                def bias(n):
                    dve.wait_ge(down_psum, 2 * IMG * i + (n + 1))
                    if n >= 2:
                        dve.wait_ge(added, 2 * IMG * i + (n - 1))
                    nc.vector.tensor_tensor(yb2[:, n % 2], bank[3 + n % 3][:].rearrange("p (k d) -> p k d", d=P),
                                            b2[:, n % NE].unsqueeze(1).broadcast_to([P, K, P]),
                                            ALU.add).then_inc(biased, 1)

                def weigh(n):
                    r, e = divmod(n, NE)
                    s, t = divmod(r, LT)
                    dve.wait_ge(biased, 2 * IMG * i + (n + 1))
                    if n:
                        dve.wait_ge(added, 2 * IMG * i + n)
                    if e == 0 and r >= 2:
                        dve.wait_ge(turned, 2 * LT * i + (r - 1))
                    for k in range(K):
                        gate = g[:, s, K * t + k, e:e + 1]
                        if e == 0:
                            last = nc.vector.tensor_scalar(acc[:, r % 2, k], yb2[:, n % 2, k], gate, None, ALU.mult)
                        else:
                            last = nc.vector.scalar_tensor_tensor(out=acc[:, r % 2, k], in0=yb2[:, n % 2, k],
                                                                  scalar=gate, in1=acc[:, r % 2, k],
                                                                  op0=ALU.mult, op1=ALU.add)
                    last.then_inc(added, 1)

                def out(r):
                    s, t = divmod(r, LT)
                    dve.wait_ge(turned, 2 * LT * i + (r + 1))
                    c = slice(t * NT, (t + 1) * NT)
                    nc.vector.tensor_tensor(xo[:, s, c], xo[:, s, c], bank[6 + r % 2][:],
                                            ALU.add).then_inc(out_ready, 1)

                nc.vector.tensor_copy(g[:], gates[:, bass.ts(i, 2 * TILES)].rearrange("p (s t) e -> p s t e", s=2)
                                      ).then_inc(g_ready, 1)
                dve.wait_ge(g_ready, i + 1)
                bias(0)
                for n in range(2 * IMG):
                    if n + 1 < 2 * IMG:
                        bias(n + 1)
                    weigh(n)
                    if n % NE == NE - 2 and n > NE:
                        if n // NE % LT == 1:
                            dve.wait_ge(loaded[n // IMG], 32 * i + 32)
                        out(n // NE - 1)
                out(2 * LT - 1)


def metaformer(nc, x, y, w):
    scratch = lambda n, s, d=F32: nc.dram_tensor(n, s, d, kind="Internal").ap()
    x1, x3, hn = (scratch(n, (B, P, HW)) for n in ("x1_dram", "x3_dram", "hn_dram"))
    xb, yb = scratch("xb_dram", (SLOTS, P)), scratch("yb_dram", (SLOTS, P))
    rows, adst = scratch("rows_dram", (M, ROW)), scratch("adst_dram", (M, NH))
    srcs, dsts = scratch("srcs_dram", (P, FE), I32), scratch("dsts_dram", (P, FE), I32)
    cont = scratch("cont_dram", (P, FE))
    endtab = scratch("endtab_dram", (N, 1), I32)
    v = scratch("v_dram", (NEDGE, NH))
    res = scratch("res_dram", (NEDGE, RES))
    with ExitStack() as ctx:
        keep = lambda n, s, d: ctx.enter_context(nc.sbuf_tensor(f"keep_{n}", s, d))
        slots = keep("slots", [P, NTL + TILES], I32)
        gates0 = keep("gates0", [P, NTL], F32)
        last_i, first_i = keep("last_i", [P, NTL], I32), keep("first_i", [P, NTL], I32)
        has = keep("has", [P, NTL], F32)
        gates1 = keep("gates1", [P, NTL, NE], F32)
        passed = ctx.enter_context(nc.semaphore("passed"))
        sort_edges(nc, w["src"], w["dst"], srcs, dsts, cont)
        count_edges(nc, passed, w["dst"], (last_i, first_i, has), endtab)
        involution_and_routing(nc, passed, x, x1, xb, (slots, gates0), w["involution"])
        experts(nc, passed, xb, yb, w["experts"])
        combine_and_conv(nc, passed, x1, yb, x3, hn, rows, adst, (slots, gates0), w["conv"])
        spread_destinations(nc, adst, dsts, first_i, v)
        edge_states(nc, passed, rows, srcs, cont, v, res)
        join_partitions(nc, res, dsts, endtab)
        node_gates(nc, res, rows, adst, (last_i, first_i, has), gates1, w["gates"])
        gelu_experts(nc, passed, hn, x3, y, gates1, w["gelu"])


def kernel(**inputs):
    import concourse.bacc as bacc
    from concourse.bass_utils import run_bass_kernel_spmd

    a = {n: np.asarray(v) for n, v in inputs.items()}
    l0, l1, f0, f1 = (lambda n, k=k: a[k + n] for k in ("L0_conv_", "L1_conv_", "L0_ffn_", "L1_ffn_"))
    row = lambda v: v.reshape(1, -1)
    weights = {
        "involution": {"w1t": l0("w1").T, "w2t": l0("w2").T, "b2": row(l0("b2")),
                       "bn": np.stack([l0(n) for n in ("b1", "bn_gamma", "bn_beta", "bn_mean", "bn_var")], axis=1),
                       "gate_w": f0("gate_w"), "gate_b": row(f0("gate_b"))},
        "experts": {"w1": f0("w1"), "w2": f0("w2"), "b1": f0("b1").reshape(E0, F0 // P, P).transpose(0, 2, 1),
                    "b2": f0("b2").reshape(E0, 1, P)},
        "conv": {"conv": l1("weight").transpose(1, 2, 3, 0).reshape(P, K3 * K3, P),
                 "conv_b": l1("bias").reshape(P, 1), "gat": f1("W_gat"),
                 "att_src": row(f1("att_src")), "att_dst": row(f1("att_dst"))},
        "gates": {n: row(f1(n)) for n in ("b_gat", "ln_gamma", "ln_beta")},
        "gelu": {"w1": f1("W1"), "w2": f1("W2"), "b1": f1("b1").reshape(NE, 2, P).transpose(2, 0, 1),
                 "b2": row(f1("b2"))},
    }
    nc = bacc.Bacc("TRN2", target_bir_lowering=False, num_devices=1)
    arrays = {}

    def put(name, v):
        arrays[name] = np.ascontiguousarray(v)
        return nc.dram_tensor(name, arrays[name].shape, mybir.dt.from_np(arrays[name].dtype),
                              kind="ExternalInput").ap()

    w = {stage: {n: put(f"in_{stage}_{n}", v) for n, v in group.items()} for stage, group in weights.items()}
    edges = f1("edge_index").astype(np.int32)
    w["src"], w["dst"] = put("in_src", edges[0].reshape(P, FE)), put("in_dst", edges[1].reshape(P, FE))
    x = put("in_x", a["x"].reshape(B, P, HW))
    y = nc.dram_tensor("out_y", (B, P, HW), F32, kind="ExternalOutput").ap()
    metaformer(nc, x, y, w)
    r = run_bass_kernel_spmd(nc, [arrays], core_ids=[0])
    return r.results[0]["out_y"].reshape(B, P, H, W)
```

```python
from contextlib import ExitStack

import numpy as np
import concourse.bass as bass
from concourse import mybir

ALU = mybir.AluOpType
ACT = mybir.ActivationFunctionType
AX = mybir.AxisListType
F32 = mybir.dt.float32
BF16 = mybir.dt.bfloat16
I32 = mybir.dt.int32

P = 128
B, H, W = 8, 64, 64
HW = H * W
M = B * HW
TILES = HW // P
NT = 512
LT = HW // NT

KS, G, CR = 7, 4, 32
TAPS = KS * KS
GC = P // G
OUT = 5
IN = OUT + KS - 1
PR = -(-H // OUT)
NP = PR * PR
PO = PR * OUT
PI = PO + KS - 1
KIN = IN * IN
NOUT = OUT * OUT
LEAD = (OUT - 1) * (IN + 1)
CAN = LEAD + KIN

NEDGE = 16 * M
FE = NEDGE // P
LP = P.bit_length() - 1
NHI = M // P
COUNT0 = 368
COUNT1 = FE // B - COUNT0

E0, F0 = 8, 512
CAP = -(-5 * M // (4 * E0))
SLOTS = E0 * CAP


class LayerNorm:

    def __init__(self, nc, sb, sem, tag):
        self.nc = nc
        self.ones = sb(f"{tag}_ones", [P, P], F32)
        self.pick = sb(f"{tag}_pick", [P, LT, LT], F32)
        self.spread = sb(f"{tag}_spread", [LT, LT, P], F32)
        self.sq = sb(f"{tag}_sq", [P, 2, NT], F32)
        self.rstd = sb(f"{tag}_rstd", [LT, NT], F32)
        self.made = sem(f"{tag}_made")
        self.mean_ready = sem(f"{tag}_mean_ready")
        self.centred = sem(f"{tag}_centred")
        self.squared = sem(f"{tag}_squared")
        self.var_ready = sem(f"{tag}_var_ready")
        self.dev_ready = sem(f"{tag}_dev_ready")
        self.rstd_ready = sem(f"{tag}_rstd_ready")
        self.factors = sem(f"{tag}_factors")
        self.normed = sem(f"{tag}_normed")

    def use(self, psum_mean, psum_var):
        self.pm, self.pv = psum_mean, psum_var

    def constants(self, pool):
        g = self.nc.gpsimd
        g.memset(self.ones[:], 1.0 / P).then_inc(self.made, 1)
        g.memset(self.pick[:], 0.0).then_inc(self.made, 1)
        g.memset(self.spread[:], 0.0).then_inc(self.made, 1)
        pool.wait_ge(self.made, 3)
        g.affine_select(out=self.pick[:], in_=self.pick[:], compare_op=ALU.not_equal, fill=1.0 / P, base=0,
                        pattern=[[1, LT], [-1, LT]], channel_multiplier=0).then_inc(self.made, 1)
        g.affine_select(out=self.spread[:], in_=self.spread[:], compare_op=ALU.not_equal, fill=1.0, base=0,
                        pattern=[[-1, LT], [0, P]], channel_multiplier=1).then_inc(self.made, 1)

    def tensor(self, pe, x, run):
        base = LT * run

        def var(t):
            pe.wait_ge(self.squared, base + (t + 1))
            self.nc.tensor.matmul(self.pv[0:LT, :], self.pick[:, t], self.sq[:, t % 2], start=(t == 0),
                                  stop=(t == LT - 1)).then_inc(self.var_ready, 1)

        for t in range(LT):
            if t >= 2:
                pe.wait_ge(self.centred, base + (t - 1))
            self.nc.tensor.matmul(self.pm[t % 2], self.ones[:], x[:, t * NT:(t + 1) * NT], start=True,
                                  stop=True).then_inc(self.mean_ready, 1)
            if t >= 1:
                var(t - 1)
        var(LT - 1)
        pe.wait_ge(self.rstd_ready, run + 1)
        for t in range(LT):
            if t >= 2:
                pe.wait_ge(self.normed, base + (t - 1))
            self.nc.tensor.matmul(self.pm[t % 2], self.spread[:, t], self.rstd[:], start=True,
                                  stop=True).then_inc(self.factors, 1)

    def scalar(self, act, xc, eps, run):
        base = LT * run
        for t in range(LT):
            act.wait_ge(self.centred, base + (t + 1))
            if t >= 2:
                act.wait_ge(self.var_ready, base + (t - 1))
            self.nc.scalar.activation(self.sq[:, t % 2], xc[:, t * NT:(t + 1) * NT],
                                      ACT.Square).then_inc(self.squared, 1)
        act.wait_ge(self.var_ready, base + LT)
        self.nc.scalar.activation(self.rstd[:], self.pv[0:LT, :], ACT.Sqrt,
                                  bias=eps[0:LT]).then_inc(self.dev_ready, 1)

    def vector(self, dve, x, xc, out, run):
        base = LT * run
        for t in range(LT):
            dve.wait_ge(self.mean_ready, base + (t + 1))
            c = slice(t * NT, (t + 1) * NT)
            self.nc.vector.tensor_tensor(xc[:, c], x[:, c], self.pm[t % 2],
                                         ALU.subtract).then_inc(self.centred, 1)
        dve.wait_ge(self.dev_ready, run + 1)
        self.nc.vector.reciprocal(self.rstd[:], self.rstd[:]).then_inc(self.rstd_ready, 1)
        for t in range(LT):
            dve.wait_ge(self.factors, base + (t + 1))
            self.nc.vector.tensor_tensor(out(t), xc[:, t * NT:(t + 1) * NT].rearrange("p (r w) -> p r w", w=W),
                                         self.pm[t % 2].rearrange("p (r w) -> p r w", w=W),
                                         ALU.mult).then_inc(self.normed, 1)


class EdgeCount:
    RING = 20

    def __init__(self, nc, sb, sem, dst, counts, psum, columns, portions, tag):
        self.nc, self.dst, self.counts, self.psum, self.C, self.portions = nc, dst, counts, psum, columns, portions
        self.raw = sb(f"{tag}_raw", [P, 2, columns], I32)
        self.part = sb(f"{tag}_part", [P, 2, columns], F32)
        self.iotai = sb(f"{tag}_iotai", [P, NHI], I32)
        self.iota = sb(f"{tag}_iota", [P, NHI], BF16)
        self.hot = sb(f"{tag}_hot", [P, self.RING, P + NHI], BF16)
        self.made = sem(f"{tag}_made")
        self.loaded = sem(f"{tag}_loaded")
        self.split = sem(f"{tag}_split")
        self.hot_ready = sem(f"{tag}_hot_ready")
        self.counted = sem(f"{tag}_counted")

    def cols(self, k):
        return range(self.C * k // self.portions, self.C * (k + 1) // self.portions)

    def constants(self, pool):
        self.nc.gpsimd.iota(self.iotai[:], pattern=[[1, NHI]], base=0, channel_multiplier=0).then_inc(self.made, 1)

    def first(self, dve):
        dve.wait_ge(self.made, 1)
        self.nc.vector.tensor_copy(self.iota[:], self.iotai[:]).then_inc(self.made, 1)
        dve.wait_ge(self.made, 2)

    def load(self, sp, i):
        sp.dma_start(self.raw[:, 0], self.dst[:, bass.ts(i, self.C)]).then_inc(self.loaded, 16)

    def begin(self, dve, i):
        dve.wait_ge(self.loaded, 16 * i + 16)
        v, s = self.nc.vector, self.split
        v.tensor_scalar(self.raw[:, 1], self.raw[:, 0], LP, None, ALU.logical_shift_right).then_inc(s, 1)
        dve.wait_ge(s, 3 * i + 1)
        v.tensor_scalar(self.raw[:, 0], self.raw[:, 0], P - 1, None, ALU.bitwise_and).then_inc(s, 1)
        dve.wait_ge(s, 3 * i + 2)
        v.tensor_copy(self.part[:], self.raw[:]).then_inc(s, 1)
        dve.wait_ge(s, 3 * i + 3)

    def make(self, dve, i, k):
        for c in self.cols(k):
            if c >= self.RING:
                dve.wait_ge(self.counted, self.C * i + (c - self.RING + 1))
            h = self.hot[:, c % self.RING]
            self.nc.vector.tensor_scalar(h[:, 0:P], self.iota[:, 0:P], self.part[:, 0, c:c + 1], None, ALU.is_equal)
            self.nc.vector.tensor_scalar(h[:, P:], self.iota[:], self.part[:, 1, c:c + 1], None,
                                         ALU.is_equal).then_inc(self.hot_ready, 1)

    def count(self, pe, i, k):
        for c in self.cols(k):
            pe.wait_ge(self.hot_ready, self.C * i + (c + 1))
            h = self.hot[:, c % self.RING]
            self.nc.tensor.matmul(self.psum, h[:, 0:P], h[:, P:], start=(c == 0),
                                  stop=(c == self.C - 1)).then_inc(self.counted, 1)

    def end(self, dve, i):
        dve.wait_ge(self.counted, self.C * i + self.C)
        self.nc.vector.tensor_tensor(self.counts[:], self.counts[:], self.psum, ALU.add)


def involution_and_routing(nc, passed, x, x1, xb, keep, edges, ln, ident, w):
    slots_all, gates_all = keep
    with ExitStack() as ctx:
        sb = lambda n, s, d: ctx.enter_context(nc.sbuf_tensor(f"a_{n}", s, d))
        sem = lambda n: ctx.enter_context(nc.semaphore(n))
        bank = [ctx.enter_context(nc.psum_tensor(f"a_bank{i}", [P, NT], F32)) for i in range(8)]

        xs = sb("xs", [P, HW], F32)
        xc = sb("xc", [P, HW], F32)
        xp = sb("xp", [P, PI, PI], F32)
        hid = sb("hid", [CR + 1, PO, PO], F32)
        taps = sb("taps", [P, G * NOUT, NP], F32)
        so = sb("so", [P, PO, PO], F32)
        ht = so[:].rearrange("p a b -> p (a b)")[:, 0:HW].rearrange("p (t c) -> p t c", c=P)
        xq = [xc[:, z * PR * KIN:(z + 1) * PR * KIN] for z in range(2)]
        xt = sb("xt", [P, 3, 4, P], F32)
        upper = sb("upper", [P, P], BF16)
        onesb = sb("onesb", [P, P], BF16)
        w1t = sb("w1t", [P, CR], F32)
        w2t = sb("w2t", [CR + 1, G, TAPS], F32)
        canvas = sb("canvas", [CR + 1, G, CAN], F32)
        wsum = sb("wsum", [CR + 1, G], F32)
        wsumt = sb("wsumt", [CR + 1, G, GC], F32)
        bn = sb("bn", [CR, 8], F32)
        eps6 = sb("eps6", [P, 1], F32)
        eps5 = sb("eps5", [P, 1], F32)
        gw = sb("gw", [P, E0], F32)
        gb = sb("gb", [P, E0], F32)
        em8 = sb("em8", [P, E0], F32)
        carry = sb("carry", [P, E0], F32)
        R = lambda n, d=F32: sb(n, [P, TILES, E0], d)
        lg, ex, eq, oh, cum, pos = R("lg"), R("ex"), R("eq"), R("oh"), R("cum"), R("pos")
        ohb = R("ohb", BF16)
        T1 = lambda n, d=F32: sb(n, [P, TILES], d)
        mx, se, prb, ix, pt, kept, sl, sg = [T1(n) for n in ("mx", "se", "prb", "ix", "pt", "kept", "sl", "sg")]
        sidx = T1("sidx", I32)
        sgi = T1("sgi", I32)

        ln.use([bank[0][:], bank[1][:]], bank[2])

        loaded = sem("a_loaded")
        consts = sem("a_consts")
        setup = sem("a_setup")
        setup_v = sem("a_setup_v")
        bn_chain = sem("a_bn_chain")
        zeroed = sem("a_zeroed")
        hid_psum = sem("a_hid_psum")
        hid_ready = sem("a_hid_ready")
        ws_psum = sem("a_ws_psum")
        scaled = sem("a_scaled")
        taps_psum = sem("a_taps_psum")
        taps_act = sem("a_taps_act")
        taps_dve = sem("a_taps_dve")
        patch_rows = sem("a_patch_rows")
        patch_psum = sem("a_patch_psum")
        patch_act = sem("a_patch_act")
        patch_dve = sem("a_patch_dve")
        sum_psum = sem("a_sum_psum")
        sum_act = sem("a_sum_act")
        sum_dve = sem("a_sum_dve")
        x1_ready = sem("a_x1_ready")
        x1_stored = sem("a_x1_stored")
        tok_psum = sem("a_tok_psum")
        tok_act = sem("a_tok_act")
        logit_psum = sem("a_logit_psum")
        shifted = sem("a_shifted")
        exps = sem("a_exps")
        chosen = sem("a_chosen")
        rank_psum = sem("a_rank_psum")
        chain = sem("a_chain")
        slots_ready = sem("a_slots_ready")
        scattered = sem("a_scattered")
        ht_free = sem("a_ht_free")

        NB3 = -(-G * NOUT // 3)
        NX4 = -(-NP // 4)
        cols = [(0, 5), (5, 10), (10, 13)]
        NS = PR * len(cols)

        dst, counts = edges

        def bank_of(z):
            return (z // PR) * 3 + (0 if z % PR < 5 else 1 if z % PR < 10 else 2)

        def group_end(u):
            return bank_of(min(4 * u + 3, NP - 1)) + 1

        order = []
        done = 0
        for u in range(NX4):
            while done < NS and u >= 3 and done < group_end(u - 3):
                order.append(("sum", done))
                done += 1
            order.append(("patch", u))
        order += [("sum", v) for v in range(done, NS)]

        hist = EdgeCount(nc, sb, sem, dst[:, 0:B * COUNT0], counts, bank[0][:, 0:NHI], COUNT0, len(order), "cnta")
        LAG = 3

        def sums(eng, copy, i, v, groups, s):
            a, (b0, b1) = v // 3, cols[v % 3]
            eng.wait_ge(sum_psum, NS * i + (v + 1))
            for g in groups:
                src = bank[6 + v % 2][GC * g:GC * (g + 1), 0:(b1 - b0) * G * NOUT].rearrange(
                    "p (b g r c) -> p b g r c", g=G, r=OUT, c=OUT)[:, :, g]
                dst = so[GC * g:GC * (g + 1), OUT * a:OUT * (a + 1), OUT * b0:OUT * b1].rearrange(
                    "p r (b c) -> p b r c", c=OUT)
                last = copy(dst, src)
            last.then_inc(s, 1)

        block = ctx.enter_context(nc.Block())

        @block.sync
        def _(sp):
            for dst, src in ((w1t[:], w["w1t"]), (w2t[0:CR].rearrange("k g t -> k (g t)"), w["w2t"]),
                             (w2t[CR:CR + 1].rearrange("k g t -> k (g t)"), w["b2"]),
                             (bn[:, 0:5], w["bn"]), (gw[:], w["gate_w"]),
                             (gb[:], w["gate_b"].broadcast_to([P, E0]))):
                sp.dma_start(dst, src).then_inc(consts, 16)
            sp.wait_ge(setup_v, 1)
            xbz = xb.rearrange("(p r) d -> p (r d)", p=P)
            step = SLOTS // 4
            for q in range(4):
                sp.dma_start(xbz[:, q * step:(q + 1) * step],
                             taps[:].rearrange("p a b -> p (a b)")[:, 0:step]).then_inc(zeroed, 16)
            with sp.Fori(0, B) as i:
                hist.load(sp, i)
                sp.dma_start(xs[:], x[i]).then_inc(loaded, 16)
                sp.wait_ge(x1_ready, LT * i + LT)
                sp.dma_start(x1[i], xs[:]).then_inc(x1_stored, 16)
                sp.wait_ge(ln.centred, 2 * LT * i + 2 * LT)
                sp.wait_ge(x1_stored, 16 * i + 16)
                sp.sem_inc(passed, 1)

        @block.gpsimd
        def _(pool):
            pool.sem_inc(ht_free, 1)
            nc.gpsimd.memset(xp[:], 0.0).then_inc(setup, 1)
            ln.constants(pool)
            hist.constants(pool)
            nc.gpsimd.memset(onesb[:], 1.0).then_inc(setup, 1)
            nc.gpsimd.memset(upper[:], 1.0).then_inc(setup, 1)
            nc.gpsimd.memset(eps6[:], 1e-6).then_inc(setup, 1)
            nc.gpsimd.memset(eps5[:], 1e-5).then_inc(setup, 1)
            nc.gpsimd.iota(em8[:], pattern=[[1, E0]], base=-E0, channel_multiplier=0,
                           allow_small_or_imprecise_dtypes=True).then_inc(setup, 1)
            pool.wait_ge(setup, 6)
            nc.gpsimd.affine_select(out=upper[:], in_=upper[:], compare_op=ALU.is_gt, fill=0.0, base=0,
                                    pattern=[[1, P]], channel_multiplier=-1).then_inc(setup, 1)
            pool.wait_ge(setup, 7)
            with pool.Fori(0, B) as i:
                pool.wait_ge(ln.normed, 2 * LT * i + LT)
                for a in range(PR):
                    if a >= 2:
                        pool.wait_ge(patch_psum, NX4 * i + (PR * (a - 1) - 1) // 4 + 1)
                    pool.sem_inc(passed, 1)
                    rows = xp[:, OUT * a:OUT * a + IN]
                    nc.gpsimd.tensor_copy(
                        xq[a % 2].rearrange("p (b r c) -> p b r c", r=IN, c=IN),
                        bass.AP(tensor=rows.tensor, offset=rows.offset,
                                ap=[list(rows.ap[0]), [OUT, PR], [PI, IN], [1, IN]])).then_inc(patch_rows, 1)
                pool.wait_ge(slots_ready, i + 1)
                pool.wait_ge(tok_act, LT * i + LT)
                pool.wait_ge(zeroed, 64)
                pool.sem_inc(passed, 1)
                for t in range(TILES):
                    nc.gpsimd.indirect_dma_start(
                        xb, bass.IndirectOffsetOnAxis(ap=sidx[:, t:t + 1], axis=0), ht[:, t], None,
                        bounds_check=SLOTS - 1, oob_is_err=False).then_inc(scattered, 16)
                pool.wait_ge(scattered, 16 * TILES * i + 16 * TILES)
                pool.sem_inc(ht_free, 1)

        @block.tensor
        def _(pe):
            pe.wait_ge(setup, 7)
            pe.wait_ge(ln.made, 5)
            pe.wait_ge(setup_v, 5)
            pe.wait_ge(consts, 96)
            with pe.Fori(0, B) as i:
                pe.wait_ge(loaded, 16 * i + 16)
                ln.tensor(pe, xs, 2 * i)
                for t in range(LT):
                    pe.wait_ge(ln.normed, 2 * LT * i + (t + 1))
                    if t >= 2:
                        pe.wait_ge(hid_ready, LT * i + (t - 1))
                    nc.tensor.matmul(bank[4 + t % 2][0:CR, :], w1t[:], xp[:, 3 + 8 * t:11 + 8 * t, 3:3 + W],
                                     start=True, stop=True).then_inc(hid_psum, 1)
                pe.wait_ge(hid_ready, LT * i + LT)
                for q in range(NB3):
                    if q >= 4:
                        s, o = (taps_act, q - 4) if q % 2 == 0 else (taps_dve, q - 4)
                        pe.wait_ge(s, (NB3 // 2) * i + (o // 2 + 1))
                    for z in range(3 * q, min(3 * q + 3, G * NOUT)):
                        g, n = z // NOUT, z % NOUT
                        r, c = n // OUT, n % OUT
                        at = LEAD - (IN * r + c)
                        nc_mm = nc.tensor.matmul(
                            bank[q % 4][0:KIN, (z % 3) * NP:(z % 3 + 1) * NP], canvas[:, g, at:at + KIN],
                            hid[:, r::OUT, c::OUT], start=True, stop=True)
                    nc_mm.then_inc(taps_psum, 1)

                def transposed(u):
                    if u >= 2:
                        s = (patch_act, patch_dve)[u % 2]
                        n = (NX4 + 1) // 2 if u % 2 == 0 else NX4 // 2
                        pe.wait_ge(s, n * i + ((u - 2) // 2 + 1))
                    last_row = min(4 * u + 3, NP - 1) // PR
                    pe.wait_ge(patch_rows, PR * i + last_row + 1)
                    for z in range(4 * u, min(4 * u + 4, NP)):
                        a, b = z // PR, z % PR
                        mm = nc.tensor.transpose(bank[4 + u % 2][0:KIN, (z % 4) * P:(z % 4 + 1) * P],
                                                 xq[a % 2][:, b * KIN:(b + 1) * KIN], ident[:])
                    mm.then_inc(patch_psum, 1)

                events = [0]

                def event():
                    events[0] += 1
                    if events[0] > LAG:
                        hist.count(pe, i, events[0] - LAG - 1)

                transposed(0)
                transposed(1)
                u_next = 2
                events[0] = 2
                pe.wait_ge(taps_act, (NB3 // 2) * i + NB3 // 2)
                pe.wait_ge(taps_dve, (NB3 // 2) * i + NB3 // 2)
                for v in range(NS):
                    a, (b0, b1) = v // 3, cols[v % 3]
                    if v >= 2:
                        pe.wait_ge(sum_act, NS * i + (v - 1))
                        pe.wait_ge(sum_dve, NS * i + (v - 1))
                    for b in range(b0, b1):
                        z = a * PR + b
                        u = z // 4
                        if z % 4 == 0:
                            s = (patch_act, patch_dve)[u % 2]
                            n = (NX4 + 1) // 2 if u % 2 == 0 else NX4 // 2
                            pe.wait_ge(s, n * i + (u // 2 + 1))
                        mm = nc.tensor.matmul(bank[6 + v % 2][:, (b - b0) * G * NOUT:(b - b0 + 1) * G * NOUT],
                                              xt[0:KIN, u % 3, z % 4, :], taps[0:KIN, :, z], start=True, stop=True)
                        if z % 4 == 3 and u_next < NX4:
                            transposed(u_next)
                            u_next += 1
                            event()
                    mm.then_inc(sum_psum, 1)
                    event()
                for k in range(len(order) - LAG, len(order)):
                    hist.count(pe, i, k)
                for t in range(LT):
                    if t >= 3:
                        pe.wait_ge(scaled, LT * i + (t - 2))
                    nc.tensor.matmul(bank[1 + t % 3][:], wsumt[:].rearrange("k g c -> k (g c)"),
                                     hid[:, 8 * t:8 * t + 8, 0:W], start=True, stop=True).then_inc(ws_psum, 1)
                pe.wait_ge(x1_ready, LT * i + LT)
                ln.tensor(pe, xs, 2 * i + 1)
                pe.wait_ge(ln.normed, 2 * LT * i + 2 * LT)
                for t in range(LT):
                    if t >= 4:
                        pe.wait_ge(tok_act, LT * i + (t - 3))
                    for k in range(4):
                        mm = nc.tensor.transpose(bank[t % 4][:, k * P:(k + 1) * P],
                                                 xc[:, t * NT + k * P:t * NT + (k + 1) * P], ident[:])
                    mm.then_inc(tok_psum, 1)
                for t in range(TILES):
                    mm = nc.tensor.matmul(bank[4][:, t * E0:(t + 1) * E0], xc[:, t * P:(t + 1) * P], gw[:],
                                          start=True, stop=True)
                mm.then_inc(logit_psum, 1)
                pe.wait_ge(chosen, i + 1)
                o2 = ohb[:].rearrange("p t e -> p (t e)")
                nc.tensor.matmul(bank[5][:, 0:256], upper[:], o2, start=True, stop=True)
                nc.tensor.matmul(bank[5][:, 256:512], onesb[:], o2, start=True, stop=True).then_inc(rank_psum, 1)
                pe.wait_ge(tok_act, LT * i + LT)

        @block.scalar
        def _(act):
            act.wait_ge(setup, 7)
            act.wait_ge(setup_v, 4)
            nc.scalar.activation(bn[:, 7:8], bn[:, 7:8], ACT.Sqrt).then_inc(bn_chain, 1)
            act.wait_ge(setup_v, 5)
            with act.Fori(0, B) as i:
                act.wait_ge(loaded, 16 * i + 16)
                ln.scalar(act, xc, eps6, 2 * i)
                for t in range(LT):
                    act.wait_ge(hid_psum, LT * i + (t + 1))
                    nc.scalar.activation(hid[0:CR, 8 * t:8 * t + 8, 0:W],
                                         bank[4 + t % 2][0:CR, :].rearrange("p (r w) -> p r w", w=W), ACT.Relu,
                                         bias=bn[:, 6:7], scale=bn[:, 5:6]).then_inc(hid_ready, 1)
                for q in range(0, NB3, 2):
                    act.wait_ge(taps_psum, NB3 * i + (q + 1))
                    n = min(3, G * NOUT - 3 * q)
                    nc.scalar.activation(taps[0:KIN, 3 * q:3 * q + n].rearrange("p a b -> p (a b)"),
                                         bank[q % 4][0:KIN, 0:n * NP], ACT.Copy).then_inc(taps_act, 1)

                def patches(u):
                    act.wait_ge(patch_psum, NX4 * i + (u + 1))
                    if u >= 3:
                        act.wait_ge(sum_psum, NS * i + group_end(u - 3))
                    n = min(4, NP - 4 * u)
                    nc.scalar.activation(xt[0:KIN, u % 3, 0:n].rearrange("p a b -> p (a b)"),
                                         bank[4 + u % 2][0:KIN, 0:n * P], ACT.Copy).then_inc(patch_act, 1)

                for kind, n in order:
                    if kind == "patch":
                        if n % 2 == 0:
                            patches(n)
                    else:
                        sums(act, nc.scalar.copy, i, n, (0, 1), sum_act)
                ln.scalar(act, xc, eps5, 2 * i + 1)
                act.wait_ge(ht_free, i + 1)
                for t in range(LT):
                    act.wait_ge(tok_psum, LT * i + (t + 1))
                    nc.scalar.activation(ht[:, 4 * t:4 * t + 4].rearrange("p a b -> p (a b)"), bank[t % 4][:],
                                         ACT.Copy).then_inc(tok_act, 1)
                act.wait_ge(shifted, i + 1)
                nc.scalar.activation(ex[:], lg[:], ACT.Exp).then_inc(exps, 1)

        @block.vector
        def _(dve):
            nc.vector.memset(taps[:].rearrange("p a b -> p (a b)"), 0.0).then_inc(setup_v, 1)
            nc.vector.memset(hid[:], 0.0)
            nc.vector.memset(canvas[:], 0.0)
            nc.vector.memset(carry[:], 0.0).then_inc(setup_v, 1)
            nc.vector.memset(counts[:], 0.0)
            hist.first(dve)
            dve.wait_ge(setup_v, 2)
            nc.vector.memset(hid[CR:CR + 1], 1.0)
            dve.wait_ge(consts, 96)
            for g in range(G):
                nc.vector.tensor_copy(canvas[:, g, LEAD:LEAD + KS * IN].rearrange("k (a b) -> k a b", b=IN)[:, :, 0:KS],
                                      w2t[:, g].rearrange("k (a b) -> k a b", b=KS))
            nc.vector.tensor_reduce(wsum[:], w2t[:], AX.X, ALU.add).then_inc(setup_v, 1)
            dve.wait_ge(setup_v, 3)
            nc.vector.tensor_copy(wsumt[:], wsum[:].unsqueeze(2).broadcast_to([CR + 1, G, GC]))
            nc.vector.tensor_scalar(bn[:, 7:8], bn[:, 4:5], 1e-5, None, ALU.add).then_inc(setup_v, 1)
            dve.wait_ge(bn_chain, 1)
            nc.vector.reciprocal(bn[:, 5:6], bn[:, 7:8]).then_inc(bn_chain, 1)
            dve.wait_ge(bn_chain, 2)
            nc.vector.tensor_tensor(bn[:, 5:6], bn[:, 5:6], bn[:, 1:2], ALU.mult).then_inc(bn_chain, 1)
            nc.vector.tensor_tensor(bn[:, 6:7], bn[:, 0:1], bn[:, 3:4], ALU.subtract).then_inc(bn_chain, 1)
            dve.wait_ge(bn_chain, 4)
            nc.vector.scalar_tensor_tensor(out=bn[:, 6:7], in0=bn[:, 6:7], scalar=bn[:, 5:6], in1=bn[:, 2:3],
                                           op0=ALU.mult, op1=ALU.add).then_inc(setup_v, 1)
            with dve.Fori(0, B) as i:
                hist.begin(dve, i)
                dve.wait_ge(loaded, 16 * i + 16)
                ln.vector(dve, xs, xc, lambda t: xp[:, 3 + 8 * t:11 + 8 * t, 3:3 + W], 2 * i)
                for q in range(1, NB3, 2):
                    dve.wait_ge(taps_psum, NB3 * i + (q + 1))
                    n = min(3, G * NOUT - 3 * q)
                    nc.vector.tensor_copy(taps[0:KIN, 3 * q:3 * q + n].rearrange("p a b -> p (a b)"),
                                          bank[q % 4][0:KIN, 0:n * NP]).then_inc(taps_dve, 1)
                dve.wait_ge(ht_free, i + 1)
                for k, (kind, n) in enumerate(order):
                    hist.make(dve, i, k)
                    if kind == "patch":
                        if n % 2 == 1:
                            u = n
                            dve.wait_ge(patch_psum, NX4 * i + (u + 1))
                            if u >= 3:
                                dve.wait_ge(sum_psum, NS * i + group_end(u - 3))
                            m = min(4, NP - 4 * u)
                            nc.vector.tensor_copy(xt[0:KIN, u % 3, 0:m].rearrange("p a b -> p (a b)"),
                                                  bank[4 + u % 2][0:KIN, 0:m * P]).then_inc(patch_dve, 1)
                    else:
                        sums(dve, nc.vector.tensor_copy, i, n, (2, 3), sum_dve)
                hist.end(dve, i)
                K = 21
                n = [0]

                def link(ins):
                    n[0] += 1
                    ins.then_inc(chain, 1)
                    dve.wait_ge(chain, K * i + n[0])

                dve.wait_ge(sum_act, NS * i + NS)
                dve.wait_ge(sum_dve, NS * i + NS)
                xv = xs[:].rearrange("p (r w) -> p r w", w=W)

                def add(t):
                    dve.wait_ge(scaled, LT * i + (t + 1))
                    c = slice(8 * t, 8 * t + 8)
                    nc.vector.tensor_tensor(xv[:, c], xv[:, c], so[:, c, 0:W], ALU.add).then_inc(x1_ready, 1)

                for t in range(LT):
                    dve.wait_ge(ws_psum, LT * i + (t + 1))
                    c = slice(8 * t, 8 * t + 8)
                    nc.vector.tensor_tensor(so[:, c, 0:W], so[:, c, 0:W],
                                            bank[1 + t % 3][:].rearrange("p (r w) -> p r w", w=W),
                                            ALU.mult).then_inc(scaled, 1)
                    if t:
                        add(t - 1)
                add(LT - 1)
                dve.wait_ge(x1_ready, LT * i + LT)
                ln.vector(dve, xs, xc, lambda t: xc[:, t * NT:(t + 1) * NT].rearrange("p (r w) -> p r w", w=W),
                          2 * i + 1)
                dve.wait_ge(logit_psum, i + 1)
                full = [P, TILES, E0]
                link(nc.vector.tensor_tensor(lg[:], bank[4][:, 0:256].rearrange("p (t e) -> p t e", e=E0),
                                             gb[:].unsqueeze(1).broadcast_to(full), ALU.add))
                link(nc.vector.tensor_reduce(mx[:], lg[:], AX.X, ALU.max))
                nc.vector.tensor_tensor(lg[:], lg[:], mx[:].unsqueeze(2).broadcast_to(full),
                                        ALU.subtract).then_inc(shifted, 1)
                dve.wait_ge(shifted, i + 1)
                link(nc.vector.tensor_scalar(eq[:], lg[:], 0.0, None, ALU.is_equal))
                link(nc.vector.tensor_tensor(eq[:], eq[:], em8[:].unsqueeze(1).broadcast_to(full), ALU.mult))
                link(nc.vector.tensor_reduce(ix[:], eq[:], AX.X, ALU.min))
                link(nc.vector.tensor_tensor(oh[:], em8[:].unsqueeze(1).broadcast_to(full),
                                             ix[:].unsqueeze(2).broadcast_to(full), ALU.is_equal))
                nc.vector.tensor_copy(ohb[:], oh[:]).then_inc(chosen, 1)
                dve.wait_ge(exps, i + 1)
                link(nc.vector.tensor_reduce(se[:], ex[:], AX.X, ALU.add))
                link(nc.vector.reciprocal(prb[:], se[:]))
                dve.wait_ge(rank_psum, i + 1)
                rank = bank[5][:, 0:256].rearrange("p (t e) -> p t e", e=E0)
                link(nc.vector.tensor_copy(ex[:], bank[5][:, 256:512].rearrange("p (t e) -> p t e", e=E0)))
                for e in range(E0):
                    last = nc.vector.tensor_tensor_scan(cum[:, :, e], ex[:, :, e], ex[:, :, e],
                                                        carry[:, e:e + 1], ALU.add, ALU.bypass)
                link(last)
                link(nc.vector.tensor_copy(carry[:], cum[:, TILES - 1]))
                link(nc.vector.tensor_tensor(cum[:], cum[:], ex[:], ALU.subtract))
                link(nc.vector.tensor_tensor(cum[:], cum[:], rank, ALU.add))
                link(nc.vector.tensor_tensor(pos[:], cum[:], oh[:], ALU.mult))
                link(nc.vector.tensor_reduce(pt[:], pos[:], AX.X, ALU.add))
                link(nc.vector.tensor_scalar(kept[:], pt[:], float(CAP), None, ALU.is_lt))
                link(nc.vector.tensor_scalar(sl[:], ix[:], float(E0), float(CAP), ALU.add, ALU.mult))
                link(nc.vector.tensor_tensor(sl[:], sl[:], pt[:], ALU.add))
                link(nc.vector.tensor_tensor(sg[:], sl[:], kept[:], ALU.mult))
                nc.vector.tensor_copy(slots_all[:, bass.ts(i, TILES)], sg[:])
                nc.vector.tensor_tensor(gates_all[:, bass.ts(i, TILES)], prb[:], kept[:], ALU.mult)
                link(nc.vector.tensor_scalar(pt[:], kept[:], -float(2 * SLOTS), float(2 * SLOTS), ALU.mult,
                                             ALU.add))
                link(nc.vector.tensor_tensor(sl[:], sl[:], pt[:], ALU.add))
                dve.wait_ge(ht_free, i + 1)
                nc.vector.tensor_copy(sidx[:], sl[:]).then_inc(slots_ready, 1)
                assert n[0] == K, n[0]


def experts(nc, passed, xb, yb, ident, w):
    NF = F0 // P
    STEPS = CAP // NT
    TURN = 2 * STEPS
    with ExitStack() as ctx:
        sb = lambda n, s, d=F32: ctx.enter_context(nc.sbuf_tensor(f"b_{n}", s, d))
        sem = lambda n: ctx.enter_context(nc.semaphore(f"b_{n}"))
        bank = [ctx.enter_context(nc.psum_tensor(f"b_bank{i}", [P, NT], F32)) for i in range(8)]
        tok = sb("tok", [P, 4, 4, P])
        xt = sb("xt", [P, 2, NT])
        hid = sb("hid", [P, 2, NF, NT])
        y = sb("y", [P, 2, 4, P])
        w1 = sb("w1", [P, 2, F0])
        w2 = sb("w2", [P, 2, NF, P])
        b1 = sb("b1", [P, 2, NF])
        b2 = sb("b2", [P, 2, P])

        wload = [sem(f"weights_loaded_{s}") for s in range(2)]
        xload = [sem(f"slots_loaded_{s}") for s in range(4)]
        turned = sem("turned")
        xt_ready = sem("xt_ready")
        up_psum = sem("up_psum")
        up_ready = sem("up_ready")
        down_psum = sem("down_psum")
        y_ready = sem("y_ready")
        y_stored = [sem(f"y_stored_{s}") for s in range(2)]

        xn = xb.rearrange("(n p k) d -> n p k d", p=P, k=4)
        yn = yb.rearrange("(n p k) d -> n p k d", p=P, k=4)
        def store(act, i, t):
            act.wait_ge(y_ready, TURN * i + (t + 1))
            act.dma_start(yn[TURN * i + t], y[:, t % 2]).then_inc(y_stored[t % 2], 16)

        block = ctx.enter_context(nc.Block())

        @block.sync
        def _(sp):
            with sp.Fori(0, E0 // 2) as i:
                for s in range(2):
                    e = 2 * i + s
                    for dst, src in ((w1[:, s], w["w1"][e]),
                                     (w2[:, s], w["w2"][e].rearrange("(f p) d -> p f d", p=P)),
                                     (b1[:, s], w["b1"][e]), (b2[:, s], w["b2"][e].broadcast_to([P, P]))):
                        sp.dma_start(dst, src).then_inc(wload[s], 16)
                for t in range(TURN):
                    if t >= 4:
                        sp.wait_ge(turned, TURN * i + (t - 3))
                    sp.dma_start(tok[:, t % 4], xn[TURN * i + t]).then_inc(xload[t % 4], 16)
                sp.wait_ge(y_ready, TURN * i + TURN)
                sp.sem_inc(passed, 1)

        @block.tensor
        def _(pe):
            with pe.Fori(0, E0 // 2) as i:
                def turn(t):
                    pe.wait_ge(xload[t % 4], (TURN // 4) * 16 * i + 16 * (t // 4 + 1))
                    if t >= 2:
                        pe.wait_ge(xt_ready, TURN * i + (t - 1))
                    for k in range(4):
                        mm = nc.tensor.transpose(bank[t % 2][:, k * P:(k + 1) * P], tok[:, t % 4, k], ident[:])
                    mm.then_inc(turned, 1)

                def up(t):
                    s = t // STEPS
                    if t % STEPS == 0:
                        pe.wait_ge(wload[s], 64 * i + 64)
                    pe.wait_ge(xt_ready, TURN * i + (t + 1))
                    for f in range(NF):
                        n = NF * t + f
                        if n >= 3:
                            pe.wait_ge(up_ready, NF * TURN * i + (n - 2))
                        nc.tensor.matmul(bank[2 + n % 3][:], w1[:, s, f * P:(f + 1) * P], xt[:, t % 2],
                                         start=True, stop=True).then_inc(up_psum, 1)

                def down(t):
                    s = t // STEPS
                    pe.wait_ge(up_ready, NF * TURN * i + NF * (t + 1))
                    if t >= 2:
                        pe.wait_ge(y_ready, TURN * i + (t - 1))
                    for k in range(4):
                        for f in range(NF):
                            mm = nc.tensor.matmul(bank[5 + t % 2][:, k * P:(k + 1) * P],
                                                  hid[:, t % 2, f, k * P:(k + 1) * P], w2[:, s, f],
                                                  start=(f == 0), stop=(f == NF - 1))
                    mm.then_inc(down_psum, 1)

                turn(0)
                for t in range(TURN + 1):
                    if t + 1 < TURN:
                        turn(t + 1)
                    if t < TURN:
                        up(t)
                    if t >= 1:
                        down(t - 1)
                pe.wait_ge(y_ready, TURN * i + TURN)

        @block.scalar
        def _(act):
            with act.Fori(0, E0 // 2) as i:
                for t in range(TURN):
                    for f in range(NF):
                        n = NF * t + f
                        act.wait_ge(up_psum, NF * TURN * i + (n + 1))
                        if t >= 2 and f == 0:
                            act.wait_ge(down_psum, TURN * i + (t - 1))
                        nc.scalar.activation(hid[:, t % 2, f], bank[2 + n % 3][:], ACT.Relu,
                                             bias=b1[:, t // STEPS, f:f + 1]).then_inc(up_ready, 1)
                    if t >= 1:
                        store(act, i, t - 1)
                store(act, i, TURN - 1)
                for s in range(2):
                    act.wait_ge(y_stored[s], 16 * (TURN // 2) * i + 16 * (TURN // 2))
                    act.sem_inc(passed, 1)

        @block.vector
        def _(dve):
            with dve.Fori(0, E0 // 2) as i:
                def cols(t):
                    dve.wait_ge(turned, TURN * i + (t + 1))
                    if t >= 2:
                        dve.wait_ge(up_psum, NF * TURN * i + NF * (t - 1))
                    nc.vector.tensor_copy(xt[:, t % 2], bank[t % 2][:]).then_inc(xt_ready, 1)

                cols(0)
                for t in range(TURN):
                    if t + 1 < TURN:
                        cols(t + 1)
                    if t % STEPS == 0:
                        dve.wait_ge(wload[t // STEPS], 64 * i + 64)
                    dve.wait_ge(down_psum, TURN * i + (t + 1))
                    if t >= 2:
                        dve.wait_ge(y_stored[t % 2], 16 * (TURN // 2) * i + 16 * (t // 2))
                    nc.vector.tensor_tensor(y[:, t % 2], bank[5 + t % 2][:].rearrange("p (k d) -> p k d", d=P),
                                            b2[:, t // STEPS].unsqueeze(1).broadcast_to([P, 4, P]),
                                            ALU.add).then_inc(y_ready, 1)
                for s in range(2):
                    dve.wait_ge(y_stored[s], 16 * (TURN // 2) * i + 16 * (TURN // 2))


NTL = M // P
K3 = 3
PC = W + K3 - 1
NH, NE = 4, 4
HF = NH * NE
ROW = HF + NH


def combine_and_conv(nc, passed, x1, yb, x3, hn, rows, adst, keep, edges, ln, ident, w):
    slots_all, gates_all = keep
    with ExitStack() as ctx:
        sb = lambda n, s, d=F32: ctx.enter_context(nc.sbuf_tensor(f"c_{n}", s, d))
        sem = lambda n: ctx.enter_context(nc.semaphore(f"c_{n}"))
        bank = [ctx.enter_context(nc.psum_tensor(f"c_bank{i}", [P, NT], F32)) for i in range(8)]
        xs = sb("xs", [P, HW])
        xc = sb("xc", [P, HW])
        xp = sb("xp", [P, PC, PC])
        yt = sb("yt", [P, TILES, P])
        yg = sb("yg", [P, TILES, P])
        yc = sb("yc", [P, TILES, P])
        mask = sb("mask", [P, TILES, P], I32)
        rl = sb("rl", [P, 2, NT])
        w9 = sb("w9", [P, K3 * K3, P])
        bias = sb("bias", [P, 1])
        wg = sb("wg", [P, HF + 2 * NH])
        att = sb("att", [P, 2, HF])
        prod = sb("prod", [P, 2, HF])
        zero = sb("zero", [P, 1])
        tr = sb("tr", [P, TILES, ROW])
        td = sb("td", [P, TILES, NH])
        sidx = sb("sidx", [P, TILES], I32)
        gate = sb("gate", [P, TILES])
        eps6 = sb("eps6", [P, 1])
        eps5 = sb("eps5", [P, 1])
        ln.use([bank[0][:], bank[1][:]], bank[2])
        RUN = 2 * B

        dst, counts = edges
        hist = EdgeCount(nc, sb, sem, dst[:, B * COUNT0:], counts, bank[6][:, 0:NHI], COUNT1, LT, "cntc")

        consts, setup, setup_v = sem("consts"), sem("setup"), sem("setup_v")
        loaded = sem("loaded")
        slots_copied = sem("slots_copied")
        gathered = sem("gathered")
        y_taken = sem("y_taken")
        clean = sem("clean")
        y_psum = sem("y_psum")
        x2_ready = sem("x2_ready")
        conv_psum = sem("conv_psum")
        conv_act = sem("conv_act")
        x3_ready = sem("x3_ready")
        table_psum = sem("table_psum")
        table_ready = sem("table_ready")
        stored = sem("stored")
        NSTORE = 4

        block = ctx.enter_context(nc.Block())
        hn_d = hn.rearrange("(i t) p n -> i p t n", t=LT)
        rows_d = rows.rearrange("(i t p) c -> i p t c", p=P, t=TILES)
        adst_d = adst.rearrange("(i t p) c -> i p t c", p=P, t=TILES)

        @block.sync
        def _(sp):
            for dst, src in ((w9[:], w["conv"]), (bias[:], w["conv_b"]), (wg[:, 0:HF], w["gat"]),
                             (att[:, 0], w["att_src"].broadcast_to([P, HF])),
                             (att[:, 1], w["att_dst"].broadcast_to([P, HF]))):
                sp.dma_start(dst, src).then_inc(consts, 16)
            with sp.Fori(0, B) as i:
                hist.load(sp, i)
                sp.dma_start(xs[:], x1[i]).then_inc(loaded, 16)
                sp.wait_ge(x3_ready, LT * i + LT)
                sp.dma_start(x3[i], xs[:]).then_inc(stored, 16)
                sp.wait_ge(ln.normed, LT * RUN + 2 * LT * i + 2 * LT)
                sp.dma_start(hn_d[i], xc[:].rearrange("p (t n) -> p t n", n=NT)).then_inc(stored, 16)
                sp.wait_ge(table_ready, 4 * i + 4)
                sp.dma_start(rows_d[i], tr[:]).then_inc(stored, 16)
                sp.dma_start(adst_d[i], td[:]).then_inc(stored, 16)
                sp.wait_ge(stored, 16 * NSTORE * i + 16 * NSTORE)
                sp.sem_inc(passed, 1)

        @block.gpsimd
        def _(pool):
            for k, (t, v) in enumerate(((xp, 0.0), (eps6, 1e-6), (eps5, 1e-5),
                                        (zero, 0.0))):
                nc.gpsimd.memset(t[:], v).then_inc(setup, 1)
            hist.constants(pool)

            def gather():
                for t in range(TILES):
                    nc.gpsimd.indirect_dma_start(yt[:, t], None, yb,
                                                 bass.IndirectOffsetOnAxis(ap=sidx[:, t:t + 1], axis=0)
                                                 ).then_inc(gathered, 16)

            pool.wait_ge(slots_copied, 1)
            gather()
            with pool.Fori(0, B) as i:
                pool.wait_ge(y_taken, i + 1)
                pool.wait_ge(slots_copied, i + 2)
                pool.sem_inc(passed, 1)
                gather()
            pool.wait_ge(gathered, 16 * TILES * (B + 1))

        @block.tensor
        def _(pe):
            pe.wait_ge(setup, 4)
            pe.wait_ge(consts, 80)
            pe.wait_ge(setup_v, 5)
            with pe.Fori(0, B) as i:
                pe.wait_ge(clean, 6 * i + 6)
                for t in range(LT):
                    if t >= 4:
                        pe.wait_ge(x2_ready, LT * i + (t - 3))
                    for k in range(4):
                        mm = nc.tensor.transpose(bank[t % 4][:, k * P:(k + 1) * P], yc[:, 4 * t + k], ident[:])
                    mm.then_inc(y_psum, 1)
                pe.wait_ge(x2_ready, LT * i + LT)
                ln.tensor(pe, xs, RUN + 2 * i)
                for t in range(LT):
                    pe.wait_ge(ln.normed, LT * RUN + 2 * LT * i + min(t + 2, LT))
                    if t >= 2:
                        pe.wait_ge(conv_act, LT * i + (t - 1))
                    for k in range(K3 * K3):
                        a, b = k // K3, k % K3
                        mm = nc.tensor.matmul(bank[4 + t % 2][:], w9[:, k], xp[:, 8 * t + a:8 * t + a + 8, b:b + W],
                                              start=(k == 0), stop=(k == K3 * K3 - 1))
                    mm.then_inc(conv_psum, 1)
                    hist.count(pe, i, t)
                pe.wait_ge(x3_ready, LT * i + LT)
                ln.tensor(pe, xs, RUN + 2 * i + 1)
                pe.wait_ge(ln.normed, LT * RUN + 2 * LT * i + 2 * LT)
                C = HF + 2 * NH
                for q in range(2):
                    for t in range(TILES // 2):
                        z = q * TILES // 2 + t
                        mm = nc.tensor.matmul(bank[6 + q][:, t * C:(t + 1) * C], xc[:, z * P:(z + 1) * P], wg[:],
                                              start=True, stop=True)
                    mm.then_inc(table_psum, 1)
                pe.wait_ge(table_ready, 4 * i + 4)

        @block.scalar
        def _(act):
            act.wait_ge(setup, 4)
            act.wait_ge(consts, 80)
            with act.Fori(0, B) as i:
                ln.scalar(act, xc, eps6, RUN + 2 * i)
                for t in range(LT):
                    act.wait_ge(conv_psum, LT * i + (t + 1))
                    if t >= 2:
                        act.wait_ge(x3_ready, LT * i + (t - 1))
                    nc.scalar.activation(rl[:, t % 2], bank[4 + t % 2][:], ACT.Relu,
                                         bias=bias[:]).then_inc(conv_act, 1)
                ln.scalar(act, xc, eps5, RUN + 2 * i + 1)

        @block.vector
        def _(dve):
            nc.vector.memset(slots_all[:, NTL:], 0).then_inc(setup_v, 1)
            hist.first(dve)
            dve.wait_ge(consts, 80)
            for k in range(2):
                nc.vector.tensor_tensor(prod[:, k], wg[:, 0:HF], att[:, k], ALU.mult).then_inc(setup_v, 1)
            dve.wait_ge(setup_v, 3)
            for k in range(2):
                nc.vector.tensor_reduce(wg[:, HF + NH * k:HF + NH * (k + 1)],
                                        prod[:, k].rearrange("p (h e) -> p h e", e=NE), AX.X,
                                        ALU.add).then_inc(setup_v, 1)
            nc.vector.tensor_copy(sidx[:], slots_all[:, 0:TILES]).then_inc(slots_copied, 1)
            with dve.Fori(0, B) as i:
                hist.begin(dve, i)
                dve.wait_ge(gathered, 16 * TILES * i + 16 * TILES)
                nc.vector.tensor_copy(sidx[:], slots_all[:, bass.ts(i + 1, TILES)]).then_inc(slots_copied, 1)
                nc.vector.tensor_copy(gate[:], gates_all[:, bass.ts(i, TILES)]).then_inc(clean, 1)
                dve.wait_ge(clean, 6 * i + 1)
                nc.vector.tensor_tensor(yg[:], yt[:], gate[:].unsqueeze(2).broadcast_to([P, TILES, P]),
                                        ALU.mult).then_inc(y_taken, 1)
                dve.wait_ge(y_taken, i + 1)
                nc.vector.tensor_scalar(yc[:], yg[:], 1e4, -1e4, ALU.min, ALU.max).then_inc(clean, 1)
                nc.vector.tensor_scalar(mask[:], yg[:], 0.0, 0.0, ALU.mult, ALU.is_equal).then_inc(clean, 1)
                dve.wait_ge(clean, 6 * i + 3)
                dve.sem_inc(passed, 1)
                nc.vector.copy_predicated(yc[:], mask[:], yg[:]).then_inc(clean, 1)
                dve.wait_ge(clean, 6 * i + 4)
                nc.vector.tensor_tensor(mask[:], yg[:], yg[:], ALU.not_equal).then_inc(clean, 1)
                dve.wait_ge(clean, 6 * i + 5)
                dve.sem_inc(passed, 1)
                nc.vector.copy_predicated(yc[:].rearrange("p a b -> p (a b)"), mask[:].rearrange("p a b -> p (a b)"),
                                          zero[:].broadcast_to([P, TILES * P])).then_inc(clean, 1)
                dve.wait_ge(loaded, 16 * i + 16)
                for t in range(LT):
                    dve.wait_ge(y_psum, LT * i + (t + 1))
                    c = slice(t * NT, (t + 1) * NT)
                    nc.vector.tensor_tensor(xs[:, c], xs[:, c], bank[t % 4][:], ALU.add).then_inc(x2_ready, 1)
                ln.vector(dve, xs, xc, lambda t: xp[:, 1 + 8 * t:9 + 8 * t, 1:1 + W], RUN + 2 * i)
                hist.make(dve, i, 0)
                for t in range(LT):
                    dve.wait_ge(conv_act, LT * i + (t + 1))
                    c = slice(t * NT, (t + 1) * NT)
                    nc.vector.tensor_tensor(xs[:, c], xs[:, c], rl[:, t % 2], ALU.add).then_inc(x3_ready, 1)
                    if t + 1 < LT:
                        hist.make(dve, i, t + 1)
                hist.end(dve, i)
                ln.vector(dve, xs, xc, lambda t: xc[:, t * NT:(t + 1) * NT].rearrange("p (r w) -> p r w", w=W),
                          RUN + 2 * i + 1)
                for q in range(2):
                    dve.wait_ge(table_psum, 2 * i + (q + 1))
                    src = bank[6 + q][:, 0:TILES // 2 * (HF + 2 * NH)].rearrange("p (t c) -> p t c", c=HF + 2 * NH)
                    h = slice(q * TILES // 2, (q + 1) * TILES // 2)
                    nc.vector.tensor_copy(tr[:, h], src[:, :, 0:ROW]).then_inc(table_ready, 1)
                    nc.vector.tensor_copy(td[:, h], src[:, :, ROW:]).then_inc(table_ready, 1)
                dve.wait_ge(stored, 16 * NSTORE * i + 16 * NSTORE)


N = M
LF = FE.bit_length() - 1
RES = HF + 2 * NH
BIG = 1e30


def sort_edges(nc, src, dst, srcs, dsts, cont, ident):
    with ExitStack() as ctx:
        sb = lambda n, s, d=F32: ctx.enter_context(nc.sbuf_tensor(f"s_{n}", s, d))
        sem = lambda n: ctx.enter_context(nc.semaphore(f"s_{n}"))
        bank = [ctx.enter_context(nc.psum_tensor(f"s_bank{i}", [P, NT], F32)) for i in range(8)]
        buf = [sb("keys0", [P, FE]), sb("keys1", [P, FE])]
        part = sb("part", [P, 1], I32)
        bit = sb("bit", [P, LP], I32)
        sign = sb("sign", [P, LP + 1])
        loaded, made, stage = sem("loaded"), sem("made"), sem("stage")
        turn_in, turn_psum, turn_act, turn_dve = sem("turn_in"), sem("turn_psum"), sem("turn_act"), sem("turn_dve")
        done, stored = sem("done"), sem("stored")

        steps = []
        for k in range(1, LF + LP + 1):
            if k >= LF:
                steps.append(("sign", k, 0))
            if k > LF:
                steps.append(("turn", 0, 0))
                steps += [("rows", k, j - LF) for j in range(k - 1, LF - 1, -1)]
                steps.append(("turn", 1, 0))
            steps += [("both" if k < LF else "rows", k, j) for j in range(min(k, LF) - 1, -1, -1)]
        NTURN = 8
        turns, at = [], 0
        for kind, back, _ in steps:
            if kind == "turn":
                turns.append((back, at))
            at ^= 1
        fin, other = buf[at], buf[1 - at]

        def bank_dst(t, q):
            back, a = turns[t]
            out = buf[1 - a][:]
            if back:
                return out.rearrange("p (q b) -> p b q", b=FE // P)[:, 4 * q:4 * q + 4]
            return out.rearrange("q (b p) -> q b p", p=P)[:, 4 * q:4 * q + 4]

        block = ctx.enter_context(nc.Block())

        @block.sync
        def _(sp):
            sp.dma_start(buf[0][:].bitcast(I32), dst).then_inc(loaded, 16)
            sp.dma_start(buf[1][:].bitcast(I32), src).then_inc(loaded, 16)
            sp.wait_ge(done, 1)
            sp.dma_start(srcs, other[:].bitcast(I32)).then_inc(stored, 16)
            sp.wait_ge(done, 2)
            sp.dma_start(dsts, fin[:].bitcast(I32)).then_inc(stored, 16)
            sp.wait_ge(done, 3)
            sp.dma_start(cont, other[:]).then_inc(stored, 16)
            sp.wait_ge(stored, 48)

        @block.gpsimd
        def _(pool):
            nc.gpsimd.iota(part[:], pattern=[[0, 1]], base=0, channel_multiplier=1).then_inc(made, 1)

        @block.tensor
        def _(pe):
            for t, (back, a) in enumerate(turns):
                pe.wait_ge(turn_in, t + 1)
                for q in range(NTURN):
                    if t:
                        pe.wait_ge((turn_act, turn_dve)[q % 2], (NTURN // 2) * (t - 1) + q // 2 + 1)
                    for z in range(4):
                        b = 4 * q + z
                        blk = (buf[a][:, b * P:(b + 1) * P] if back else
                               buf[a][:].rearrange("p (q b) -> p b q", b=FE // P)[:, b])
                        mm = nc.tensor.transpose(bank[q][:, z * P:(z + 1) * P], blk, ident[:])
                    mm.then_inc(turn_psum, 1)

        @block.scalar
        def _(act):
            for t in range(len(turns)):
                for q in range(0, NTURN, 2):
                    act.wait_ge(turn_psum, NTURN * t + q + 1)
                    nc.scalar.copy(bank_dst(t, q), bank[q][:].rearrange("p (b q) -> p b q", b=4)
                                   ).then_inc(turn_act, 1)

        @block.vector
        def _(dve):
            key = buf[0][:].bitcast(I32)
            dve.wait_ge(loaded, 32)
            nc.vector.tensor_scalar(key, key, 256.0, None, ALU.add).then_inc(stage, 1)
            dve.wait_ge(stage, 1)
            nc.vector.tensor_scalar(key, key, 15, None, ALU.logical_shift_left).then_inc(stage, 1)
            dve.wait_ge(stage, 2)
            nc.vector.tensor_tensor(key, key, buf[1][:].bitcast(I32), ALU.bitwise_or).then_inc(stage, 1)
            dve.wait_ge(made, 1)
            for c in range(LP):
                nc.vector.tensor_scalar(bit[:, c:c + 1], part[:], c, 1, ALU.logical_shift_right,
                                        ALU.bitwise_and).then_inc(stage, 1)
            dve.wait_ge(stage, 3 + LP)
            nc.vector.tensor_scalar(sign[:, 0:LP], bit[:], -2.0, 1.0, ALU.mult, ALU.add)
            nc.vector.memset(sign[:, LP:LP + 1], 1.0).then_inc(stage, 1)
            n, t, a = 4 + LP, 0, 0
            dve.wait_ge(stage, n)
            for kind, k, j in steps:
                x, y = buf[a][:], buf[1 - a][:]
                d = 1 << j
                if kind == "turn":
                    dve.sem_inc(turn_in, 1)
                    for q in range(1, NTURN, 2):
                        dve.wait_ge(turn_psum, NTURN * t + q + 1)
                        nc.vector.tensor_copy(bank_dst(t, q), bank[q][:].rearrange("p (b q) -> p b q", b=4)
                                              ).then_inc(turn_dve, 1)
                    t += 1
                    dve.wait_ge(turn_act, (NTURN // 2) * t)
                    dve.wait_ge(turn_dve, (NTURN // 2) * t)
                    a ^= 1
                    continue
                if kind == "sign":
                    m = k - LF
                    if m == 0:
                        ins = nc.vector.tensor_scalar(y, x, sign[:, 0:1], None, ALU.mult)
                    else:
                        ins = nc.vector.tensor_scalar(y, x, sign[:, m - 1:m], sign[:, m:m + 1], ALU.mult, ALU.mult)
                elif kind == "rows":
                    vx, vy = (v.rearrange("p (m two d) -> p m two d", two=2, d=d) for v in (x, y))
                    nc.vector.tensor_tensor(vy[:, :, 0], vx[:, :, 0], vx[:, :, 1], ALU.min)
                    ins = nc.vector.tensor_tensor(vy[:, :, 1], vx[:, :, 0], vx[:, :, 1], ALU.max)
                else:
                    vx, vy = (v.rearrange("p (n e m two d) -> p n e m two d", e=2, two=2, d=d, m=1 << (k - j - 1))
                              for v in (x, y))
                    for e in range(2):
                        nc.vector.tensor_tensor(vy[:, :, e, :, e], vx[:, :, e, :, 0], vx[:, :, e, :, 1], ALU.min)
                        ins = nc.vector.tensor_tensor(vy[:, :, e, :, 1 - e], vx[:, :, e, :, 0], vx[:, :, e, :, 1],
                                                      ALU.max)
                ins.then_inc(stage, 1)
                n += 1
                dve.wait_ge(stage, n)
                a ^= 1
            key = fin[:].bitcast(I32)
            nc.vector.tensor_scalar(other[:].bitcast(I32), key, (1 << 15) - 1, None, ALU.bitwise_and).then_inc(done, 1)
            dve.wait_ge(done, 1)
            nc.vector.tensor_scalar(key, key, 15, None, ALU.logical_shift_right).then_inc(stage, 1)
            dve.wait_ge(stage, n + 1)
            nc.vector.tensor_scalar(key, key, -256.0, None, ALU.add).then_inc(done, 1)
            dve.wait_ge(done, 2)
            dve.wait_ge(stored, 32)
            nc.vector.memset(other[:, 0:1], 0.0)
            nc.vector.tensor_tensor(other[:, 1:FE], key[:, 1:FE], key[:, 0:FE - 1], ALU.is_equal).then_inc(done, 1)


def node_ranges(nc, counts, ends, endtab, ident):
    last_i, first_i, has = ends
    with ExitStack() as ctx:
        sb = lambda n, s, d=F32: ctx.enter_context(nc.sbuf_tensor(f"h_{n}", s, d))
        sem = lambda n: ctx.enter_context(nc.semaphore(f"h_{n}"))
        ps = [ctx.enter_context(nc.psum_tensor(f"h_ps{i}", [P, NT], F32)) for i in range(2)]
        cum, tot = sb("cum", [P, NTL]), sb("tot", [P, NTL])
        endc, tmp = sb("endc", [P, NTL]), sb("tmp", [P, NTL])
        endt = sb("endt", [P, 2, P], I32)
        lower, ones = sb("lower", [P, P]), sb("ones", [P, P])
        made, chain, sums, turned, out = sem("made"), sem("chain"), sem("sums"), sem("turned"), sem("out")
        STEPS = 11
        block = ctx.enter_context(nc.Block())

        @block.sync
        def _(sp):
            sp.wait_ge(chain, STEPS + 1)
            sp.dma_start(endtab.rearrange("(q h l) c -> h q (l c)", q=2, l=P), endt[:]).then_inc(out, 16)
            sp.wait_ge(out, 16)

        @block.gpsimd
        def _(pool):
            nc.gpsimd.memset(ones[:], 1.0).then_inc(made, 1)
            nc.gpsimd.memset(lower[:], 1.0).then_inc(made, 1)
            pool.wait_ge(made, 2)
            nc.gpsimd.affine_select(out=lower[:], in_=lower[:], compare_op=ALU.is_ge, fill=0.0, base=0,
                                    pattern=[[1, P]], channel_multiplier=-1).then_inc(made, 1)

        @block.tensor
        def _(pe):
            pe.wait_ge(made, 3)
            nc.tensor.matmul(ps[0][:, 0:NTL], lower[:], counts[:], start=True, stop=True)
            nc.tensor.matmul(ps[0][:, NTL:2 * NTL], ones[:], counts[:], start=True, stop=True).then_inc(sums, 1)
            pe.wait_ge(chain, 4)
            for q in range(2):
                mm = nc.tensor.transpose(ps[1][:, q * P:(q + 1) * P], endc[:, q * P:(q + 1) * P], ident[:])
            mm.then_inc(turned, 1)

        @block.vector
        def _(dve):
            n = [0]

            def link(ins):
                n[0] += 1
                ins.then_inc(chain, 1)
                dve.wait_ge(chain, n[0])

            dve.wait_ge(sums, 1)
            link(nc.vector.tensor_copy(tot[:], ps[0][:, NTL:2 * NTL]))
            link(nc.vector.tensor_tensor_scan(cum[:], tot[:], tot[:], 0.0, ALU.add, ALU.bypass))
            link(nc.vector.tensor_tensor(cum[:], cum[:], tot[:], ALU.subtract))
            link(nc.vector.tensor_tensor(endc[:], cum[:], ps[0][:, 0:NTL], ALU.add))
            link(nc.vector.tensor_scalar(has[:], counts[:], 1.0, None, ALU.min))
            link(nc.vector.tensor_scalar(tmp[:], endc[:], -1.0, 0.0, ALU.add, ALU.max))
            link(nc.vector.tensor_copy(last_i[:], tmp[:]))
            link(nc.vector.tensor_tensor(cum[:], endc[:], counts[:], ALU.subtract))
            link(nc.vector.tensor_scalar(tmp[:], has[:], -2.0 * NEDGE, 2.0 * NEDGE, ALU.mult, ALU.add))
            link(nc.vector.tensor_tensor(cum[:], cum[:], tmp[:], ALU.add))
            link(nc.vector.tensor_copy(first_i[:], cum[:]))
            assert n[0] == STEPS
            dve.wait_ge(turned, 1)
            nc.vector.tensor_copy(endt[:], ps[1][:, 0:2 * P].rearrange("p (q l) -> p q l", q=2)
                                  ).then_inc(chain, 1)


def spread_destinations(nc, adst, dsts, first_i, v):
    with ExitStack() as ctx:
        sb = lambda n, s, d=F32: ctx.enter_context(nc.sbuf_tensor(f"v_{n}", s, d))
        sem = lambda n: ctx.enter_context(nc.semaphore(f"v_{n}"))
        zeros = sb("zeros", [P, FE])
        td = sb("td", [P, NTL, NH])
        d0 = sb("d0", [P, 1], I32)
        a0 = sb("a0", [P, NH])
        made, zeroed, loaded, spread, got, fixed = (sem(n) for n in ("made", "zeroed", "loaded", "spread", "got",
                                                                     "fixed"))
        block = ctx.enter_context(nc.Block())

        @block.vector
        def _(dve):
            nc.vector.memset(zeros[:], 0.0).then_inc(made, 1)

        @block.sync
        def _(sp):
            sp.dma_start(td[:], adst.rearrange("(t p) c -> p t c", p=P)).then_inc(loaded, 16)
            sp.dma_start(d0[:], dsts[:, 0:1], allow_slow_non_contiguous=True).then_inc(loaded, 16)
            sp.wait_ge(made, 1)
            vz = v.rearrange("(q p f) c -> q p (f c)", q=4, p=P)
            for q in range(4):
                sp.dma_start(vz[q], zeros[:]).then_inc(zeroed, 16)
            sp.wait_ge(spread, 16 * NTL)
            sp.wait_ge(got, 16)
            sp.dma_start(v.rearrange("(p f) c -> p f c", p=P)[:, 0], a0[:]).then_inc(fixed, 16)
            sp.wait_ge(fixed, 16)

        @block.gpsimd
        def _(pool):
            pool.wait_ge(loaded, 32)
            nc.gpsimd.indirect_dma_start(a0[:], None, adst, bass.IndirectOffsetOnAxis(ap=d0[:], axis=0)
                                         ).then_inc(got, 16)
            pool.wait_ge(zeroed, 64)
            for t in range(NTL):
                nc.gpsimd.indirect_dma_start(v, bass.IndirectOffsetOnAxis(ap=first_i[:, t:t + 1], axis=0),
                                             td[:, t], None, bounds_check=NEDGE - 1, oob_is_err=False
                                             ).then_inc(spread, 16)
            pool.wait_ge(spread, 16 * NTL)


COMP = HF + NH


class Chain:

    def __init__(self, eng, sem, base=0):
        self.eng, self.sem, self.base, self.n = eng, sem, base, 0

    def __call__(self, ins):
        self.n += 1
        ins.then_inc(self.sem, 1)
        self.eng.wait_ge(self.sem, self.base + self.n)


F1 = 2 * P
NF1 = F1 // P
K1 = NT // P


def edge_states(nc, passed, rows, srcs, cont, v, res, hn, ys, w):
    U = 64
    TURNS = FE // (2 * U)
    with ExitStack() as ctx:
        sb = lambda n, s, d=F32: ctx.enter_context(nc.sbuf_tensor(f"e_{n}", s, d))
        sem = lambda n: ctx.enter_context(nc.semaphore(f"e_{n}"))
        allidx = sb("allidx", [P, FE + 2 * U], I32)
        idx = sb("idx", [P, 2, U], I32)
        same = sb("same", [P, 2, U])
        vd = sb("vd", [P, 2, U, NH])
        row = sb("row", [P, 2, U, ROW])
        neg = sb("neg", [P, U])
        dst = sb("dst", [P, 1 + U, NH])
        mx = sb("mx", [P, 1 + U, NH])
        score = sb("score", [P, U, NH])
        lrel = sb("lrel", [P, U, NH])
        dx = sb("dx", [P, 2, U, NH])
        ex = sb("ex", [P, 2, U, NH])
        msg = sb("msg", [P, U, NH, NE])
        st = sb("st", [P, 2, U, RES])
        h = sb("h", [P, 2, NT])
        hid = sb("hid", [P, 2, NF1, NT])
        y = sb("y", [P, 2, K1, NE, P])
        w1 = sb("w1", [P, NE, F1])
        w2 = sb("w2", [P, NE, NF1, P])
        b1 = sb("b1", [P, NE, NF1])
        b2 = sb("b2", [P, NE, P])
        bank = [ctx.enter_context(nc.psum_tensor(f"e_bank{i}", [P, NT], F32)) for i in range(6)]
        consts = sem("consts")
        h_loaded = [sem(f"h_loaded{s}") for s in range(2)]
        up_psum, up_ready = sem("up_psum"), sem("up_ready")
        down_psum, y_ready = sem("down_psum"), sem("y_ready")
        y_stored = [sem(f"y_stored{s}") for s in range(2)]
        STEP = NE
        TURN = 2 * STEP
        init = sem("init")
        fload = [sem(f"flags_loaded{s}") for s in range(2)]
        gath = [sem(f"gathered{s}") for s in range(2)]
        idx_ready, slot_free, rows_free = sem("idx_ready"), sem("slot_free"), sem("rows_free")
        chain, dx_ready, ex_ready, st_ready = sem("chain"), sem("dx_ready"), sem("ex_ready"), sem("states_ready")
        stored = [sem(f"stored{s}") for s in range(2)]
        same_c = cont.rearrange("p (n u) -> n p u", u=U)
        v_c = v.rearrange("(p n u) c -> n p u c", p=P, u=U)
        res_c = res.rearrange("(p n u) c -> n p u c", p=P, u=U)
        block = ctx.enter_context(nc.Block())

        @block.sync
        def _(sp):
            sp.dma_start(allidx[:, 0:FE], srcs).then_inc(consts, 16)
            for dst, src in ((w1[:], w["w1"].rearrange("e d f -> d e f")),
                             (w2[:], w["w2"].rearrange("e (f p) d -> p e f d", p=P)),
                             (b1[:], w["b1"]),
                             (b2[:].rearrange("p e d -> p (e d)"), w["b2"].broadcast_to([P, NE * P]))):
                sp.dma_start(dst, src).then_inc(consts, 16)
            with sp.Fori(0, TURNS) as i:
                for s in range(2):
                    sp.dma_start(h[:, s], hn[2 * i + s]).then_inc(h_loaded[s], 16)
                for s in range(2):
                    sp.wait_ge(slot_free, 2 * i + s + 1)
                    sp.dma_start(same[:, s], same_c[2 * i + s]).then_inc(fload[s], 16)
                    sp.dma_start(vd[:, s], v_c[2 * i + s]).then_inc(fload[s], 16)
                sp.wait_ge(up_psum, NF1 * TURN * i + NF1 * TURN)
                sp.sem_inc(passed, 1)

        @block.tensor
        def _(pe):
            pe.wait_ge(consts, 80)
            with pe.Fori(0, TURNS) as i:
                def up(n):
                    s, e = divmod(n, NE)
                    if e == 0:
                        pe.wait_ge(h_loaded[s], 16 * i + 16)
                    for f in range(NF1):
                        m = NF1 * n + f
                        if m >= 3:
                            pe.wait_ge(up_ready, NF1 * TURN * i + (m - 2))
                        nc.tensor.matmul(bank[m % 3][:], w1[:, e, f * P:(f + 1) * P], h[:, s], start=True,
                                         stop=True).then_inc(up_psum, 1)

                def down(n):
                    pe.wait_ge(up_ready, NF1 * TURN * i + NF1 * (n + 1))
                    if n >= 3:
                        pe.wait_ge(y_ready, TURN * i + (n - 2))
                    for k in range(K1):
                        for f in range(NF1):
                            mm = nc.tensor.matmul(bank[3 + n % 3][:, k * P:(k + 1) * P],
                                                  hid[:, n % 2, f, k * P:(k + 1) * P], w2[:, n % NE, f],
                                                  start=(f == 0), stop=(f == NF1 - 1))
                    mm.then_inc(down_psum, 1)

                up(0)
                for n in range(TURN):
                    if n + 1 < TURN:
                        up(n + 1)
                    down(n)
                pe.wait_ge(y_ready, TURN * i + TURN)

        @block.scalar
        def _(act):
            act.wait_ge(consts, 80)
            with act.Fori(0, TURNS) as i:
                for s in range(2):
                    for n in range(s * STEP, (s + 1) * STEP):
                        if n >= 2:
                            act.wait_ge(down_psum, TURN * i + (n - 1))
                        for f in range(NF1):
                            m = NF1 * n + f
                            act.wait_ge(up_psum, NF1 * TURN * i + (m + 1))
                            nc.scalar.activation(hid[:, n % 2, f], bank[m % 3][:], ACT.Gelu,
                                                 bias=b1[:, n % NE, f:f + 1]).then_inc(up_ready, 1)
                    act.wait_ge(y_ready, TURN * i + (s + 1) * STEP)
                    act.dma_start(ys[2 * i + s], y[:, s]).then_inc(y_stored[s], 16)
                    act.wait_ge(dx_ready, 2 * i + s + 1)
                    nc.scalar.activation(ex[:], dx[:], ACT.Exp).then_inc(ex_ready, 1)
                    act.wait_ge(st_ready, 2 * i + s + 1)
                    act.dma_start(res_c[2 * i + s], st[:, s]).then_inc(stored[s], 16)
            for s in range(2):
                act.wait_ge(stored[s], 16 * TURNS)
                act.wait_ge(y_stored[s], 16 * TURNS)

        @block.gpsimd
        def _(pool):
            pool.sem_inc(rows_free, 2)
            with pool.Fori(0, TURNS) as i:
                for s in range(2):
                    pool.wait_ge(rows_free, 2 * i + s + 1)
                    pool.wait_ge(idx_ready, 2 * i + s + 1)
                    pool.sem_inc(passed, 1)
                    for u in range(U):
                        nc.gpsimd.indirect_dma_start(row[:, s, u], None, rows,
                                                     bass.IndirectOffsetOnAxis(ap=idx[:, s, u:u + 1], axis=0)
                                                     ).then_inc(gath[s], 16)
            for s in range(2):
                pool.wait_ge(gath[s], 16 * U * TURNS)

        @block.vector
        def _(dve):
            nc.vector.memset(allidx[:, FE:], 0)
            nc.vector.memset(st[:, 1], 0.0)
            nc.vector.memset(dst[:, U], 0.0)
            nc.vector.memset(mx[:, U], -BIG).then_inc(init, 1)
            dve.sem_inc(slot_free, 2)
            dve.wait_ge(consts, 80)
            for s in range(2):
                nc.vector.tensor_copy(idx[:, s], allidx[:, s * U:(s + 1) * U]).then_inc(idx_ready, 1)
            dve.wait_ge(init, 1)
            K = 13
            with dve.Fori(0, TURNS) as i:
                for s in range(2):
                    n = 2 * i + s
                    link = Chain(dve, chain, K * n)
                    link(nc.vector.tensor_copy(mx[:, 0], mx[:, U]))
                    link(nc.vector.tensor_copy(dst[:, 0], dst[:, U]))
                    dve.wait_ge(fload[s], 32 * i + 32)
                    link(nc.vector.tensor_scalar(neg[:], same[:, s], BIG, -BIG, ALU.mult, ALU.add))
                    for h in range(NH):
                        last = nc.vector.tensor_tensor_scan(dst[:, 1:, h], same[:, s], vd[:, s, :, h],
                                                            dst[:, 0, h:h + 1], ALU.mult, ALU.add)
                    link(last)
                    dve.sem_inc(slot_free, 1)
                    for e in range(NE):
                        m = s * STEP + e
                        dve.wait_ge(down_psum, TURN * i + (m + 1))
                        nc.vector.tensor_tensor(y[:, s, :, e], bank[3 + m % 3][:].rearrange("p (k d) -> p k d", d=P),
                                                b2[:, e].unsqueeze(1).broadcast_to([P, K1, P]),
                                                ALU.add).then_inc(y_ready, 1)
                    dve.wait_ge(gath[s], 16 * U * i + 16 * U)
                    nc.vector.tensor_copy(idx[:, s], allidx[:, bass.ds((2 * i + s + 2) * U, U)]
                                          ).then_inc(idx_ready, 1)
                    link(nc.vector.tensor_tensor(score[:], row[:, s, :, HF:], dst[:, 1:], ALU.add))
                    link(nc.vector.scalar_tensor_tensor(out=lrel[:], in0=score[:], scalar=0.2, in1=score[:],
                                                        op0=ALU.mult, op1=ALU.max))
                    for h in range(NH):
                        last = nc.vector.tensor_tensor_scan(mx[:, 1:, h], neg[:], lrel[:, :, h], mx[:, 0, h:h + 1],
                                                            ALU.add, ALU.max)
                    link(last)
                    link(nc.vector.tensor_tensor(dx[:, 0], mx[:, 0:U], neg[:].unsqueeze(2).broadcast_to([P, U, NH]),
                                                 ALU.add))
                    link(nc.vector.tensor_tensor(dx[:, 0], dx[:, 0], mx[:, 1:], ALU.subtract))
                    link(nc.vector.tensor_tensor(dx[:, 1], lrel[:], mx[:, 1:], ALU.subtract))
                    dve.sem_inc(dx_ready, 1)
                    link(nc.vector.tensor_copy(st[:, s, :, COMP:], mx[:, 1:]))
                    dve.wait_ge(ex_ready, n + 1)
                    link(nc.vector.tensor_tensor(msg[:], row[:, s, :, 0:HF].rearrange("p u (h e) -> p u h e", e=NE),
                                                 ex[:, 1].unsqueeze(3).broadcast_to([P, U, NH, NE]), ALU.mult))
                    dve.sem_inc(rows_free, 1)
                    for c in range(COMP):
                        h = c // NE if c < HF else c - HF
                        add = msg[:, :, c // NE, c % NE] if c < HF else ex[:, 1, :, h]
                        last = nc.vector.tensor_tensor_scan(st[:, s, :, c], ex[:, 0, :, h], add,
                                                            st[:, 1 - s, U - 1, c:c + 1], ALU.mult, ALU.add)
                    link(last)
                    dve.sem_inc(st_ready, 1)
                    assert link.n == K, link.n
                for s in range(2):
                    dve.wait_ge(stored[s], 16 * i + 16)
                    dve.wait_ge(y_stored[s], 16 * i + 16)


def join_partitions(nc, res, dsts, endtab, ident):
    with ExitStack() as ctx:
        sb = lambda n, s, d=F32: ctx.enter_context(nc.sbuf_tensor(f"j_{n}", s, d))
        sem = lambda n: ctx.enter_context(nc.semaphore(f"j_{n}"))
        ps = ctx.enter_context(nc.psum_tensor("j_ps", [P, NT], F32))
        pb = ctx.enter_context(nc.psum_tensor("j_pb", [P, NT], F32))
        ends = sb("ends", [P, RES])
        di = sb("di", [P, 3], I32)
        df = sb("df", [P, 3])
        place = sb("place", [P, 1], I32)
        pf = sb("pf", [P, 4])
        first = sb("first", [P, 1], I32)
        x3 = sb("x3", [P, 3, COMP])
        t3 = sb("t3", [COMP, 3, P])
        neg = sb("neg", [COMP, P])
        mc = sb("mc", [COMP, 1 + P])
        xc = sb("xc", [COMP, 1 + P])
        dx = sb("dx", [COMP, 2, P])
        fr = sb("fr", [P, 2, COMP])
        rr = sb("rr", [P, RES])
        gi = sb("gi", [P, 2], I32)
        d2 = sb("d2", [P, 2, COMP])
        new = sb("new", [P, RES])
        mn = sb("mn", [P, COMP])
        made, loaded, chain, asked, got = sem("made"), sem("loaded"), sem("chain"), sem("asked"), sem("got")
        turned, back, exps, exped, ready, put = (sem(n) for n in ("turned", "back", "exps", "exped", "ready", "put"))
        block = ctx.enter_context(nc.Block())

        @block.sync
        def _(sp):
            slow = dict(allow_slow_non_contiguous=True)
            sp.dma_start(ends[:], res.rearrange("(p f) c -> p f c", p=P)[:, FE - 1]).then_inc(loaded, 16)
            sp.dma_start(di[:, 0:1], dsts[:, FE - 1:FE], **slow).then_inc(loaded, 16)
            sp.dma_start(di[:, 2:3], dsts[:, 0:1], **slow).then_inc(loaded, 16)
            sp.wait_ge(made, 1)
            sp.dma_start(di[1:P, 1:2], dsts[0:P - 1, FE - 1:FE], **slow).then_inc(loaded, 16)

        @block.gpsimd
        def _(pool):
            nc.gpsimd.memset(di[:, 1:2], -1).then_inc(made, 1)
            nc.gpsimd.iota(first[:], pattern=[[0, 1]], base=0, channel_multiplier=FE).then_inc(made, 1)
            pool.wait_ge(asked, 1)
            nc.gpsimd.indirect_dma_start(place[:], None, endtab, bass.IndirectOffsetOnAxis(ap=gi[:, 0:1], axis=0)
                                         ).then_inc(got, 16)
            pool.wait_ge(asked, 2)
            nc.gpsimd.indirect_dma_start(rr[:], None, res, bass.IndirectOffsetOnAxis(ap=gi[:, 0:1], axis=0)
                                         ).then_inc(got, 16)
            pool.wait_ge(ready, 1)
            nc.gpsimd.indirect_dma_start(res, bass.IndirectOffsetOnAxis(ap=gi[:, 1:2], axis=0), new[:], None,
                                         bounds_check=NEDGE - 1, oob_is_err=False).then_inc(put, 16)
            pool.wait_ge(put, 16)

        @block.tensor
        def _(pe):
            pe.wait_ge(made, 2)
            pe.wait_ge(exps, 1)
            for k in range(3):
                mm = nc.tensor.transpose(ps[0:COMP, k * P:(k + 1) * P], x3[:, k], ident[:])
            mm.then_inc(turned, 1)
            pe.wait_ge(exps, 3)
            nc.tensor.transpose(pb[:, 0:COMP], xc[:, 0:P], ident[0:COMP, 0:COMP])
            nc.tensor.transpose(pb[:, COMP:2 * COMP], mc[:, 0:P], ident[0:COMP, 0:COMP]).then_inc(back, 1)

        @block.scalar
        def _(act):
            act.wait_ge(exps, 2)
            nc.scalar.activation(dx[:], dx[:], ACT.Exp).then_inc(exped, 1)
            act.wait_ge(exps, 4)
            nc.scalar.activation(d2[:], d2[:], ACT.Exp).then_inc(exped, 1)

        @block.vector
        def _(dve):
            link = Chain(dve, chain)
            by_head = lambda a: a.rearrange("p (h e) -> p h e", e=NE)
            dve.wait_ge(made, 2)
            dve.wait_ge(loaded, 64)
            nc.vector.tensor_copy(gi[:, 0:1], di[:, 2:3]).then_inc(asked, 1)
            link(nc.vector.tensor_copy(df[:], di[:]))
            nc.vector.tensor_copy(x3[:, 0], ends[:, 0:COMP])
            nc.vector.tensor_copy(by_head(x3[:, 1, 0:HF]), ends[:, COMP:].unsqueeze(2).broadcast_to([P, NH, NE]))
            nc.vector.tensor_copy(x3[:, 1, HF:], ends[:, COMP:])
            nc.vector.tensor_copy(x3[:, 2], df[:, 0:1].broadcast_to([P, COMP])).then_inc(exps, 1)
            dve.wait_ge(turned, 1)
            nc.vector.memset(mc[:, 0:1], -BIG)
            nc.vector.memset(xc[:, 0:1], 0.0)
            nc.vector.memset(neg[:, 0:1], 0.0)
            link(nc.vector.tensor_copy(t3[:], ps[0:COMP, 0:3 * P].rearrange("c (k p) -> c k p", k=3)))
            link(nc.vector.tensor_tensor(neg[:, 1:], t3[:, 2, 1:], t3[:, 2, 0:P - 1], ALU.is_equal))
            link(nc.vector.tensor_scalar(neg[:], neg[:], BIG, -BIG, ALU.mult, ALU.add))
            link(nc.vector.tensor_tensor_scan(mc[:, 1:], neg[:], t3[:, 1], -BIG, ALU.add, ALU.max))
            link(nc.vector.tensor_tensor(dx[:, 0], mc[:, 0:P], neg[:], ALU.add))
            link(nc.vector.tensor_tensor(dx[:, 0], dx[:, 0], mc[:, 1:], ALU.subtract))
            nc.vector.tensor_tensor(dx[:, 1], t3[:, 1], mc[:, 1:], ALU.subtract).then_inc(exps, 1)
            dve.wait_ge(exped, 1)
            link(nc.vector.tensor_tensor(dx[:, 1], dx[:, 1], t3[:, 0], ALU.mult))
            nc.vector.tensor_tensor_scan(xc[:, 1:], dx[:, 0], dx[:, 1], 0.0, ALU.mult, ALU.add).then_inc(exps, 1)
            dve.wait_ge(got, 16)
            link(nc.vector.tensor_copy(pf[:, 0:1], place[:]))
            link(nc.vector.tensor_copy(pf[:, 1:2], first[:]))
            link(nc.vector.tensor_scalar(pf[:, 0:1], pf[:, 0:1], -1.0, None, ALU.add))
            nc.vector.tensor_copy(gi[:, 0:1], pf[:, 0:1]).then_inc(asked, 1)
            link(nc.vector.tensor_tensor(pf[:, 1:2], pf[:, 0:1], pf[:, 1:2], ALU.subtract))
            link(nc.vector.tensor_scalar(pf[:, 1:2], pf[:, 1:2], float(FE), None, ALU.is_lt))
            link(nc.vector.tensor_tensor(pf[:, 2:3], df[:, 1:2], df[:, 2:3], ALU.is_equal))
            link(nc.vector.tensor_tensor(pf[:, 1:2], pf[:, 1:2], pf[:, 2:3], ALU.mult))
            link(nc.vector.tensor_scalar(pf[:, 1:2], pf[:, 1:2], -2.0 * NEDGE, 2.0 * NEDGE, ALU.mult, ALU.add))
            link(nc.vector.tensor_tensor(pf[:, 0:1], pf[:, 0:1], pf[:, 1:2], ALU.add))
            nc.vector.tensor_copy(gi[:, 1:2], pf[:, 0:1])
            dve.wait_ge(back, 1)
            link(nc.vector.tensor_copy(fr[:], pb[:, 0:2 * COMP].rearrange("p (k c) -> p k c", k=2)))
            dve.wait_ge(got, 32)
            nc.vector.tensor_copy(by_head(d2[:, 0, 0:HF]), rr[:, COMP:].unsqueeze(2).broadcast_to([P, NH, NE]))
            link(nc.vector.tensor_copy(d2[:, 0, HF:], rr[:, COMP:]))
            link(nc.vector.tensor_tensor(mn[:], d2[:, 0], fr[:, 1], ALU.max))
            link(nc.vector.tensor_tensor(d2[:, 0], d2[:, 0], mn[:], ALU.subtract))
            nc.vector.tensor_tensor(d2[:, 1], fr[:, 1], mn[:], ALU.subtract).then_inc(exps, 1)
            dve.wait_ge(exped, 2)
            link(nc.vector.tensor_tensor(new[:, 0:COMP], rr[:, 0:COMP], d2[:, 0], ALU.mult))
            link(nc.vector.tensor_tensor(d2[:, 1], d2[:, 1], fr[:, 0], ALU.mult))
            link(nc.vector.tensor_tensor(new[:, 0:COMP], new[:, 0:COMP], d2[:, 1], ALU.add))
            nc.vector.tensor_copy(new[:, COMP:], mn[:, HF:COMP]).then_inc(ready, 1)


def node_gates(nc, res, rows, adst, ends, gates, w):
    last_i, _, has = ends
    with ExitStack() as ctx:
        sb = lambda n, s, d=F32: ctx.enter_context(nc.sbuf_tensor(f"n_{n}", s, d))
        sem = lambda n: ctx.enter_context(nc.semaphore(f"n_{n}"))
        st = sb("st", [P, NTL, RES])
        tr = sb("tr", [P, NTL, ROW])
        td = sb("td", [P, NTL, NH])
        par = sb("par", [P, 3, HF])
        e4 = sb("e4", [P, NE])
        F4 = lambda n: sb(n, [P, NTL, NH])
        es, mh, mn, d0, d1, den = (F4(n) for n in ("es", "mh", "mn", "d0", "d1", "den"))
        agg = sb("agg", [P, NTL, HF])
        tmp = sb("tmp", [P, NTL, HF])
        hb = sb("hb", [P, NTL])
        mean = sb("mean", [P, NTL])
        var = sb("var", [P, NTL])
        m1, m2, i1 = (sb(n, [P, NTL]) for n in ("m1", "m2", "i1"))
        made, loaded, got, chain, asks, exped = (sem(n) for n in ("made", "loaded", "got", "chain", "asks", "exped"))
        block = ctx.enter_context(nc.Block())

        @block.sync
        def _(sp):
            sp.dma_start(tr[:], rows.rearrange("(t p) c -> p t c", p=P)).then_inc(loaded, 16)
            sp.dma_start(td[:], adst.rearrange("(t p) c -> p t c", p=P)).then_inc(loaded, 16)
            for k, n in enumerate(("b_gat", "ln_gamma", "ln_beta")):
                sp.dma_start(par[:, k], w[n].broadcast_to([P, HF])).then_inc(loaded, 16)

        @block.gpsimd
        def _(pool):
            nc.gpsimd.iota(e4[:], pattern=[[1, NE]], base=-NE, channel_multiplier=0,
                           allow_small_or_imprecise_dtypes=True).then_inc(made, 1)
            for t in range(NTL):
                nc.gpsimd.indirect_dma_start(st[:, t], None, res,
                                             bass.IndirectOffsetOnAxis(ap=last_i[:, t:t + 1], axis=0)
                                             ).then_inc(got, 16)

        @block.scalar
        def _(act):
            act.wait_ge(asks, 1)
            nc.scalar.activation(d0[:], d0[:], ACT.Exp)
            nc.scalar.activation(d1[:], d1[:], ACT.Exp).then_inc(exped, 1)
            act.wait_ge(asks, 2)
            nc.scalar.activation(var[:], var[:], ACT.Sqrt).then_inc(exped, 1)
            act.wait_ge(asks, 3)
            nc.scalar.activation(m2[:], m2[:], ACT.Exp).then_inc(exped, 1)

        @block.vector
        def _(dve):
            link = Chain(dve, chain)
            tt, ts = nc.vector.tensor_tensor, nc.vector.tensor_scalar
            A4 = [P, NTL, NH]
            A16 = [P, NTL, HF]
            per_node = lambda a, s=A4: a[:].unsqueeze(2).broadcast_to(s)
            heads = lambda a: a.rearrange("p t (h e) -> p t h e", e=NE)
            bh = lambda a: a[:].unsqueeze(3).broadcast_to([P, NTL, NH, NE])
            by_feature = lambda k: par[:, k].unsqueeze(1).broadcast_to(A16)
            dve.wait_ge(made, 1)
            dve.wait_ge(loaded, 80)
            link(tt(es[:], tr[:, :, HF:], td[:], ALU.add))
            link(nc.vector.scalar_tensor_tensor(out=es[:], in0=es[:], scalar=0.2, in1=es[:], op0=ALU.mult,
                                                op1=ALU.max))
            link(ts(hb[:], has[:], BIG, -BIG, ALU.mult, ALU.add))
            dve.wait_ge(got, 16 * NTL)
            link(tt(mh[:], st[:, :, COMP:], per_node(has), ALU.mult))
            link(tt(mh[:], mh[:], per_node(hb), ALU.add))
            link(tt(mn[:], mh[:], es[:], ALU.max))
            link(tt(d0[:], mh[:], mn[:], ALU.subtract))
            tt(d1[:], es[:], mn[:], ALU.subtract).then_inc(asks, 1)
            dve.wait_ge(exped, 1)
            link(tt(den[:], st[:, :, HF:COMP], d0[:], ALU.mult))
            link(tt(den[:], den[:], d1[:], ALU.add))
            link(ts(den[:], den[:], 1e-16, None, ALU.add))
            link(nc.vector.reciprocal(den[:], den[:]))
            link(tt(heads(agg[:]), heads(st[:, :, 0:HF]), bh(d0), ALU.mult))
            link(tt(heads(tmp[:]), heads(tr[:, :, 0:HF]), bh(d1), ALU.mult))
            link(tt(agg[:], agg[:], tmp[:], ALU.add))
            link(tt(heads(agg[:]), heads(agg[:]), bh(den), ALU.mult))
            link(tt(agg[:], agg[:], by_feature(0), ALU.add))
            link(nc.vector.tensor_reduce(mean[:], agg[:], AX.X, ALU.add))
            link(ts(mean[:], mean[:], 1.0 / HF, None, ALU.mult))
            link(tt(agg[:], agg[:], per_node(mean, A16), ALU.subtract))
            link(tt(tmp[:], agg[:], agg[:], ALU.mult))
            link(nc.vector.tensor_reduce(var[:], tmp[:], AX.X, ALU.add))
            ts(var[:], var[:], 1.0 / HF, 1e-5, ALU.mult, ALU.add).then_inc(asks, 1)
            dve.wait_ge(exped, 2)
            link(nc.vector.reciprocal(var[:], var[:]))
            link(tt(agg[:], agg[:], per_node(var, A16), ALU.mult))
            link(tt(agg[:], agg[:], by_feature(1), ALU.mult))
            link(tt(agg[:], agg[:], by_feature(2), ALU.add))
            link(nc.vector.tensor_reduce(es[:], agg[:].rearrange("p t (h e) -> p t e h", e=NE), AX.X, ALU.add))
            link(ts(es[:], es[:], 1.0 / NH, None, ALU.mult))
            be = e4[:].unsqueeze(1).broadcast_to(A4)

            def pick(scores, top, hot):
                link(nc.vector.tensor_reduce(top[:], scores[:], AX.X, ALU.max))
                link(tt(hot[:], scores[:], per_node(top), ALU.is_equal))
                link(tt(hot[:], hot[:], be, ALU.mult))
                link(nc.vector.tensor_reduce(i1[:], hot[:], AX.X, ALU.min))
                link(tt(hot[:], be, per_node(i1), ALU.is_equal))

            pick(es, m1, d0)
            link(nc.vector.scalar_tensor_tensor(out=mh[:], in0=d0[:], scalar=-BIG, in1=es[:], op0=ALU.mult,
                                                op1=ALU.add))
            pick(mh, m2, d1)
            tt(m2[:], m2[:], m1[:], ALU.subtract).then_inc(asks, 1)
            dve.wait_ge(exped, 3)
            link(ts(m1[:], m2[:], 1.0, None, ALU.add))
            link(nc.vector.reciprocal(m1[:], m1[:]))
            link(tt(m2[:], m2[:], m1[:], ALU.mult))
            link(tt(d0[:], d0[:], per_node(m1), ALU.mult))
            link(tt(d1[:], d1[:], per_node(m2), ALU.mult))
            link(tt(gates[:], d0[:], d1[:], ALU.add))


def join_experts(nc, passed, x3, ys, y, gates, ident):
    RING = 4
    with ExitStack() as ctx:
        sb = lambda n, s, d=F32: ctx.enter_context(nc.sbuf_tensor(f"f_{n}", s, d))
        sem = lambda n: ctx.enter_context(nc.semaphore(f"f_{n}"))
        bank = [ctx.enter_context(nc.psum_tensor(f"f_bank{i}", [P, NT], F32)) for i in range(2)]
        xo = sb("xo", [P, 2, HW])
        ye = sb("ye", [P, RING, K1, NE, P])
        acc = sb("acc", [P, 2, K1, P])
        g = sb("g", [P, 2, TILES, NE])
        x_loaded = [sem(f"image_loaded{s}") for s in range(2)]
        y_loaded = [sem(f"experts_loaded{s}") for s in range(RING)]
        g_ready = sem("gates_ready")
        added = sem("added")
        summed = sem("summed")
        turned = sem("turned")
        out_ready = sem("out_ready")
        stored = [sem(f"stored{s}") for s in range(2)]
        STEPS = 2 * LT
        block = ctx.enter_context(nc.Block())

        @block.sync
        def _(sp):
            with sp.Fori(0, B // 2) as i:
                for r in range(STEPS):
                    sp.wait_ge(summed, STEPS * i + (r + 1))
                    sp.dma_start(ye[:, r % RING], ys[STEPS * i + r]).then_inc(y_loaded[r % RING], 16)

        @block.tensor
        def _(pe):
            with pe.Fori(0, B // 2) as i:
                for r in range(STEPS):
                    pe.wait_ge(summed, RING + STEPS * i + (r + 1))
                    if r >= 2:
                        pe.wait_ge(out_ready, STEPS * i + (r - 1))
                    for k in range(K1):
                        mm = nc.tensor.transpose(bank[r % 2][:, k * P:(k + 1) * P], acc[:, r % 2, k], ident[:])
                    mm.then_inc(turned, 1)
                pe.wait_ge(out_ready, STEPS * i + STEPS)

        @block.scalar
        def _(act):
            with act.Fori(0, B // 2) as i:
                for s in range(2):
                    act.dma_start(xo[:, s], x3[2 * i + s]).then_inc(x_loaded[s], 16)
                for s in range(2):
                    act.wait_ge(out_ready, STEPS * i + LT * (s + 1))
                    act.dma_start(y[2 * i + s], xo[:, s]).then_inc(stored[s], 16)
                for s in range(2):
                    act.wait_ge(stored[s], 16 * i + 16)
                    act.sem_inc(passed, 1)

        @block.vector
        def _(dve):
            dve.sem_inc(summed, RING)
            with dve.Fori(0, B // 2) as i:
                def share(r, e):
                    s, t = divmod(r, LT)
                    if e == 0:
                        dve.wait_ge(y_loaded[r % RING], 16 * (STEPS // RING) * i + 16 * (r // RING + 1))
                        if r >= 2:
                            dve.wait_ge(turned, STEPS * i + (r - 1))
                    else:
                        dve.wait_ge(added, (NE - 1) * STEPS * i + ((NE - 1) * r + e))
                    for k in range(K1):
                        gate = g[:, s, K1 * t + k, e:e + 1]
                        if e == 0:
                            last = nc.vector.tensor_scalar(acc[:, r % 2, k], ye[:, r % RING, k, e], gate, None,
                                                           ALU.mult)
                        else:
                            last = nc.vector.scalar_tensor_tensor(out=acc[:, r % 2, k], in0=ye[:, r % RING, k, e],
                                                                  scalar=gate, in1=acc[:, r % 2, k],
                                                                  op0=ALU.mult, op1=ALU.add)
                    last.then_inc(added if e < NE - 1 else summed, 1)

                def out(r):
                    s, t = divmod(r, LT)
                    if t == 0:
                        dve.wait_ge(x_loaded[s], 16 * i + 16)
                    dve.wait_ge(turned, STEPS * i + (r + 1))
                    c = slice(t * NT, (t + 1) * NT)
                    nc.vector.tensor_tensor(xo[:, s, c], xo[:, s, c], bank[r % 2][:], ALU.add).then_inc(out_ready, 1)

                nc.vector.tensor_copy(g[:], gates[:, bass.ts(i, 2 * TILES)].rearrange("p (s t) e -> p s t e", s=2)
                                      ).then_inc(g_ready, 1)
                dve.wait_ge(g_ready, i + 1)
                for r in range(STEPS):
                    for e in range(NE):
                        share(r, e)
                    if r:
                        out(r - 1)
                out(STEPS - 1)


def metaformer(nc, x, y, w):
    scratch = lambda n, s, d=F32: nc.dram_tensor(n, s, d, kind="Internal").ap()
    x1, x3 = scratch("x1_dram", (B, P, HW)), scratch("x3_dram", (B, P, HW))
    hn = scratch("hn_dram", (B * LT, P, NT))
    ys = scratch("ys_dram", (B * LT, P, K1, NE, P))
    xb, yb = scratch("xb_dram", (SLOTS, P)), scratch("yb_dram", (SLOTS, P))
    rows, adst = scratch("rows_dram", (M, ROW)), scratch("adst_dram", (M, NH))
    srcs, dsts = scratch("srcs_dram", (P, FE), I32), scratch("dsts_dram", (P, FE), I32)
    cont = scratch("cont_dram", (P, FE))
    endtab = scratch("endtab_dram", (N, 1), I32)
    v = scratch("v_dram", (NEDGE, NH))
    res = scratch("res_dram", (NEDGE, RES))
    with ExitStack() as ctx:
        keep = lambda n, s, d: ctx.enter_context(nc.sbuf_tensor(f"keep_{n}", s, d))
        ln = LayerNorm(nc, keep, lambda n: ctx.enter_context(nc.semaphore(n)), "ln")
        made = ctx.enter_context(nc.semaphore("ident_made"))
        ident = keep("ident", [P, P], F32)
        with nc.Block() as block:
            @block.gpsimd
            def _(pool):
                nc.gpsimd.memset(ident[:], 0.0).then_inc(made, 1)
                pool.wait_ge(made, 1)
                nc.gpsimd.affine_select(out=ident[:], in_=ident[:], compare_op=ALU.not_equal, fill=1.0, base=0,
                                        pattern=[[-1, P]], channel_multiplier=1).then_inc(made, 1)
                pool.wait_ge(made, 2)
        slots = keep("slots", [P, NTL + TILES], I32)
        gates0 = keep("gates0", [P, NTL], F32)
        counts = keep("counts", [P, NTL], F32)
        passed = ctx.enter_context(nc.semaphore("passed"))
        sort_edges(nc, w["src"], w["dst"], srcs, dsts, cont, ident)
        involution_and_routing(nc, passed, x, x1, xb, (slots, gates0), (w["dst"], counts), ln, ident, w["involution"])
        experts(nc, passed, xb, yb, ident, w["experts"])
        combine_and_conv(nc, passed, x1, yb, x3, hn, rows, adst, (slots, gates0),
                         (w["dst"], counts), ln, ident, w["conv"])
        last_i, first_i = keep("last_i", [P, NTL], I32), keep("first_i", [P, NTL], I32)
        has = keep("has", [P, NTL], F32)
        gates1 = keep("gates1", [P, NTL, NE], F32)
        node_ranges(nc, counts, (last_i, first_i, has), endtab, ident)
        spread_destinations(nc, adst, dsts, first_i, v)
        edge_states(nc, passed, rows, srcs, cont, v, res, hn, ys, w["gelu"])
        join_partitions(nc, res, dsts, endtab, ident)
        node_gates(nc, res, rows, adst, (last_i, first_i, has), gates1, w["gates"])
        join_experts(nc, passed, x3, ys, y, gates1, ident)


def kernel(**inputs):
    import concourse.bacc as bacc
    from concourse.bass_utils import run_bass_kernel_spmd

    a = {n: np.asarray(v) for n, v in inputs.items()}
    l0, l1, f0, f1 = (lambda n, k=k: a[k + n] for k in ("L0_conv_", "L1_conv_", "L0_ffn_", "L1_ffn_"))
    row = lambda v: v.reshape(1, -1)
    weights = {
        "involution": {"w1t": l0("w1").T, "w2t": l0("w2").T, "b2": row(l0("b2")),
                       "bn": np.stack([l0(n) for n in ("b1", "bn_gamma", "bn_beta", "bn_mean", "bn_var")], axis=1),
                       "gate_w": f0("gate_w"), "gate_b": row(f0("gate_b"))},
        "experts": {"w1": f0("w1"), "w2": f0("w2"), "b1": f0("b1").reshape(E0, F0 // P, P).transpose(0, 2, 1),
                    "b2": f0("b2").reshape(E0, 1, P)},
        "conv": {"conv": l1("weight").transpose(1, 2, 3, 0).reshape(P, K3 * K3, P),
                 "conv_b": l1("bias").reshape(P, 1), "gat": f1("W_gat"),
                 "att_src": row(f1("att_src")), "att_dst": row(f1("att_dst"))},
        "gates": {n: row(f1(n)) for n in ("b_gat", "ln_gamma", "ln_beta")},
        "gelu": {"w1": f1("W1"), "w2": f1("W2"), "b1": f1("b1").reshape(NE, 2, P).transpose(2, 0, 1),
                 "b2": row(f1("b2"))},
    }
    nc = bacc.Bacc("TRN2", target_bir_lowering=False, num_devices=1)
    arrays = {}

    def put(name, v):
        arrays[name] = np.ascontiguousarray(v)
        return nc.dram_tensor(name, arrays[name].shape, mybir.dt.from_np(arrays[name].dtype),
                              kind="ExternalInput").ap()

    w = {stage: {n: put(f"in_{stage}_{n}", v) for n, v in group.items()} for stage, group in weights.items()}
    edges = f1("edge_index").astype(np.int32)
    w["src"], w["dst"] = put("in_src", edges[0].reshape(P, FE)), put("in_dst", edges[1].reshape(P, FE))
    x = put("in_x", a["x"].reshape(B, P, HW))
    y = nc.dram_tensor("out_y", (B, P, HW), F32, kind="ExternalOutput").ap()
    metaformer(nc, x, y, w)
    r = run_bass_kernel_spmd(nc, [arrays], core_ids=[0])
    return r.results[0]["out_y"].reshape(B, P, H, W)
```

```python
from contextlib import ExitStack

import numpy as np
import concourse.bass as bass
from concourse import mybir

ALU = mybir.AluOpType
ACT = mybir.ActivationFunctionType
AX = mybir.AxisListType
F32 = mybir.dt.float32
BF16 = mybir.dt.bfloat16
I32 = mybir.dt.int32

P = 128
B, H, W = 8, 64, 64
HW = H * W
M = B * HW
TILES = HW // P
NT = 512
LT = HW // NT

KS, G, CR = 7, 4, 32
TAPS = KS * KS
GC = P // G
OUT = 5
IN = OUT + KS - 1
PR = -(-H // OUT)
NP = PR * PR
PO = PR * OUT
PI = PO + KS - 1
KIN = IN * IN
NOUT = OUT * OUT
LEAD = (OUT - 1) * (IN + 1)
CAN = LEAD + KIN

NEDGE = 16 * M
FE = NEDGE // P
LP = P.bit_length() - 1
NHI = M // P
COUNT0 = 296
COUNT1 = FE - B * COUNT0

E0, F0 = 8, 512
CAP = -(-5 * M // (4 * E0))
SLOTS = E0 * CAP


class LayerNorm:

    def __init__(self, nc, sb, sem, tag):
        self.nc = nc
        self.ones = sb(f"{tag}_ones", [P, P], F32)
        self.pick = sb(f"{tag}_pick", [P, LT, LT], F32)
        self.spread = sb(f"{tag}_spread", [LT, LT, P], F32)
        self.sq = sb(f"{tag}_sq", [P, 2, NT], F32)
        self.rstd = sb(f"{tag}_rstd", [LT, NT], F32)
        self.made = sem(f"{tag}_made")
        self.mean_ready = sem(f"{tag}_mean_ready")
        self.centred = sem(f"{tag}_centred")
        self.squared = sem(f"{tag}_squared")
        self.var_ready = sem(f"{tag}_var_ready")
        self.dev_ready = sem(f"{tag}_dev_ready")
        self.rstd_ready = sem(f"{tag}_rstd_ready")
        self.factors = sem(f"{tag}_factors")
        self.normed = sem(f"{tag}_normed")

    def use(self, psum_mean, psum_var):
        self.pm, self.pv = psum_mean, psum_var

    def constants(self, pool):
        g = self.nc.gpsimd
        g.memset(self.ones[:], 1.0 / P).then_inc(self.made, 1)
        g.memset(self.pick[:], 0.0).then_inc(self.made, 1)
        g.memset(self.spread[:], 0.0).then_inc(self.made, 1)
        pool.wait_ge(self.made, 3)
        g.affine_select(out=self.pick[:], in_=self.pick[:], compare_op=ALU.not_equal, fill=1.0 / P, base=0,
                        pattern=[[1, LT], [-1, LT]], channel_multiplier=0).then_inc(self.made, 1)
        g.affine_select(out=self.spread[:], in_=self.spread[:], compare_op=ALU.not_equal, fill=1.0, base=0,
                        pattern=[[-1, LT], [0, P]], channel_multiplier=1).then_inc(self.made, 1)

    def tensor(self, pe, x, run):
        base = LT * run

        def var(t):
            pe.wait_ge(self.squared, base + (t + 1))
            self.nc.tensor.matmul(self.pv[0:LT, :], self.pick[:, t], self.sq[:, t % 2], start=(t == 0),
                                  stop=(t == LT - 1)).then_inc(self.var_ready, 1)

        for t in range(LT):
            if t >= 2:
                pe.wait_ge(self.centred, base + (t - 1))
            self.nc.tensor.matmul(self.pm[t % 2], self.ones[:], x[:, t * NT:(t + 1) * NT], start=True,
                                  stop=True).then_inc(self.mean_ready, 1)
            if t >= 1:
                var(t - 1)
        var(LT - 1)
        pe.wait_ge(self.rstd_ready, run + 1)
        for t in range(LT):
            if t >= 2:
                pe.wait_ge(self.normed, base + (t - 1))
            self.nc.tensor.matmul(self.pm[t % 2], self.spread[:, t], self.rstd[:], start=True,
                                  stop=True).then_inc(self.factors, 1)

    def scalar(self, act, xc, eps, run):
        base = LT * run
        for t in range(LT):
            act.wait_ge(self.centred, base + (t + 1))
            if t >= 2:
                act.wait_ge(self.var_ready, base + (t - 1))
            self.nc.scalar.activation(self.sq[:, t % 2], xc[:, t * NT:(t + 1) * NT],
                                      ACT.Square).then_inc(self.squared, 1)
        act.wait_ge(self.var_ready, base + LT)
        self.nc.scalar.activation(self.rstd[:], self.pv[0:LT, :], ACT.Sqrt,
                                  bias=eps[0:LT]).then_inc(self.dev_ready, 1)

    def vector(self, dve, x, xc, out, run):
        base = LT * run
        for t in range(LT):
            dve.wait_ge(self.mean_ready, base + (t + 1))
            c = slice(t * NT, (t + 1) * NT)
            self.nc.vector.tensor_tensor(xc[:, c], x[:, c], self.pm[t % 2],
                                         ALU.subtract).then_inc(self.centred, 1)
        dve.wait_ge(self.dev_ready, run + 1)
        self.nc.vector.reciprocal(self.rstd[:], self.rstd[:]).then_inc(self.rstd_ready, 1)
        for t in range(LT):
            dve.wait_ge(self.factors, base + (t + 1))
            self.nc.vector.tensor_tensor(out(t), xc[:, t * NT:(t + 1) * NT].rearrange("p (r w) -> p r w", w=W),
                                         self.pm[t % 2].rearrange("p (r w) -> p r w", w=W),
                                         ALU.mult).then_inc(self.normed, 1)


class EdgeCount:
    def __init__(self, nc, sb, sem, dst, counts, psum, columns, portions, tag,
                 ring=20):
        self.nc, self.dst, self.counts, self.psum, self.C, self.portions = nc, dst, counts, psum, columns, portions
        self.RING = ring
        self.raw = sb(f"{tag}_raw", [P, 2, columns], I32)
        self.part = sb(f"{tag}_part", [P, 2, columns], F32)
        self.iotai = sb(f"{tag}_iotai", [P, NHI], I32)
        self.iota = sb(f"{tag}_iota", [P, NHI], BF16)
        self.hot = sb(f"{tag}_hot", [P, self.RING, P + NHI], BF16)
        self.made = sem(f"{tag}_made")
        self.loaded = sem(f"{tag}_loaded")
        self.split = sem(f"{tag}_split")
        self.hot_ready = sem(f"{tag}_hot_ready")
        self.counted = sem(f"{tag}_counted")

    def cols(self, k):
        return range(self.C * k // self.portions, self.C * (k + 1) // self.portions)

    def constants(self, pool):
        self.nc.gpsimd.iota(self.iotai[:], pattern=[[1, NHI]], base=0, channel_multiplier=0).then_inc(self.made, 1)

    def first(self, dve):
        dve.wait_ge(self.made, 1)
        self.nc.vector.tensor_copy(self.iota[:], self.iotai[:]).then_inc(self.made, 1)
        dve.wait_ge(self.made, 2)

    def load(self, sp, i):
        sp.dma_start(self.raw[:, 0], self.dst[:, bass.ts(i, self.C)]).then_inc(self.loaded, 16)

    def begin(self, dve, i):
        dve.wait_ge(self.loaded, 16 * i + 16)
        v, s = self.nc.vector, self.split
        v.tensor_scalar(self.raw[:, 1], self.raw[:, 0], LP, None, ALU.logical_shift_right).then_inc(s, 1)
        dve.wait_ge(s, 3 * i + 1)
        v.tensor_scalar(self.raw[:, 0], self.raw[:, 0], P - 1, None, ALU.bitwise_and).then_inc(s, 1)
        dve.wait_ge(s, 3 * i + 2)
        v.tensor_copy(self.part[:], self.raw[:]).then_inc(s, 1)
        dve.wait_ge(s, 3 * i + 3)

    def make(self, dve, i, k):
        for c in self.cols(k):
            if c >= self.RING:
                dve.wait_ge(self.counted, self.C * i + (c - self.RING + 1))
            h = self.hot[:, c % self.RING]
            self.nc.vector.tensor_scalar(h[:, 0:P], self.iota[:, 0:P], self.part[:, 0, c:c + 1], None, ALU.is_equal)
            self.nc.vector.tensor_scalar(h[:, P:], self.iota[:], self.part[:, 1, c:c + 1], None,
                                         ALU.is_equal).then_inc(self.hot_ready, 1)

    def count(self, pe, i, k):
        for c in self.cols(k):
            pe.wait_ge(self.hot_ready, self.C * i + (c + 1))
            h = self.hot[:, c % self.RING]
            self.nc.tensor.matmul(self.psum, h[:, 0:P], h[:, P:], start=(c == 0),
                                  stop=(c == self.C - 1)).then_inc(self.counted, 1)

    def end(self, dve, i):
        dve.wait_ge(self.counted, self.C * i + self.C)
        self.nc.vector.tensor_tensor(self.counts[:], self.counts[:], self.psum, ALU.add)


def involution_and_routing(nc, passed, x, x1, xb, keep, edges, ln, ident, w):
    slots_all, gates_all = keep
    with ExitStack() as ctx:
        sb = lambda n, s, d: ctx.enter_context(nc.sbuf_tensor(f"a_{n}", s, d))
        sem = lambda n: ctx.enter_context(nc.semaphore(n))
        bank = [ctx.enter_context(nc.psum_tensor(f"a_bank{i}", [P, NT], F32)) for i in range(8)]

        xs = sb("xs", [P, HW], F32)
        xc = sb("xc", [P, HW], F32)
        xp = sb("xp", [P, PI, PI], F32)
        hid = sb("hid", [CR + 1, PO, PO], F32)
        taps = sb("taps", [P, G * NOUT, NP], F32)
        so = sb("so", [P, PO, PO], F32)
        ht = so[:].rearrange("p a b -> p (a b)")[:, 0:HW].rearrange("p (t c) -> p t c", c=P)
        xq = [xc[:, z * PR * KIN:(z + 1) * PR * KIN] for z in range(2)]
        xt = sb("xt", [P, 3, 4, P], F32)
        upper = sb("upper", [P, P], BF16)
        onesb = sb("onesb", [P, P], BF16)
        w1t = sb("w1t", [P, CR], F32)
        w2t = sb("w2t", [CR + 1, G, TAPS], F32)
        canvas = sb("canvas", [CR + 1, G, CAN], F32)
        wsum = sb("wsum", [CR + 1, G], F32)
        wsumt = sb("wsumt", [CR + 1, G, GC], F32)
        bn = sb("bn", [CR, 8], F32)
        eps6 = sb("eps6", [P, 1], F32)
        eps5 = sb("eps5", [P, 1], F32)
        gw = sb("gw", [P, E0], F32)
        gb = sb("gb", [P, E0], F32)
        em8 = sb("em8", [P, E0], F32)
        carry = sb("carry", [P, E0], F32)
        R = lambda n, d=F32: sb(n, [P, TILES, E0], d)
        lg, ex, eq, oh, cum, pos = R("lg"), R("ex"), R("eq"), R("oh"), R("cum"), R("pos")
        ohb = R("ohb", BF16)
        T1 = lambda n, d=F32: sb(n, [P, TILES], d)
        mx, se, prb, ix, pt, kept, sl, sg = [T1(n) for n in ("mx", "se", "prb", "ix", "pt", "kept", "sl", "sg")]
        sidx = T1("sidx", I32)
        sgi = T1("sgi", I32)

        ln.use([bank[0][:], bank[1][:]], bank[2])

        loaded = sem("a_loaded")
        consts = sem("a_consts")
        setup = sem("a_setup")
        setup_v = sem("a_setup_v")
        bn_chain = sem("a_bn_chain")
        zeroed = sem("a_zeroed")
        hid_psum = sem("a_hid_psum")
        hid_ready = sem("a_hid_ready")
        ws_psum = sem("a_ws_psum")
        scaled = sem("a_scaled")
        taps_psum = sem("a_taps_psum")
        taps_act = sem("a_taps_act")
        taps_dve = sem("a_taps_dve")
        patch_rows = sem("a_patch_rows")
        patch_psum = sem("a_patch_psum")
        patch_act = sem("a_patch_act")
        sum_psum = sem("a_sum_psum")
        sum_act = sem("a_sum_act")
        x1_ready = sem("a_x1_ready")
        x1_stored = sem("a_x1_stored")
        tok_psum = sem("a_tok_psum")
        tok_act = sem("a_tok_act")
        logit_psum = sem("a_logit_psum")
        shifted = sem("a_shifted")
        exps = sem("a_exps")
        chosen = sem("a_chosen")
        rank_psum = sem("a_rank_psum")
        chain = sem("a_chain")
        slots_ready = sem("a_slots_ready")
        scattered = sem("a_scattered")
        ht_free = sem("a_ht_free")

        NB3 = -(-G * NOUT // 3)
        NX4 = -(-NP // 4)
        cols = [(0, 5), (5, 10), (10, 13)]
        NS = PR * len(cols)

        dst, counts = edges

        def bank_of(z):
            return (z // PR) * 3 + (0 if z % PR < 5 else 1 if z % PR < 10 else 2)

        def group_end(u):
            return bank_of(min(4 * u + 3, NP - 1)) + 1

        order = []
        done = 0
        for u in range(NX4):
            while done < NS and u >= 3 and done < group_end(u - 3):
                order.append(("sum", done))
                done += 1
            order.append(("patch", u))
        order += [("sum", v) for v in range(done, NS)]

        hist = EdgeCount(nc, sb, sem, dst[:, 0:B * COUNT0], counts, bank[0][:, 0:NHI], COUNT0, len(order), "cnta")
        LAG = 3

        def sums(act, i, v):
            a, (b0, b1) = v // 3, cols[v % 3]
            act.wait_ge(sum_psum, NS * i + (v + 1))
            for g in range(G):
                src = bank[6 + v % 2][GC * g:GC * (g + 1), 0:(b1 - b0) * G * NOUT].rearrange(
                    "p (b g r c) -> p b g r c", g=G, r=OUT, c=OUT)[:, :, g]
                dst = so[GC * g:GC * (g + 1), OUT * a:OUT * (a + 1), OUT * b0:OUT * b1].rearrange(
                    "p r (b c) -> p b r c", c=OUT)
                last = nc.scalar.copy(dst, src)
            last.then_inc(sum_act, 1)

        block = ctx.enter_context(nc.Block())

        @block.sync
        def _(sp):
            for dst, src in ((w1t[:], w["w1t"]), (w2t[0:CR].rearrange("k g t -> k (g t)"), w["w2t"]),
                             (w2t[CR:CR + 1].rearrange("k g t -> k (g t)"), w["b2"]),
                             (bn[:, 0:5], w["bn"]), (gw[:], w["gate_w"]),
                             (gb[:], w["gate_b"].broadcast_to([P, E0]))):
                sp.dma_start(dst, src).then_inc(consts, 16)
            sp.wait_ge(setup_v, 1)
            xbz = xb.rearrange("(p r) d -> p (r d)", p=P)
            step = SLOTS // 4
            for q in range(4):
                sp.dma_start(xbz[:, q * step:(q + 1) * step],
                             taps[:].rearrange("p a b -> p (a b)")[:, 0:step]).then_inc(zeroed, 16)
            with sp.Fori(0, B) as i:
                hist.load(sp, i)
                sp.dma_start(xs[:], x[i]).then_inc(loaded, 16)
                sp.wait_ge(x1_ready, LT * i + LT)
                sp.dma_start(x1[i], xs[:]).then_inc(x1_stored, 16)
                sp.wait_ge(ln.centred, 2 * LT * i + 2 * LT)
                sp.wait_ge(x1_stored, 16 * i + 16)
                sp.sem_inc(passed, 1)
            sp.dma_start(x1[B], xs[:]).then_inc(x1_stored, 16)
            sp.wait_ge(x1_stored, 16 * (B + 1))

        @block.gpsimd
        def _(pool):
            pool.sem_inc(ht_free, 1)
            nc.gpsimd.memset(xp[:], 0.0).then_inc(setup, 1)
            ln.constants(pool)
            hist.constants(pool)
            nc.gpsimd.memset(onesb[:], 1.0).then_inc(setup, 1)
            nc.gpsimd.memset(upper[:], 1.0).then_inc(setup, 1)
            nc.gpsimd.memset(eps6[:], 1e-6).then_inc(setup, 1)
            nc.gpsimd.memset(eps5[:], 1e-5).then_inc(setup, 1)
            nc.gpsimd.iota(em8[:], pattern=[[1, E0]], base=-E0, channel_multiplier=0,
                           allow_small_or_imprecise_dtypes=True).then_inc(setup, 1)
            pool.wait_ge(setup, 6)
            nc.gpsimd.affine_select(out=upper[:], in_=upper[:], compare_op=ALU.is_gt, fill=0.0, base=0,
                                    pattern=[[1, P]], channel_multiplier=-1).then_inc(setup, 1)
            pool.wait_ge(setup, 7)
            with pool.Fori(0, B) as i:
                pool.wait_ge(ln.normed, 2 * LT * i + LT)
                for a in range(PR):
                    if a >= 2:
                        pool.wait_ge(patch_psum, NX4 * i + (PR * (a - 1) - 1) // 4 + 1)
                    pool.sem_inc(passed, 1)
                    rows = xp[:, OUT * a:OUT * a + IN]
                    nc.gpsimd.tensor_copy(
                        xq[a % 2].rearrange("p (b r c) -> p b r c", r=IN, c=IN),
                        bass.AP(tensor=rows.tensor, offset=rows.offset,
                                ap=[list(rows.ap[0]), [OUT, PR], [PI, IN], [1, IN]])).then_inc(patch_rows, 1)
                pool.wait_ge(slots_ready, i + 1)
                pool.wait_ge(tok_act, LT * i + LT)
                pool.wait_ge(zeroed, 64)
                pool.sem_inc(passed, 1)
                for t in range(TILES):
                    nc.gpsimd.indirect_dma_start(
                        xb, bass.IndirectOffsetOnAxis(ap=sidx[:, t:t + 1], axis=0), ht[:, t], None,
                        bounds_check=SLOTS - 1, oob_is_err=False).then_inc(scattered, 16)
                pool.wait_ge(scattered, 16 * TILES * i + 16 * TILES)
                pool.sem_inc(ht_free, 1)

        @block.tensor
        def _(pe):
            pe.wait_ge(setup, 7)
            pe.wait_ge(ln.made, 5)
            pe.wait_ge(setup_v, 5)
            pe.wait_ge(consts, 96)
            with pe.Fori(0, B) as i:
                pe.wait_ge(loaded, 16 * i + 16)
                ln.tensor(pe, xs, 2 * i)
                for t in range(LT):
                    pe.wait_ge(ln.normed, 2 * LT * i + (t + 1))
                    if t >= 2:
                        pe.wait_ge(hid_ready, LT * i + (t - 1))
                    nc.tensor.matmul(bank[4 + t % 2][0:CR, :], w1t[:], xp[:, 3 + 8 * t:11 + 8 * t, 3:3 + W],
                                     start=True, stop=True).then_inc(hid_psum, 1)
                pe.wait_ge(hid_ready, LT * i + LT)
                for q in range(NB3):
                    if q >= 4:
                        s, o = (taps_act, q - 4) if q % 2 == 0 else (taps_dve, q - 4)
                        pe.wait_ge(s, (NB3 // 2) * i + (o // 2 + 1))
                    for z in range(3 * q, min(3 * q + 3, G * NOUT)):
                        g, n = z // NOUT, z % NOUT
                        r, c = n // OUT, n % OUT
                        at = LEAD - (IN * r + c)
                        nc_mm = nc.tensor.matmul(
                            bank[q % 4][0:KIN, (z % 3) * NP:(z % 3 + 1) * NP], canvas[:, g, at:at + KIN],
                            hid[:, r::OUT, c::OUT], start=True, stop=True)
                    nc_mm.then_inc(taps_psum, 1)

                def transposed(u):
                    if u >= 2:
                        pe.wait_ge(patch_act, NX4 * i + (u - 1))
                    last_row = min(4 * u + 3, NP - 1) // PR
                    pe.wait_ge(patch_rows, PR * i + last_row + 1)
                    for z in range(4 * u, min(4 * u + 4, NP)):
                        a, b = z // PR, z % PR
                        mm = nc.tensor.transpose(bank[4 + u % 2][0:KIN, (z % 4) * P:(z % 4 + 1) * P],
                                                 xq[a % 2][:, b * KIN:(b + 1) * KIN], ident[:])
                    mm.then_inc(patch_psum, 1)

                events = [0]

                def event():
                    events[0] += 1
                    if events[0] > LAG:
                        hist.count(pe, i, events[0] - LAG - 1)

                transposed(0)
                transposed(1)
                u_next = 2
                events[0] = 2
                pe.wait_ge(taps_act, (NB3 // 2) * i + NB3 // 2)
                pe.wait_ge(taps_dve, (NB3 // 2) * i + NB3 // 2)
                for v in range(NS):
                    a, (b0, b1) = v // 3, cols[v % 3]
                    if v >= 2:
                        pe.wait_ge(sum_act, NS * i + (v - 1))
                    for b in range(b0, b1):
                        z = a * PR + b
                        u = z // 4
                        if z % 4 == 0:
                            pe.wait_ge(patch_act, NX4 * i + (u + 1))
                        mm = nc.tensor.matmul(bank[6 + v % 2][:, (b - b0) * G * NOUT:(b - b0 + 1) * G * NOUT],
                                              xt[0:KIN, u % 3, z % 4, :], taps[0:KIN, :, z], start=True, stop=True)
                        if z % 4 == 3 and u_next < NX4:
                            transposed(u_next)
                            u_next += 1
                            event()
                    mm.then_inc(sum_psum, 1)
                    event()
                for k in range(len(order) - LAG, len(order)):
                    hist.count(pe, i, k)
                for t in range(LT):
                    if t >= 3:
                        pe.wait_ge(scaled, LT * i + (t - 2))
                    nc.tensor.matmul(bank[1 + t % 3][:], wsumt[:].rearrange("k g c -> k (g c)"),
                                     hid[:, 8 * t:8 * t + 8, 0:W], start=True, stop=True).then_inc(ws_psum, 1)
                pe.wait_ge(x1_ready, LT * i + LT)
                ln.tensor(pe, xs, 2 * i + 1)
                pe.wait_ge(ln.normed, 2 * LT * i + 2 * LT)
                for t in range(LT):
                    if t >= 4:
                        pe.wait_ge(tok_act, LT * i + (t - 3))
                    for k in range(4):
                        mm = nc.tensor.transpose(bank[t % 4][:, k * P:(k + 1) * P],
                                                 xc[:, t * NT + k * P:t * NT + (k + 1) * P], ident[:])
                    mm.then_inc(tok_psum, 1)
                for t in range(TILES):
                    mm = nc.tensor.matmul(bank[4][:, t * E0:(t + 1) * E0], xc[:, t * P:(t + 1) * P], gw[:],
                                          start=True, stop=True)
                mm.then_inc(logit_psum, 1)
                pe.wait_ge(chosen, i + 1)
                o2 = ohb[:].rearrange("p t e -> p (t e)")
                nc.tensor.matmul(bank[5][:, 0:256], upper[:], o2, start=True, stop=True)
                nc.tensor.matmul(bank[5][:, 256:512], onesb[:], o2, start=True, stop=True).then_inc(rank_psum, 1)
                pe.wait_ge(tok_act, LT * i + LT)

        @block.scalar
        def _(act):
            act.wait_ge(setup, 7)
            act.wait_ge(setup_v, 4)
            nc.scalar.activation(bn[:, 7:8], bn[:, 7:8], ACT.Sqrt).then_inc(bn_chain, 1)
            act.wait_ge(setup_v, 5)
            with act.Fori(0, B) as i:
                act.wait_ge(loaded, 16 * i + 16)
                ln.scalar(act, xc, eps6, 2 * i)
                for t in range(LT):
                    act.wait_ge(hid_psum, LT * i + (t + 1))
                    nc.scalar.activation(hid[0:CR, 8 * t:8 * t + 8, 0:W],
                                         bank[4 + t % 2][0:CR, :].rearrange("p (r w) -> p r w", w=W), ACT.Relu,
                                         bias=bn[:, 6:7], scale=bn[:, 5:6]).then_inc(hid_ready, 1)
                for q in range(0, NB3, 2):
                    act.wait_ge(taps_psum, NB3 * i + (q + 1))
                    n = min(3, G * NOUT - 3 * q)
                    nc.scalar.activation(taps[0:KIN, 3 * q:3 * q + n].rearrange("p a b -> p (a b)"),
                                         bank[q % 4][0:KIN, 0:n * NP], ACT.Copy).then_inc(taps_act, 1)

                def patches(u):
                    act.wait_ge(patch_psum, NX4 * i + (u + 1))
                    if u >= 3:
                        act.wait_ge(sum_psum, NS * i + group_end(u - 3))
                    n = min(4, NP - 4 * u)
                    nc.scalar.activation(xt[0:KIN, u % 3, 0:n].rearrange("p a b -> p (a b)"),
                                         bank[4 + u % 2][0:KIN, 0:n * P], ACT.Copy).then_inc(patch_act, 1)

                act.wait_ge(ht_free, i + 1)
                for kind, n in order:
                    if kind == "patch":
                        patches(n)
                    else:
                        sums(act, i, n)
                ln.scalar(act, xc, eps5, 2 * i + 1)
                for t in range(LT):
                    act.wait_ge(tok_psum, LT * i + (t + 1))
                    nc.scalar.activation(ht[:, 4 * t:4 * t + 4].rearrange("p a b -> p (a b)"), bank[t % 4][:],
                                         ACT.Copy).then_inc(tok_act, 1)
                act.wait_ge(shifted, i + 1)
                nc.scalar.activation(ex[:], lg[:], ACT.Exp).then_inc(exps, 1)

        @block.vector
        def _(dve):
            nc.vector.memset(taps[:].rearrange("p a b -> p (a b)"), 0.0).then_inc(setup_v, 1)
            nc.vector.memset(hid[:], 0.0)
            nc.vector.memset(canvas[:], 0.0)
            nc.vector.memset(carry[:], 0.0).then_inc(setup_v, 1)
            nc.vector.memset(counts[:], 0.0)
            hist.first(dve)
            dve.wait_ge(setup_v, 2)
            nc.vector.memset(hid[CR:CR + 1], 1.0)
            dve.wait_ge(consts, 96)
            for g in range(G):
                nc.vector.tensor_copy(canvas[:, g, LEAD:LEAD + KS * IN].rearrange("k (a b) -> k a b", b=IN)[:, :, 0:KS],
                                      w2t[:, g].rearrange("k (a b) -> k a b", b=KS))
            nc.vector.tensor_reduce(wsum[:], w2t[:], AX.X, ALU.add).then_inc(setup_v, 1)
            dve.wait_ge(setup_v, 3)
            nc.vector.tensor_copy(wsumt[:], wsum[:].unsqueeze(2).broadcast_to([CR + 1, G, GC]))
            nc.vector.tensor_scalar(bn[:, 7:8], bn[:, 4:5], 1e-5, None, ALU.add).then_inc(setup_v, 1)
            dve.wait_ge(bn_chain, 1)
            nc.vector.reciprocal(bn[:, 5:6], bn[:, 7:8]).then_inc(bn_chain, 1)
            dve.wait_ge(bn_chain, 2)
            nc.vector.tensor_tensor(bn[:, 5:6], bn[:, 5:6], bn[:, 1:2], ALU.mult).then_inc(bn_chain, 1)
            nc.vector.tensor_tensor(bn[:, 6:7], bn[:, 0:1], bn[:, 3:4], ALU.subtract).then_inc(bn_chain, 1)
            dve.wait_ge(bn_chain, 4)
            nc.vector.scalar_tensor_tensor(out=bn[:, 6:7], in0=bn[:, 6:7], scalar=bn[:, 5:6], in1=bn[:, 2:3],
                                           op0=ALU.mult, op1=ALU.add).then_inc(setup_v, 1)
            with dve.Fori(0, B) as i:
                hist.begin(dve, i)
                dve.wait_ge(loaded, 16 * i + 16)
                ln.vector(dve, xs, xc, lambda t: xp[:, 3 + 8 * t:11 + 8 * t, 3:3 + W], 2 * i)
                for q in range(1, NB3, 2):
                    dve.wait_ge(taps_psum, NB3 * i + (q + 1))
                    n = min(3, G * NOUT - 3 * q)
                    nc.vector.tensor_copy(taps[0:KIN, 3 * q:3 * q + n].rearrange("p a b -> p (a b)"),
                                          bank[q % 4][0:KIN, 0:n * NP]).then_inc(taps_dve, 1)
                for k in range(len(order)):
                    hist.make(dve, i, k)
                hist.end(dve, i)
                K = 21
                n = [0]

                def link(ins):
                    n[0] += 1
                    ins.then_inc(chain, 1)
                    dve.wait_ge(chain, K * i + n[0])

                dve.wait_ge(sum_act, NS * i + NS)
                xv = xs[:].rearrange("p (r w) -> p r w", w=W)

                def add(t):
                    dve.wait_ge(scaled, LT * i + (t + 1))
                    c = slice(8 * t, 8 * t + 8)
                    nc.vector.tensor_tensor(xv[:, c], xv[:, c], so[:, c, 0:W], ALU.add).then_inc(x1_ready, 1)

                for t in range(LT):
                    dve.wait_ge(ws_psum, LT * i + (t + 1))
                    c = slice(8 * t, 8 * t + 8)
                    nc.vector.tensor_tensor(so[:, c, 0:W], so[:, c, 0:W],
                                            bank[1 + t % 3][:].rearrange("p (r w) -> p r w", w=W),
                                            ALU.mult).then_inc(scaled, 1)
                    if t:
                        add(t - 1)
                add(LT - 1)
                dve.wait_ge(x1_ready, LT * i + LT)
                ln.vector(dve, xs, xc, lambda t: xc[:, t * NT:(t + 1) * NT].rearrange("p (r w) -> p r w", w=W),
                          2 * i + 1)
                dve.wait_ge(logit_psum, i + 1)
                full = [P, TILES, E0]
                link(nc.vector.tensor_tensor(lg[:], bank[4][:, 0:256].rearrange("p (t e) -> p t e", e=E0),
                                             gb[:].unsqueeze(1).broadcast_to(full), ALU.add))
                link(nc.vector.tensor_reduce(mx[:], lg[:], AX.X, ALU.max))
                nc.vector.tensor_tensor(lg[:], lg[:], mx[:].unsqueeze(2).broadcast_to(full),
                                        ALU.subtract).then_inc(shifted, 1)
                dve.wait_ge(shifted, i + 1)
                link(nc.vector.tensor_scalar(eq[:], lg[:], 0.0, None, ALU.is_equal))
                link(nc.vector.tensor_tensor(eq[:], eq[:], em8[:].unsqueeze(1).broadcast_to(full), ALU.mult))
                link(nc.vector.tensor_reduce(ix[:], eq[:], AX.X, ALU.min))
                link(nc.vector.tensor_tensor(oh[:], em8[:].unsqueeze(1).broadcast_to(full),
                                             ix[:].unsqueeze(2).broadcast_to(full), ALU.is_equal))
                nc.vector.tensor_copy(ohb[:], oh[:]).then_inc(chosen, 1)
                dve.wait_ge(exps, i + 1)
                link(nc.vector.tensor_reduce(se[:], ex[:], AX.X, ALU.add))
                link(nc.vector.reciprocal(prb[:], se[:]))
                dve.wait_ge(rank_psum, i + 1)
                rank = bank[5][:, 0:256].rearrange("p (t e) -> p t e", e=E0)
                link(nc.vector.tensor_copy(ex[:], bank[5][:, 256:512].rearrange("p (t e) -> p t e", e=E0)))
                for e in range(E0):
                    last = nc.vector.tensor_tensor_scan(cum[:, :, e], ex[:, :, e], ex[:, :, e],
                                                        carry[:, e:e + 1], ALU.add, ALU.bypass)
                link(last)
                link(nc.vector.tensor_copy(carry[:], cum[:, TILES - 1]))
                link(nc.vector.tensor_tensor(cum[:], cum[:], ex[:], ALU.subtract))
                link(nc.vector.tensor_tensor(cum[:], cum[:], rank, ALU.add))
                link(nc.vector.tensor_tensor(pos[:], cum[:], oh[:], ALU.mult))
                link(nc.vector.tensor_reduce(pt[:], pos[:], AX.X, ALU.add))
                link(nc.vector.tensor_scalar(kept[:], pt[:], float(CAP), None, ALU.is_lt))
                link(nc.vector.tensor_scalar(sl[:], ix[:], float(E0), float(CAP), ALU.add, ALU.mult))
                link(nc.vector.tensor_tensor(sl[:], sl[:], pt[:], ALU.add))
                link(nc.vector.tensor_tensor(sg[:], sl[:], kept[:], ALU.mult))
                nc.vector.tensor_copy(slots_all[:, bass.ts(i, TILES)], sg[:])
                nc.vector.tensor_tensor(gates_all[:, bass.ts(i, TILES)], prb[:], kept[:], ALU.mult)
                link(nc.vector.tensor_scalar(pt[:], kept[:], -float(2 * SLOTS), float(2 * SLOTS), ALU.mult,
                                             ALU.add))
                link(nc.vector.tensor_tensor(sl[:], sl[:], pt[:], ALU.add))
                dve.wait_ge(ht_free, i + 1)
                nc.vector.tensor_copy(sidx[:], sl[:]).then_inc(slots_ready, 1)
                assert n[0] == K, n[0]


def experts(nc, passed, xb, yb, v, edges, ident, w):
    NF = F0 // P
    STEPS = CAP // NT
    TURN = 2 * STEPS
    with ExitStack() as ctx:
        sb = lambda n, s, d=F32: ctx.enter_context(nc.sbuf_tensor(f"b_{n}", s, d))
        sem = lambda n: ctx.enter_context(nc.semaphore(f"b_{n}"))
        bank = [ctx.enter_context(nc.psum_tensor(f"b_bank{i}", [P, NT], F32)) for i in range(8)]
        tok = sb("tok", [P, 4, 4, P])
        xt = sb("xt", [P, 2, NT])
        hid = sb("hid", [P, 2, NF, NT])
        y = sb("y", [P, 2, 4, P])
        w1 = sb("w1", [P, 2, F0])
        w2 = sb("w2", [P, 2, NF, P])
        b1 = sb("b1", [P, 2, NF])
        b2 = sb("b2", [P, 2, P])

        zeros = sb("zeros", [P, FE])
        dst, counts = edges
        turns = E0 // 2
        hist = EdgeCount(nc, sb, sem, dst[:, B * COUNT0:], counts, bank[7][:, 0:NHI], COUNT1 // turns, TURN, "cntb",
                         ring=40)

        zeroed = sem("v_zeroed")
        cleared = sem("v_cleared")
        wload = [sem(f"weights_loaded_{s}") for s in range(2)]
        xload = [sem(f"slots_loaded_{s}") for s in range(4)]
        turned = sem("turned")
        xt_ready = sem("xt_ready")
        up_psum = sem("up_psum")
        up_ready = sem("up_ready")
        down_psum = sem("down_psum")
        y_ready = sem("y_ready")
        y_stored = [sem(f"y_stored_{s}") for s in range(2)]

        xn = xb.rearrange("(n p k) d -> n p k d", p=P, k=4)
        yn = yb.rearrange("(n p k) d -> n p k d", p=P, k=4)
        def store(act, i, t):
            act.wait_ge(y_ready, TURN * i + (t + 1))
            act.dma_start(yn[TURN * i + t], y[:, t % 2]).then_inc(y_stored[t % 2], 16)

        block = ctx.enter_context(nc.Block())

        @block.sync
        def _(sp):
            sp.wait_ge(zeroed, 1)
            vz = v.rearrange("(q p f) c -> q p (f c)", q=4, p=P)
            for q in range(4):
                sp.dma_start(vz[q], zeros[:]).then_inc(cleared, 16)
            with sp.Fori(0, E0 // 2) as i:
                hist.load(sp, i)
                for s in range(2):
                    e = 2 * i + s
                    for dst, src in ((w1[:, s], w["w1"][e]),
                                     (w2[:, s], w["w2"][e].rearrange("(f p) d -> p f d", p=P)),
                                     (b1[:, s], w["b1"][e]), (b2[:, s], w["b2"][e].broadcast_to([P, P]))):
                        sp.dma_start(dst, src).then_inc(wload[s], 16)
                for t in range(TURN):
                    if t >= 4:
                        sp.wait_ge(turned, TURN * i + (t - 3))
                    sp.dma_start(tok[:, t % 4], xn[TURN * i + t]).then_inc(xload[t % 4], 16)
                sp.wait_ge(y_ready, TURN * i + TURN)
                sp.sem_inc(passed, 1)
            sp.wait_ge(cleared, 64)

        @block.gpsimd
        def _(pool):
            hist.constants(pool)
            nc.gpsimd.memset(zeros[:], 0.0).then_inc(zeroed, 1)

        @block.tensor
        def _(pe):
            with pe.Fori(0, E0 // 2) as i:
                def turn(t):
                    pe.wait_ge(xload[t % 4], (TURN // 4) * 16 * i + 16 * (t // 4 + 1))
                    if t >= 2:
                        pe.wait_ge(xt_ready, TURN * i + (t - 1))
                    for k in range(4):
                        mm = nc.tensor.transpose(bank[t % 2][:, k * P:(k + 1) * P], tok[:, t % 4, k], ident[:])
                    mm.then_inc(turned, 1)

                def up(t):
                    s = t // STEPS
                    if t % STEPS == 0:
                        pe.wait_ge(wload[s], 64 * i + 64)
                    pe.wait_ge(xt_ready, TURN * i + (t + 1))
                    for f in range(NF):
                        n = NF * t + f
                        if n >= 3:
                            pe.wait_ge(up_ready, NF * TURN * i + (n - 2))
                        nc.tensor.matmul(bank[2 + n % 3][:], w1[:, s, f * P:(f + 1) * P], xt[:, t % 2],
                                         start=True, stop=True).then_inc(up_psum, 1)

                def down(t):
                    s = t // STEPS
                    pe.wait_ge(up_ready, NF * TURN * i + NF * (t + 1))
                    if t >= 2:
                        pe.wait_ge(y_ready, TURN * i + (t - 1))
                    for k in range(4):
                        for f in range(NF):
                            mm = nc.tensor.matmul(bank[5 + t % 2][:, k * P:(k + 1) * P],
                                                  hid[:, t % 2, f, k * P:(k + 1) * P], w2[:, s, f],
                                                  start=(f == 0), stop=(f == NF - 1))
                    mm.then_inc(down_psum, 1)

                turn(0)
                for t in range(TURN + 1):
                    if t + 1 < TURN:
                        turn(t + 1)
                    if t < TURN:
                        up(t)
                    if t >= 1:
                        down(t - 1)
                        hist.count(pe, i, t - 1)
                pe.wait_ge(y_ready, TURN * i + TURN)

        @block.scalar
        def _(act):
            with act.Fori(0, E0 // 2) as i:
                def cols(t):
                    act.wait_ge(turned, TURN * i + (t + 1))
                    if t >= 2:
                        act.wait_ge(up_psum, NF * TURN * i + NF * (t - 1))
                    nc.scalar.activation(xt[:, t % 2], bank[t % 2][:], ACT.Copy).then_inc(xt_ready, 1)

                cols(0)
                for t in range(TURN):
                    if t + 1 < TURN:
                        cols(t + 1)
                    for f in range(NF):
                        n = NF * t + f
                        act.wait_ge(up_psum, NF * TURN * i + (n + 1))
                        if t >= 2 and f == 0:
                            act.wait_ge(down_psum, TURN * i + (t - 1))
                        nc.scalar.activation(hid[:, t % 2, f], bank[2 + n % 3][:], ACT.Relu,
                                             bias=b1[:, t // STEPS, f:f + 1]).then_inc(up_ready, 1)
                    if t >= 1:
                        store(act, i, t - 1)
                store(act, i, TURN - 1)
                for s in range(2):
                    act.wait_ge(y_stored[s], 16 * (TURN // 2) * i + 16 * (TURN // 2))
                    act.sem_inc(passed, 1)

        @block.vector
        def _(dve):
            hist.first(dve)
            with dve.Fori(0, E0 // 2) as i:
                hist.begin(dve, i)
                for t in range(TURN):
                    hist.make(dve, i, t)
                    if t % STEPS == 0:
                        dve.wait_ge(wload[t // STEPS], 64 * i + 64)
                    dve.wait_ge(down_psum, TURN * i + (t + 1))
                    if t >= 2:
                        dve.wait_ge(y_stored[t % 2], 16 * (TURN // 2) * i + 16 * (t // 2))
                    nc.vector.tensor_tensor(y[:, t % 2], bank[5 + t % 2][:].rearrange("p (k d) -> p k d", d=P),
                                            b2[:, t // STEPS].unsqueeze(1).broadcast_to([P, 4, P]),
                                            ALU.add).then_inc(y_ready, 1)
                hist.end(dve, i)
                for s in range(2):
                    dve.wait_ge(y_stored[s], 16 * (TURN // 2) * i + 16 * (TURN // 2))


NTL = M // P
K3 = 3
PC = W + K3 - 1
NH, NE = 4, 4
HF = NH * NE
ROW = HF + NH


def combine_and_conv(nc, passed, x1, yb, x3, hn, rows, adst, v, first_i, keep, ln, ident, w):
    slots_all, gates_all = keep
    with ExitStack() as ctx:
        sb = lambda n, s, d=F32: ctx.enter_context(nc.sbuf_tensor(f"c_{n}", s, d))
        sem = lambda n: ctx.enter_context(nc.semaphore(f"c_{n}"))
        bank = [ctx.enter_context(nc.psum_tensor(f"c_bank{i}", [P, NT], F32)) for i in range(8)]
        xs = sb("xs", [P, HW])
        xc = sb("xc", [P, HW])
        xp = sb("xp", [P, PC, PC])
        yt = sb("yt", [P, TILES, P])
        yg = sb("yg", [P, TILES, P])
        yc = sb("yc", [P, TILES, P])
        mask = sb("mask", [P, TILES, P], I32)
        rl = sb("rl", [P, 2, NT])
        w9 = sb("w9", [P, K3 * K3, P])
        bias = sb("bias", [P, 1])
        wg = sb("wg", [P, HF + 2 * NH])
        att = sb("att", [P, 2, HF])
        prod = sb("prod", [P, 2, HF])
        zero = sb("zero", [P, 1])
        tr = sb("tr", [P, TILES, ROW])
        td = sb("td", [P, TILES, NH])
        sidx = sb("sidx", [P, TILES], I32)
        gate = sb("gate", [P, TILES])
        eps6 = sb("eps6", [P, 1])
        eps5 = sb("eps5", [P, 1])
        ln.use([bank[0][:], bank[1][:]], bank[2])
        RUN = 2 * B
        fidx = sb("fidx", [P, TILES], I32)

        spread = sem("spread")
        td_free = sem("td_free")

        consts, setup, setup_v = sem("consts"), sem("setup"), sem("setup_v")
        loaded = sem("loaded")
        slots_copied = sem("slots_copied")
        gathered = sem("gathered")
        clean = sem("clean")
        y_psum = sem("y_psum")
        x2_ready = sem("x2_ready")
        conv_psum = sem("conv_psum")
        conv_act = sem("conv_act")
        x3_ready = sem("x3_ready")
        table_psum = sem("table_psum")
        table_ready = sem("table_ready")
        x3_stored = sem("x3_stored")
        stored = sem("stored")
        buffers_free = sem("buffers_free")
        NSTORE = 3

        block = ctx.enter_context(nc.Block())
        hn_d = hn.rearrange("(i t) p n -> i p t n", t=LT)
        rows_d = rows.rearrange("(i t p) c -> i p t c", p=P, t=TILES)
        adst_d = adst.rearrange("(i t p) c -> i p t c", p=P, t=TILES)

        @block.sync
        def _(sp):
            for dst, src in ((w9[:], w["conv"]), (bias[:], w["conv_b"]), (wg[:, 0:HF], w["gat"]),
                             (att[:, 0], w["att_src"].broadcast_to([P, HF])),
                             (att[:, 1], w["att_dst"].broadcast_to([P, HF]))):
                sp.dma_start(dst, src).then_inc(consts, 16)
            sp.dma_start(xs[:], x1[0]).then_inc(loaded, 16)
            with sp.Fori(0, B) as i:
                sp.wait_ge(x3_ready, LT * i + LT)
                sp.sem_inc(passed, 1)
                sp.dma_start(x3[i], xs[:]).then_inc(x3_stored, 16)
                sp.wait_ge(ln.centred, LT * RUN + 2 * LT * i + 2 * LT)
                sp.sem_inc(passed, 1)
                sp.wait_ge(x3_stored, 16 * i + 16)
                sp.sem_inc(passed, 1)
                sp.dma_start(xs[:], x1[i + 1]).then_inc(loaded, 16)
                sp.wait_ge(ln.normed, LT * RUN + 2 * LT * i + 2 * LT)
                sp.sem_inc(passed, 1)
                sp.dma_start(hn_d[i], xc[:].rearrange("p (t n) -> p t n", n=NT)).then_inc(stored, 16)
                sp.wait_ge(table_ready, 5 * i + 5)
                sp.sem_inc(passed, 1)
                sp.dma_start(rows_d[i], tr[:]).then_inc(stored, 16)
                sp.dma_start(adst_d[i], td[:]).then_inc(stored, 16)
                sp.wait_ge(stored, 16 * NSTORE * i + 16 * NSTORE)
                sp.sem_inc(buffers_free, 1)
            sp.wait_ge(loaded, 16 * (B + 1))

        @block.gpsimd
        def _(pool):
            for t, value in ((xp, 0.0), (eps6, 1e-6), (eps5, 1e-5), (zero, 0.0)):
                nc.gpsimd.memset(t[:], value).then_inc(setup, 1)

            def gather():
                for t in range(TILES):
                    nc.gpsimd.indirect_dma_start(yt[:, t], None, yb,
                                                 bass.IndirectOffsetOnAxis(ap=sidx[:, t:t + 1], axis=0)
                                                 ).then_inc(gathered, 16)

            pool.sem_inc(td_free, 1)
            pool.sem_inc(buffers_free, 1)
            pool.wait_ge(slots_copied, 1)
            gather()
            with pool.Fori(0, B) as i:
                pool.wait_ge(clean, 7 * i + 2)
                pool.wait_ge(slots_copied, i + 2)
                pool.sem_inc(passed, 1)
                gather()
                pool.wait_ge(table_ready, 5 * i + 5)
                pool.sem_inc(passed, 1)
                for t in range(TILES):
                    nc.gpsimd.indirect_dma_start(v, bass.IndirectOffsetOnAxis(ap=fidx[:, t:t + 1], axis=0),
                                                 td[:, t], None, bounds_check=NEDGE - 1, oob_is_err=False
                                                 ).then_inc(spread, 16)
                pool.wait_ge(spread, 16 * TILES * i + 16 * TILES)
                pool.sem_inc(td_free, 1)
            pool.wait_ge(gathered, 16 * TILES * (B + 1))

        @block.tensor
        def _(pe):
            pe.wait_ge(setup, 4)
            pe.wait_ge(consts, 80)
            pe.wait_ge(setup_v, 5)
            with pe.Fori(0, B) as i:
                pe.wait_ge(clean, 7 * i + 7)
                for t in range(LT):
                    if t >= 4:
                        pe.wait_ge(x2_ready, LT * i + (t - 3))
                    for k in range(4):
                        mm = nc.tensor.transpose(bank[t % 4][:, k * P:(k + 1) * P], yc[:, 4 * t + k], ident[:])
                    mm.then_inc(y_psum, 1)
                pe.wait_ge(x2_ready, LT * i + LT)
                ln.tensor(pe, xs, RUN + 2 * i)
                for t in range(LT):
                    pe.wait_ge(ln.normed, LT * RUN + 2 * LT * i + min(t + 2, LT))
                    if t >= 2:
                        pe.wait_ge(conv_act, LT * i + (t - 1))
                    for k in range(K3 * K3):
                        a, b = k // K3, k % K3
                        mm = nc.tensor.matmul(bank[4 + t % 2][:], w9[:, k], xp[:, 8 * t + a:8 * t + a + 8, b:b + W],
                                              start=(k == 0), stop=(k == K3 * K3 - 1))
                    mm.then_inc(conv_psum, 1)
                pe.wait_ge(x3_ready, LT * i + LT)
                ln.tensor(pe, xs, RUN + 2 * i + 1)
                pe.wait_ge(ln.normed, LT * RUN + 2 * LT * i + 2 * LT)
                C = HF + 2 * NH
                for q in range(2):
                    for t in range(TILES // 2):
                        z = q * TILES // 2 + t
                        mm = nc.tensor.matmul(bank[6 + q][:, t * C:(t + 1) * C], xc[:, z * P:(z + 1) * P], wg[:],
                                              start=True, stop=True)
                    mm.then_inc(table_psum, 1)
                pe.wait_ge(table_ready, 5 * i + 5)

        @block.scalar
        def _(act):
            act.wait_ge(setup, 4)
            act.wait_ge(consts, 80)
            with act.Fori(0, B) as i:
                ln.scalar(act, xc, eps6, RUN + 2 * i)
                for t in range(LT):
                    act.wait_ge(conv_psum, LT * i + (t + 1))
                    if t >= 2:
                        act.wait_ge(x3_ready, LT * i + (t - 1))
                    nc.scalar.activation(rl[:, t % 2], bank[4 + t % 2][:], ACT.Relu,
                                         bias=bias[:]).then_inc(conv_act, 1)
                ln.scalar(act, xc, eps5, RUN + 2 * i + 1)

        def clean_step(dve, j, k):
            if k == 0:
                dve.wait_ge(gathered, 16 * TILES * j + 16 * TILES)
                nc.vector.tensor_copy(sidx[:], slots_all[:, bass.ts(j + 1, TILES)]).then_inc(slots_copied, 1)
                nc.vector.tensor_copy(gate[:], gates_all[:, bass.ts(j, TILES)]).then_inc(clean, 1)
            elif k == 1:
                dve.wait_ge(clean, 7 * j + 1)
                nc.vector.tensor_tensor(yg[:], yt[:], gate[:].unsqueeze(2).broadcast_to([P, TILES, P]),
                                        ALU.mult).then_inc(clean, 1)
            elif k == 2:
                dve.wait_ge(clean, 7 * j + 2)
                nc.vector.tensor_scalar(yc[:], yg[:], 1e4, -1e4, ALU.min, ALU.max).then_inc(clean, 1)
                nc.vector.tensor_scalar(mask[:], yg[:], 0.0, 0.0, ALU.mult, ALU.is_equal).then_inc(clean, 1)
            elif k == 3:
                dve.wait_ge(clean, 7 * j + 4)
                dve.sem_inc(passed, 1)
                nc.vector.copy_predicated(yc[:], mask[:], yg[:]).then_inc(clean, 1)
            elif k == 4:
                dve.wait_ge(clean, 7 * j + 5)
                nc.vector.tensor_tensor(mask[:], yg[:], yg[:], ALU.not_equal).then_inc(clean, 1)
            elif k == 5:
                dve.wait_ge(clean, 7 * j + 6)
                dve.sem_inc(passed, 1)
                nc.vector.copy_predicated(yc[:].rearrange("p a b -> p (a b)"), mask[:].rearrange("p a b -> p (a b)"),
                                          zero[:].broadcast_to([P, TILES * P])).then_inc(clean, 1)

        @block.vector
        def _(dve):
            dve.wait_ge(setup, 4)
            nc.vector.memset(gates_all[:, NTL:], 0.0)
            nc.vector.memset(slots_all[:, NTL:], 0).then_inc(setup_v, 1)
            dve.wait_ge(consts, 80)
            for k in range(2):
                nc.vector.tensor_tensor(prod[:, k], wg[:, 0:HF], att[:, k], ALU.mult).then_inc(setup_v, 1)
            dve.wait_ge(setup_v, 3)
            for k in range(2):
                nc.vector.tensor_reduce(wg[:, HF + NH * k:HF + NH * (k + 1)],
                                        prod[:, k].rearrange("p (h e) -> p h e", e=NE), AX.X,
                                        ALU.add).then_inc(setup_v, 1)
            nc.vector.tensor_copy(sidx[:], slots_all[:, 0:TILES]).then_inc(slots_copied, 1)
            for k in range(6):
                clean_step(dve, 0, k)
            with dve.Fori(0, B) as i:
                dve.wait_ge(loaded, 16 * i + 16)
                for t in range(LT):
                    dve.wait_ge(y_psum, LT * i + (t + 1))
                    c = slice(t * NT, (t + 1) * NT)
                    nc.vector.tensor_tensor(xs[:, c], xs[:, c], bank[t % 4][:], ALU.add).then_inc(x2_ready, 1)
                dve.wait_ge(buffers_free, i + 1)
                ln.vector(dve, xs, xc, lambda t: xp[:, 1 + 8 * t:9 + 8 * t, 1:1 + W], RUN + 2 * i)
                for t in range(LT):
                    dve.wait_ge(conv_act, LT * i + (t + 1))
                    c = slice(t * NT, (t + 1) * NT)
                    nc.vector.tensor_tensor(xs[:, c], xs[:, c], rl[:, t % 2], ALU.add).then_inc(x3_ready, 1)
                    clean_step(dve, i + 1, t)
                ln.vector(dve, xs, xc, lambda t: xc[:, t * NT:(t + 1) * NT].rearrange("p (r w) -> p r w", w=W),
                          RUN + 2 * i + 1)
                dve.wait_ge(td_free, i + 1)
                nc.vector.tensor_copy(fidx[:], first_i[:, bass.ts(i, TILES)]).then_inc(table_ready, 1)
                for q in range(2):
                    dve.wait_ge(table_psum, 2 * i + (q + 1))
                    src = bank[6 + q][:, 0:TILES // 2 * (HF + 2 * NH)].rearrange("p (t c) -> p t c", c=HF + 2 * NH)
                    h = slice(q * TILES // 2, (q + 1) * TILES // 2)
                    nc.vector.tensor_copy(tr[:, h], src[:, :, 0:ROW]).then_inc(table_ready, 1)
                    nc.vector.tensor_copy(td[:, h], src[:, :, ROW:]).then_inc(table_ready, 1)


N = M
LF = FE.bit_length() - 1
RES = HF + 2 * NH
BIG = 1e30


def sort_edges(nc, src, dst, srcs, dsts, cont, ident):
    with ExitStack() as ctx:
        sb = lambda n, s, d=F32: ctx.enter_context(nc.sbuf_tensor(f"s_{n}", s, d))
        sem = lambda n: ctx.enter_context(nc.semaphore(f"s_{n}"))
        bank = [ctx.enter_context(nc.psum_tensor(f"s_bank{i}", [P, NT], F32)) for i in range(8)]
        buf = [sb("keys0", [P, FE]), sb("keys1", [P, FE])]
        part = sb("part", [P, 1], I32)
        bit = sb("bit", [P, LP], I32)
        sign = sb("sign", [P, LP + 1])
        loaded, made, stage = sem("loaded"), sem("made"), sem("stage")
        turn_in, turn_psum, turn_act, turn_dve = sem("turn_in"), sem("turn_psum"), sem("turn_act"), sem("turn_dve")
        done, stored = sem("done"), sem("stored")

        steps = []
        for k in range(1, LF + LP + 1):
            if k >= LF:
                steps.append(("sign", k, 0))
            if k > LF:
                steps.append(("turn", 0, 0))
                steps += [("rows", k, j - LF) for j in range(k - 1, LF - 1, -1)]
                steps.append(("turn", 1, 0))
            steps += [("both" if k < LF else "rows", k, j) for j in range(min(k, LF) - 1, -1, -1)]
        NTURN = 8
        turns, at = [], 0
        for kind, back, _ in steps:
            if kind == "turn":
                turns.append((back, at))
            at ^= 1
        fin, other = buf[at], buf[1 - at]

        def bank_dst(t, q):
            back, a = turns[t]
            out = buf[1 - a][:]
            if back:
                return out.rearrange("p (q b) -> p b q", b=FE // P)[:, 4 * q:4 * q + 4]
            return out.rearrange("q (b p) -> q b p", p=P)[:, 4 * q:4 * q + 4]

        block = ctx.enter_context(nc.Block())

        @block.sync
        def _(sp):
            sp.dma_start(buf[0][:].bitcast(I32), dst).then_inc(loaded, 16)
            sp.dma_start(buf[1][:].bitcast(I32), src).then_inc(loaded, 16)
            sp.wait_ge(done, 1)
            sp.dma_start(srcs, other[:].bitcast(I32)).then_inc(stored, 16)
            sp.wait_ge(done, 2)
            sp.dma_start(dsts, fin[:].bitcast(I32)).then_inc(stored, 16)
            sp.wait_ge(done, 3)
            sp.dma_start(cont, other[:]).then_inc(stored, 16)
            sp.wait_ge(stored, 48)

        @block.gpsimd
        def _(pool):
            nc.gpsimd.iota(part[:], pattern=[[0, 1]], base=0, channel_multiplier=1).then_inc(made, 1)

        @block.tensor
        def _(pe):
            for t, (back, a) in enumerate(turns):
                pe.wait_ge(turn_in, t + 1)
                for q in range(NTURN):
                    if t:
                        pe.wait_ge((turn_act, turn_dve)[q % 2], (NTURN // 2) * (t - 1) + q // 2 + 1)
                    for z in range(4):
                        b = 4 * q + z
                        blk = (buf[a][:, b * P:(b + 1) * P] if back else
                               buf[a][:].rearrange("p (q b) -> p b q", b=FE // P)[:, b])
                        mm = nc.tensor.transpose(bank[q][:, z * P:(z + 1) * P], blk, ident[:])
                    mm.then_inc(turn_psum, 1)

        @block.scalar
        def _(act):
            for t in range(len(turns)):
                for q in range(0, NTURN, 2):
                    act.wait_ge(turn_psum, NTURN * t + q + 1)
                    nc.scalar.copy(bank_dst(t, q), bank[q][:].rearrange("p (b q) -> p b q", b=4)
                                   ).then_inc(turn_act, 1)

        @block.vector
        def _(dve):
            key = buf[0][:].bitcast(I32)
            dve.wait_ge(loaded, 32)
            nc.vector.tensor_scalar(key, key, 256.0, None, ALU.add).then_inc(stage, 1)
            dve.wait_ge(stage, 1)
            nc.vector.tensor_scalar(key, key, 15, None, ALU.logical_shift_left).then_inc(stage, 1)
            dve.wait_ge(stage, 2)
            nc.vector.tensor_tensor(key, key, buf[1][:].bitcast(I32), ALU.bitwise_or).then_inc(stage, 1)
            dve.wait_ge(made, 1)
            for c in range(LP):
                nc.vector.tensor_scalar(bit[:, c:c + 1], part[:], c, 1, ALU.logical_shift_right,
                                        ALU.bitwise_and).then_inc(stage, 1)
            dve.wait_ge(stage, 3 + LP)
            nc.vector.tensor_scalar(sign[:, 0:LP], bit[:], -2.0, 1.0, ALU.mult, ALU.add)
            nc.vector.memset(sign[:, LP:LP + 1], 1.0).then_inc(stage, 1)
            n, t, a = 4 + LP, 0, 0
            dve.wait_ge(stage, n)
            for kind, k, j in steps:
                x, y = buf[a][:], buf[1 - a][:]
                d = 1 << j
                if kind == "turn":
                    dve.sem_inc(turn_in, 1)
                    for q in range(1, NTURN, 2):
                        dve.wait_ge(turn_psum, NTURN * t + q + 1)
                        nc.vector.tensor_copy(bank_dst(t, q), bank[q][:].rearrange("p (b q) -> p b q", b=4)
                                              ).then_inc(turn_dve, 1)
                    t += 1
                    dve.wait_ge(turn_act, (NTURN // 2) * t)
                    dve.wait_ge(turn_dve, (NTURN // 2) * t)
                    a ^= 1
                    continue
                if kind == "sign":
                    m = k - LF
                    if m == 0:
                        ins = nc.vector.tensor_scalar(y, x, sign[:, 0:1], None, ALU.mult)
                    else:
                        ins = nc.vector.tensor_scalar(y, x, sign[:, m - 1:m], sign[:, m:m + 1], ALU.mult, ALU.mult)
                elif kind == "rows":
                    vx, vy = (v.rearrange("p (m two d) -> p m two d", two=2, d=d) for v in (x, y))
                    nc.vector.tensor_tensor(vy[:, :, 0], vx[:, :, 0], vx[:, :, 1], ALU.min)
                    ins = nc.vector.tensor_tensor(vy[:, :, 1], vx[:, :, 0], vx[:, :, 1], ALU.max)
                else:
                    vx, vy = (v.rearrange("p (n e m two d) -> p n e m two d", e=2, two=2, d=d, m=1 << (k - j - 1))
                              for v in (x, y))
                    for e in range(2):
                        nc.vector.tensor_tensor(vy[:, :, e, :, e], vx[:, :, e, :, 0], vx[:, :, e, :, 1], ALU.min)
                        ins = nc.vector.tensor_tensor(vy[:, :, e, :, 1 - e], vx[:, :, e, :, 0], vx[:, :, e, :, 1],
                                                      ALU.max)
                ins.then_inc(stage, 1)
                n += 1
                dve.wait_ge(stage, n)
                a ^= 1
            key = fin[:].bitcast(I32)
            nc.vector.tensor_scalar(other[:].bitcast(I32), key, (1 << 15) - 1, None, ALU.bitwise_and).then_inc(done, 1)
            dve.wait_ge(done, 1)
            nc.vector.tensor_scalar(key, key, 15, None, ALU.logical_shift_right).then_inc(stage, 1)
            dve.wait_ge(stage, n + 1)
            nc.vector.tensor_scalar(key, key, -256.0, None, ALU.add).then_inc(done, 1)
            dve.wait_ge(done, 2)
            dve.wait_ge(stored, 32)
            nc.vector.memset(other[:, 0:1], 0.0)
            nc.vector.tensor_tensor(other[:, 1:FE], key[:, 1:FE], key[:, 0:FE - 1], ALU.is_equal).then_inc(done, 1)


def node_ranges(nc, counts, ends, endtab, ident):
    last_i, first_i, has = ends
    with ExitStack() as ctx:
        sb = lambda n, s, d=F32: ctx.enter_context(nc.sbuf_tensor(f"h_{n}", s, d))
        sem = lambda n: ctx.enter_context(nc.semaphore(f"h_{n}"))
        ps = [ctx.enter_context(nc.psum_tensor(f"h_ps{i}", [P, NT], F32)) for i in range(2)]
        cum, tot = sb("cum", [P, NTL]), sb("tot", [P, NTL])
        endc, tmp = sb("endc", [P, NTL]), sb("tmp", [P, NTL])
        endt = sb("endt", [P, 2, P], I32)
        lower, ones = sb("lower", [P, P]), sb("ones", [P, P])
        made, chain, out = sem("made"), sem("chain"), sem("out")
        sums = sem("sums")
        STEPS = 11
        block = ctx.enter_context(nc.Block())

        @block.sync
        def _(sp):
            sp.wait_ge(chain, STEPS + 1)
            sp.dma_start(endtab.rearrange("(q h l) c -> h q (l c)", q=2, l=P), endt[:]).then_inc(out, 16)
            sp.wait_ge(out, 16)

        @block.gpsimd
        def _(pool):
            nc.gpsimd.memset(ones[:], 1.0).then_inc(made, 1)
            nc.gpsimd.memset(lower[:], 1.0).then_inc(made, 1)
            pool.wait_ge(made, 2)
            nc.gpsimd.affine_select(out=lower[:], in_=lower[:], compare_op=ALU.is_ge, fill=0.0, base=0,
                                    pattern=[[1, P]], channel_multiplier=-1).then_inc(made, 1)

        @block.tensor
        def _(pe):
            pe.wait_ge(made, 3)
            nc.tensor.matmul(ps[0][:, 0:NTL], lower[:], counts[:], start=True, stop=True)
            nc.tensor.matmul(ps[0][:, NTL:2 * NTL], ones[:], counts[:], start=True, stop=True).then_inc(sums, 1)
            pe.wait_ge(chain, 4)
            for q in range(2):
                mm = nc.tensor.transpose(ps[1][:, q * P:(q + 1) * P], endc[:, q * P:(q + 1) * P], ident[:])
            mm.then_inc(sums, 1)

        @block.vector
        def _(dve):
            n = [0]

            def link(ins):
                n[0] += 1
                ins.then_inc(chain, 1)
                dve.wait_ge(chain, n[0])

            dve.wait_ge(sums, 1)
            link(nc.vector.tensor_copy(tot[:], ps[0][:, NTL:2 * NTL]))
            link(nc.vector.tensor_tensor_scan(cum[:], tot[:], tot[:], 0.0, ALU.add, ALU.bypass))
            link(nc.vector.tensor_tensor(cum[:], cum[:], tot[:], ALU.subtract))
            link(nc.vector.tensor_tensor(endc[:], cum[:], ps[0][:, 0:NTL], ALU.add))
            link(nc.vector.tensor_scalar(has[:], counts[:], 1.0, None, ALU.min))
            link(nc.vector.tensor_scalar(tmp[:], endc[:], -1.0, 0.0, ALU.add, ALU.max))
            link(nc.vector.tensor_copy(last_i[:, 0:NTL], tmp[:]))
            link(nc.vector.tensor_tensor(cum[:], endc[:], counts[:], ALU.subtract))
            link(nc.vector.tensor_scalar(tmp[:], has[:], -2.0 * NEDGE, 2.0 * NEDGE, ALU.mult, ALU.add))
            link(nc.vector.tensor_tensor(cum[:], cum[:], tmp[:], ALU.add))
            link(nc.vector.tensor_copy(first_i[:], cum[:]))
            assert n[0] == STEPS
            dve.wait_ge(sums, 2)
            nc.vector.tensor_copy(endt[:], ps[1][:, 0:2 * P].rearrange("p (q l) -> p q l", q=2)
                                  ).then_inc(chain, 1)


def partition_starts(nc, adst, dsts, v):
    with ExitStack() as ctx:
        d0 = ctx.enter_context(nc.sbuf_tensor("v_d0", [P, 1], I32))
        a0 = ctx.enter_context(nc.sbuf_tensor("v_a0", [P, NH], F32))
        loaded, got, fixed = (ctx.enter_context(nc.semaphore(f"v_{n}")) for n in ("loaded", "got", "fixed"))
        block = ctx.enter_context(nc.Block())

        @block.sync
        def _(sp):
            sp.dma_start(d0[:], dsts[:, 0:1], allow_slow_non_contiguous=True).then_inc(loaded, 16)
            sp.wait_ge(got, 16)
            sp.dma_start(v.rearrange("(p f) c -> p f c", p=P)[:, 0], a0[:]).then_inc(fixed, 16)
            sp.wait_ge(fixed, 16)

        @block.gpsimd
        def _(pool):
            pool.wait_ge(loaded, 16)
            nc.gpsimd.indirect_dma_start(a0[:], None, adst, bass.IndirectOffsetOnAxis(ap=d0[:], axis=0)
                                         ).then_inc(got, 16)


COMP = HF + NH


class Chain:

    def __init__(self, eng, sem, base=0):
        self.eng, self.sem, self.base, self.n = eng, sem, base, 0

    def __call__(self, ins):
        self.n += 1
        ins.then_inc(self.sem, 1)
        self.eng.wait_ge(self.sem, self.base + self.n)


F1 = 2 * P
NF1 = F1 // P
K1 = NT // P


def edge_states(nc, passed, rows, srcs, cont, v, res, hn, ys, w):
    U = 64
    TURNS = FE // (2 * U)
    with ExitStack() as ctx:
        sb = lambda n, s, d=F32: ctx.enter_context(nc.sbuf_tensor(f"e_{n}", s, d))
        sem = lambda n: ctx.enter_context(nc.semaphore(f"e_{n}"))
        allidx = sb("allidx", [P, FE + 2 * U], I32)
        idx = sb("idx", [P, 2, U], I32)
        same = sb("same", [P, 2, U])
        vd = sb("vd", [P, 2, U, NH])
        row = sb("row", [P, 2, U, ROW])
        neg = sb("neg", [P, U])
        dst = sb("dst", [P, 1 + U, NH])
        mx = sb("mx", [P, 1 + U, NH])
        score = sb("score", [P, U, NH])
        lrel = sb("lrel", [P, U, NH])
        dx = sb("dx", [P, 2, U, NH])
        ex = sb("ex", [P, 2, U, NH])
        msg = sb("msg", [P, U, NH, NE])
        st = sb("st", [P, 2, U, RES])
        h = sb("h", [P, 2, NT])
        hid = sb("hid", [P, 2, NF1, NT])
        y = sb("y", [P, 2, K1, NE, P])
        w1 = sb("w1", [P, NE, F1])
        w2 = sb("w2", [P, NE, NF1, P])
        b1 = sb("b1", [P, NE, NF1])
        b2 = sb("b2", [P, NE, P])
        bank = [ctx.enter_context(nc.psum_tensor(f"e_bank{i}", [P, NT], F32)) for i in range(6)]
        consts = sem("consts")
        h_loaded = [sem(f"h_loaded{s}") for s in range(2)]
        up_psum, up_ready = sem("up_psum"), sem("up_ready")
        down_psum, y_ready = sem("down_psum"), sem("y_ready")
        y_stored = [sem(f"y_stored{s}") for s in range(2)]
        STEP = NE
        TURN = 2 * STEP
        init = sem("init")
        fload = [sem(f"flags_loaded{s}") for s in range(2)]
        gath = [sem(f"gathered{s}") for s in range(2)]
        idx_ready, slot_free, rows_free = sem("idx_ready"), sem("slot_free"), sem("rows_free")
        chain, dx_ready, ex_ready, st_ready = sem("chain"), sem("dx_ready"), sem("ex_ready"), sem("states_ready")
        stored = [sem(f"stored{s}") for s in range(2)]
        same_c = cont.rearrange("p (n u) -> n p u", u=U)
        v_c = v.rearrange("(p n u) c -> n p u c", p=P, u=U)
        res_c = res.rearrange("(p n u) c -> n p u c", p=P, u=U)
        block = ctx.enter_context(nc.Block())

        @block.sync
        def _(sp):
            sp.dma_start(allidx[:, 0:FE], srcs).then_inc(consts, 16)
            for dst, src in ((w1[:], w["w1"].rearrange("e d f -> d e f")),
                             (w2[:], w["w2"].rearrange("e (f p) d -> p e f d", p=P)),
                             (b1[:], w["b1"]),
                             (b2[:].rearrange("p e d -> p (e d)"), w["b2"].broadcast_to([P, NE * P]))):
                sp.dma_start(dst, src).then_inc(consts, 16)
            with sp.Fori(0, TURNS) as i:
                for s in range(2):
                    sp.dma_start(h[:, s], hn[2 * i + s]).then_inc(h_loaded[s], 16)
                for s in range(2):
                    sp.wait_ge(slot_free, 2 * i + s + 1)
                    sp.dma_start(same[:, s], same_c[2 * i + s]).then_inc(fload[s], 16)
                    sp.dma_start(vd[:, s], v_c[2 * i + s]).then_inc(fload[s], 16)
                sp.wait_ge(up_psum, NF1 * TURN * i + NF1 * TURN)
                sp.sem_inc(passed, 1)

        @block.tensor
        def _(pe):
            pe.wait_ge(consts, 80)
            with pe.Fori(0, TURNS) as i:
                def up(n):
                    s, e = divmod(n, NE)
                    if e == 0:
                        pe.wait_ge(h_loaded[s], 16 * i + 16)
                    for f in range(NF1):
                        m = NF1 * n + f
                        if m >= 3:
                            pe.wait_ge(up_ready, NF1 * TURN * i + (m - 2))
                        nc.tensor.matmul(bank[m % 3][:], w1[:, e, f * P:(f + 1) * P], h[:, s], start=True,
                                         stop=True).then_inc(up_psum, 1)

                def down(n):
                    pe.wait_ge(up_ready, NF1 * TURN * i + NF1 * (n + 1))
                    if n >= 3:
                        pe.wait_ge(y_ready, TURN * i + (n - 2))
                    for k in range(K1):
                        for f in range(NF1):
                            mm = nc.tensor.matmul(bank[3 + n % 3][:, k * P:(k + 1) * P],
                                                  hid[:, n % 2, f, k * P:(k + 1) * P], w2[:, n % NE, f],
                                                  start=(f == 0), stop=(f == NF1 - 1))
                    mm.then_inc(down_psum, 1)

                up(0)
                for n in range(TURN):
                    if n + 1 < TURN:
                        up(n + 1)
                    down(n)
                pe.wait_ge(y_ready, TURN * i + TURN)

        @block.scalar
        def _(act):
            act.wait_ge(consts, 80)
            with act.Fori(0, TURNS) as i:
                for s in range(2):
                    for n in range(s * STEP, (s + 1) * STEP):
                        if n >= 2:
                            act.wait_ge(down_psum, TURN * i + (n - 1))
                        for f in range(NF1):
                            m = NF1 * n + f
                            act.wait_ge(up_psum, NF1 * TURN * i + (m + 1))
                            nc.scalar.activation(hid[:, n % 2, f], bank[m % 3][:], ACT.Gelu,
                                                 bias=b1[:, n % NE, f:f + 1]).then_inc(up_ready, 1)
                    act.wait_ge(y_ready, TURN * i + (s + 1) * STEP)
                    act.dma_start(ys[2 * i + s], y[:, s]).then_inc(y_stored[s], 16)
                    act.wait_ge(dx_ready, 2 * i + s + 1)
                    nc.scalar.activation(ex[:], dx[:], ACT.Exp).then_inc(ex_ready, 1)
                    act.wait_ge(st_ready, 2 * i + s + 1)
                    act.dma_start(res_c[2 * i + s], st[:, s]).then_inc(stored[s], 16)
            for s in range(2):
                act.wait_ge(stored[s], 16 * TURNS)
                act.wait_ge(y_stored[s], 16 * TURNS)

        @block.gpsimd
        def _(pool):
            pool.sem_inc(rows_free, 2)
            with pool.Fori(0, TURNS) as i:
                for s in range(2):
                    pool.wait_ge(rows_free, 2 * i + s + 1)
                    pool.wait_ge(idx_ready, 2 * i + s + 1)
                    pool.sem_inc(passed, 1)
                    for u in range(U):
                        nc.gpsimd.indirect_dma_start(row[:, s, u], None, rows,
                                                     bass.IndirectOffsetOnAxis(ap=idx[:, s, u:u + 1], axis=0)
                                                     ).then_inc(gath[s], 16)
            for s in range(2):
                pool.wait_ge(gath[s], 16 * U * TURNS)

        @block.vector
        def _(dve):
            nc.vector.memset(allidx[:, FE:], 0)
            nc.vector.memset(st[:, 1], 0.0)
            nc.vector.memset(dst[:, U], 0.0)
            nc.vector.memset(mx[:, U], -BIG).then_inc(init, 1)
            dve.sem_inc(slot_free, 2)
            dve.wait_ge(consts, 80)
            for s in range(2):
                nc.vector.tensor_copy(idx[:, s], allidx[:, s * U:(s + 1) * U]).then_inc(idx_ready, 1)
            dve.wait_ge(init, 1)
            K = 13
            with dve.Fori(0, TURNS) as i:
                for s in range(2):
                    n = 2 * i + s
                    link = Chain(dve, chain, K * n)
                    link(nc.vector.tensor_copy(mx[:, 0], mx[:, U]))
                    link(nc.vector.tensor_copy(dst[:, 0], dst[:, U]))
                    dve.wait_ge(fload[s], 32 * i + 32)
                    link(nc.vector.tensor_scalar(neg[:], same[:, s], BIG, -BIG, ALU.mult, ALU.add))
                    for h in range(NH):
                        last = nc.vector.tensor_tensor_scan(dst[:, 1:, h], same[:, s], vd[:, s, :, h],
                                                            dst[:, 0, h:h + 1], ALU.mult, ALU.add)
                    link(last)
                    dve.sem_inc(slot_free, 1)
                    for e in range(NE):
                        m = s * STEP + e
                        dve.wait_ge(down_psum, TURN * i + (m + 1))
                        nc.vector.tensor_tensor(y[:, s, :, e], bank[3 + m % 3][:].rearrange("p (k d) -> p k d", d=P),
                                                b2[:, e].unsqueeze(1).broadcast_to([P, K1, P]),
                                                ALU.add).then_inc(y_ready, 1)
                    dve.wait_ge(gath[s], 16 * U * i + 16 * U)
                    nc.vector.tensor_copy(idx[:, s], allidx[:, bass.ds((2 * i + s + 2) * U, U)]
                                          ).then_inc(idx_ready, 1)
                    link(nc.vector.tensor_tensor(score[:], row[:, s, :, HF:], dst[:, 1:], ALU.add))
                    link(nc.vector.scalar_tensor_tensor(out=lrel[:], in0=score[:], scalar=0.2, in1=score[:],
                                                        op0=ALU.mult, op1=ALU.max))
                    for h in range(NH):
                        last = nc.vector.tensor_tensor_scan(mx[:, 1:, h], neg[:], lrel[:, :, h], mx[:, 0, h:h + 1],
                                                            ALU.add, ALU.max)
                    link(last)
                    link(nc.vector.tensor_tensor(dx[:, 0], mx[:, 0:U], neg[:].unsqueeze(2).broadcast_to([P, U, NH]),
                                                 ALU.add))
                    link(nc.vector.tensor_tensor(dx[:, 0], dx[:, 0], mx[:, 1:], ALU.subtract))
                    link(nc.vector.tensor_tensor(dx[:, 1], lrel[:], mx[:, 1:], ALU.subtract))
                    dve.sem_inc(dx_ready, 1)
                    link(nc.vector.tensor_copy(st[:, s, :, COMP:], mx[:, 1:]))
                    dve.wait_ge(ex_ready, n + 1)
                    link(nc.vector.tensor_tensor(msg[:], row[:, s, :, 0:HF].rearrange("p u (h e) -> p u h e", e=NE),
                                                 ex[:, 1].unsqueeze(3).broadcast_to([P, U, NH, NE]), ALU.mult))
                    dve.sem_inc(rows_free, 1)
                    for c in range(COMP):
                        h = c // NE if c < HF else c - HF
                        add = msg[:, :, c // NE, c % NE] if c < HF else ex[:, 1, :, h]
                        last = nc.vector.tensor_tensor_scan(st[:, s, :, c], ex[:, 0, :, h], add,
                                                            st[:, 1 - s, U - 1, c:c + 1], ALU.mult, ALU.add)
                    link(last)
                    dve.sem_inc(st_ready, 1)
                    assert link.n == K, link.n
                for s in range(2):
                    dve.wait_ge(stored[s], 16 * i + 16)
                    dve.wait_ge(y_stored[s], 16 * i + 16)


def join_partitions(nc, res, dsts, endtab, ident):
    with ExitStack() as ctx:
        sb = lambda n, s, d=F32: ctx.enter_context(nc.sbuf_tensor(f"j_{n}", s, d))
        sem = lambda n: ctx.enter_context(nc.semaphore(f"j_{n}"))
        ps = ctx.enter_context(nc.psum_tensor("j_ps", [P, NT], F32))
        pb = ctx.enter_context(nc.psum_tensor("j_pb", [P, NT], F32))
        ends = sb("ends", [P, RES])
        di = sb("di", [P, 3], I32)
        df = sb("df", [P, 3])
        place = sb("place", [P, 1], I32)
        pf = sb("pf", [P, 4])
        first = sb("first", [P, 1], I32)
        x3 = sb("x3", [P, 3, COMP])
        t3 = sb("t3", [COMP, 3, P])
        neg = sb("neg", [COMP, P])
        mc = sb("mc", [COMP, 1 + P])
        xc = sb("xc", [COMP, 1 + P])
        dx = sb("dx", [COMP, 2, P])
        fr = sb("fr", [P, 2, COMP])
        rr = sb("rr", [P, RES])
        gi = sb("gi", [P, 2], I32)
        d2 = sb("d2", [P, 2, COMP])
        new = sb("new", [P, RES])
        mn = sb("mn", [P, COMP])
        made, loaded, chain, asked, got = sem("made"), sem("loaded"), sem("chain"), sem("asked"), sem("got")
        turned, exps, exped = sem("turned"), sem("exps"), sem("exped")
        block = ctx.enter_context(nc.Block())

        @block.sync
        def _(sp):
            slow = dict(allow_slow_non_contiguous=True)
            sp.dma_start(ends[:], res.rearrange("(p f) c -> p f c", p=P)[:, FE - 1]).then_inc(loaded, 16)
            sp.dma_start(di[:, 0:1], dsts[:, FE - 1:FE], **slow).then_inc(loaded, 16)
            sp.dma_start(di[:, 2:3], dsts[:, 0:1], **slow).then_inc(loaded, 16)
            sp.wait_ge(made, 1)
            sp.dma_start(di[1:P, 1:2], dsts[0:P - 1, FE - 1:FE], **slow).then_inc(loaded, 16)

        @block.gpsimd
        def _(pool):
            nc.gpsimd.memset(di[:, 1:2], -1).then_inc(made, 1)
            nc.gpsimd.iota(first[:], pattern=[[0, 1]], base=0, channel_multiplier=FE).then_inc(made, 1)
            pool.wait_ge(asked, 1)
            nc.gpsimd.indirect_dma_start(place[:], None, endtab, bass.IndirectOffsetOnAxis(ap=gi[:, 0:1], axis=0)
                                         ).then_inc(got, 16)
            pool.wait_ge(asked, 2)
            nc.gpsimd.indirect_dma_start(rr[:], None, res, bass.IndirectOffsetOnAxis(ap=gi[:, 0:1], axis=0)
                                         ).then_inc(got, 16)
            pool.wait_ge(asked, 3)
            nc.gpsimd.indirect_dma_start(res, bass.IndirectOffsetOnAxis(ap=gi[:, 1:2], axis=0), new[:], None,
                                         bounds_check=NEDGE - 1, oob_is_err=False).then_inc(got, 16)
            pool.wait_ge(got, 48)

        @block.tensor
        def _(pe):
            pe.wait_ge(made, 2)
            pe.wait_ge(exps, 1)
            for k in range(3):
                mm = nc.tensor.transpose(ps[0:COMP, k * P:(k + 1) * P], x3[:, k], ident[:])
            mm.then_inc(turned, 1)
            pe.wait_ge(exps, 3)
            nc.tensor.transpose(pb[:, 0:COMP], xc[:, 0:P], ident[0:COMP, 0:COMP])
            nc.tensor.transpose(pb[:, COMP:2 * COMP], mc[:, 0:P], ident[0:COMP, 0:COMP]).then_inc(turned, 1)

        @block.scalar
        def _(act):
            act.wait_ge(exps, 2)
            nc.scalar.activation(dx[:], dx[:], ACT.Exp).then_inc(exped, 1)
            act.wait_ge(exps, 4)
            nc.scalar.activation(d2[:], d2[:], ACT.Exp).then_inc(exped, 1)

        @block.vector
        def _(dve):
            link = Chain(dve, chain)
            by_head = lambda a: a.rearrange("p (h e) -> p h e", e=NE)
            dve.wait_ge(made, 2)
            dve.wait_ge(loaded, 64)
            nc.vector.tensor_copy(gi[:, 0:1], di[:, 2:3]).then_inc(asked, 1)
            link(nc.vector.tensor_copy(df[:], di[:]))
            nc.vector.tensor_copy(x3[:, 0], ends[:, 0:COMP])
            nc.vector.tensor_copy(by_head(x3[:, 1, 0:HF]), ends[:, COMP:].unsqueeze(2).broadcast_to([P, NH, NE]))
            nc.vector.tensor_copy(x3[:, 1, HF:], ends[:, COMP:])
            nc.vector.tensor_copy(x3[:, 2], df[:, 0:1].broadcast_to([P, COMP])).then_inc(exps, 1)
            dve.wait_ge(turned, 1)
            nc.vector.memset(mc[:, 0:1], -BIG)
            nc.vector.memset(xc[:, 0:1], 0.0)
            nc.vector.memset(neg[:, 0:1], 0.0)
            link(nc.vector.tensor_copy(t3[:], ps[0:COMP, 0:3 * P].rearrange("c (k p) -> c k p", k=3)))
            link(nc.vector.tensor_tensor(neg[:, 1:], t3[:, 2, 1:], t3[:, 2, 0:P - 1], ALU.is_equal))
            link(nc.vector.tensor_scalar(neg[:], neg[:], BIG, -BIG, ALU.mult, ALU.add))
            link(nc.vector.tensor_tensor_scan(mc[:, 1:], neg[:], t3[:, 1], -BIG, ALU.add, ALU.max))
            link(nc.vector.tensor_tensor(dx[:, 0], mc[:, 0:P], neg[:], ALU.add))
            link(nc.vector.tensor_tensor(dx[:, 0], dx[:, 0], mc[:, 1:], ALU.subtract))
            nc.vector.tensor_tensor(dx[:, 1], t3[:, 1], mc[:, 1:], ALU.subtract).then_inc(exps, 1)
            dve.wait_ge(exped, 1)
            link(nc.vector.tensor_tensor(dx[:, 1], dx[:, 1], t3[:, 0], ALU.mult))
            nc.vector.tensor_tensor_scan(xc[:, 1:], dx[:, 0], dx[:, 1], 0.0, ALU.mult, ALU.add).then_inc(exps, 1)
            dve.wait_ge(got, 16)
            link(nc.vector.tensor_copy(pf[:, 0:1], place[:]))
            link(nc.vector.tensor_copy(pf[:, 1:2], first[:]))
            link(nc.vector.tensor_scalar(pf[:, 0:1], pf[:, 0:1], -1.0, None, ALU.add))
            nc.vector.tensor_copy(gi[:, 0:1], pf[:, 0:1]).then_inc(asked, 1)
            link(nc.vector.tensor_tensor(pf[:, 1:2], pf[:, 0:1], pf[:, 1:2], ALU.subtract))
            link(nc.vector.tensor_scalar(pf[:, 1:2], pf[:, 1:2], float(FE), None, ALU.is_lt))
            link(nc.vector.tensor_tensor(pf[:, 2:3], df[:, 1:2], df[:, 2:3], ALU.is_equal))
            link(nc.vector.tensor_tensor(pf[:, 1:2], pf[:, 1:2], pf[:, 2:3], ALU.mult))
            link(nc.vector.tensor_scalar(pf[:, 1:2], pf[:, 1:2], -2.0 * NEDGE, 2.0 * NEDGE, ALU.mult, ALU.add))
            link(nc.vector.tensor_tensor(pf[:, 0:1], pf[:, 0:1], pf[:, 1:2], ALU.add))
            nc.vector.tensor_copy(gi[:, 1:2], pf[:, 0:1])
            dve.wait_ge(turned, 2)
            link(nc.vector.tensor_copy(fr[:], pb[:, 0:2 * COMP].rearrange("p (k c) -> p k c", k=2)))
            dve.wait_ge(got, 32)
            nc.vector.tensor_copy(by_head(d2[:, 0, 0:HF]), rr[:, COMP:].unsqueeze(2).broadcast_to([P, NH, NE]))
            link(nc.vector.tensor_copy(d2[:, 0, HF:], rr[:, COMP:]))
            link(nc.vector.tensor_tensor(mn[:], d2[:, 0], fr[:, 1], ALU.max))
            link(nc.vector.tensor_tensor(d2[:, 0], d2[:, 0], mn[:], ALU.subtract))
            nc.vector.tensor_tensor(d2[:, 1], fr[:, 1], mn[:], ALU.subtract).then_inc(exps, 1)
            dve.wait_ge(exped, 2)
            link(nc.vector.tensor_tensor(new[:, 0:COMP], rr[:, 0:COMP], d2[:, 0], ALU.mult))
            link(nc.vector.tensor_tensor(d2[:, 1], d2[:, 1], fr[:, 0], ALU.mult))
            link(nc.vector.tensor_tensor(new[:, 0:COMP], new[:, 0:COMP], d2[:, 1], ALU.add))
            nc.vector.tensor_copy(new[:, COMP:], mn[:, HF:COMP]).then_inc(asked, 1)


def gates_and_output(nc, passed, x3, ys, y, res, rows, adst, ends, ident, w):
    last_i, _, has = ends
    RING = 4
    with ExitStack() as ctx:
        sb = lambda n, s, d=F32: ctx.enter_context(nc.sbuf_tensor(f"f_{n}", s, d))
        sem = lambda n: ctx.enter_context(nc.semaphore(f"f_{n}"))
        bank = [ctx.enter_context(nc.psum_tensor(f"f_bank{i}", [P, NT], F32)) for i in range(2)]
        xo = sb("xo", [P, 2, HW])
        ye = sb("ye", [P, RING, K1, NE, P])
        acc = sb("acc", [P, 2, K1, P])
        g = sb("g", [P, 2, TILES, NE])
        st = sb("st", [P, 2, TILES, RES])
        tr = sb("tr", [P, 2, TILES, ROW])
        td = sb("td", [P, 2, TILES, NH])
        lidx = [sb(f"lidx{s}", [P, TILES], I32) for s in range(2)]
        par = sb("par", [P, 3, HF])
        e4 = sb("e4", [P, NE])
        F4 = lambda n: sb(n, [P, TILES, NH])
        es, mh, mn, d0, d1, den = (F4(n) for n in ("es", "mh", "mn", "d0", "d1", "den"))
        agg = sb("agg", [P, TILES, HF])
        tmp = sb("tmp", [P, TILES, HF])
        hs, hb, mean, var, m1, m2, i1 = (sb(n, [P, TILES]) for n in ("hs", "hb", "mean", "var", "m1", "m2", "i1"))
        made, consts, chain, asks, exped = (sem(n) for n in ("made", "consts", "chain", "asks", "exped"))
        t_loaded = [sem(f"tables_loaded{s}") for s in range(2)]
        got = [sem(f"got{s}") for s in range(2)]
        idx_ready = sem("idx_ready")
        nodes_done = sem("nodes_done")
        x_loaded = [sem(f"image_loaded{s}") for s in range(2)]
        y_loaded = [sem(f"experts_loaded{s}") for s in range(RING)]
        added = sem("added")
        summed = sem("summed")
        turned = sem("turned")
        out_ready = sem("out_ready")
        stored = [sem(f"stored{s}") for s in range(2)]
        STEPS = 2 * LT
        rows_d = rows.rearrange("(i t p) c -> i p t c", p=P, t=TILES)
        adst_d = adst.rearrange("(i t p) c -> i p t c", p=P, t=TILES)
        block = ctx.enter_context(nc.Block())

        @block.sync
        def _(sp):
            for k, n in enumerate(("b_gat", "ln_gamma", "ln_beta")):
                sp.dma_start(par[:, k], w[n].broadcast_to([P, HF])).then_inc(consts, 16)
            with sp.Fori(0, B // 2) as i:
                for r in range(STEPS):
                    if r % LT == 0:
                        s = r // LT
                        sp.wait_ge(nodes_done, 2 * i + s + 1)
                        sp.dma_start(tr[:, s], rows_d[2 * i + s]).then_inc(t_loaded[s], 16)
                        sp.dma_start(td[:, s], adst_d[2 * i + s]).then_inc(t_loaded[s], 16)
                    sp.wait_ge(summed, STEPS * i + (r + 1))
                    sp.dma_start(ye[:, r % RING], ys[STEPS * i + r]).then_inc(y_loaded[r % RING], 16)

        @block.gpsimd
        def _(pool):
            nc.gpsimd.iota(e4[:], pattern=[[1, NE]], base=-NE, channel_multiplier=0,
                           allow_small_or_imprecise_dtypes=True).then_inc(made, 1)
            with pool.Fori(0, B // 2) as i:
                for s in range(2):
                    pool.wait_ge(nodes_done, 2 * i + s + 1)
                    pool.wait_ge(idx_ready, 2 * i + s + 1)
                    pool.sem_inc(passed, 1)
                    for t in range(TILES):
                        nc.gpsimd.indirect_dma_start(st[:, s, t], None, res,
                                                     bass.IndirectOffsetOnAxis(ap=lidx[s][:, t:t + 1], axis=0)
                                                     ).then_inc(got[s], 16)
            for s in range(2):
                pool.wait_ge(got[s], 16 * TILES * (B // 2))

        @block.tensor
        def _(pe):
            with pe.Fori(0, B // 2) as i:
                for r in range(STEPS):
                    pe.wait_ge(summed, RING + STEPS * i + (r + 1))
                    if r >= 2:
                        pe.wait_ge(out_ready, STEPS * i + (r - 1))
                    for k in range(K1):
                        mm = nc.tensor.transpose(bank[r % 2][:, k * P:(k + 1) * P], acc[:, r % 2, k], ident[:])
                    mm.then_inc(turned, 1)
                pe.wait_ge(out_ready, STEPS * i + STEPS)

        @block.scalar
        def _(act):
            with act.Fori(0, B // 2) as i:
                for s in range(2):
                    act.dma_start(xo[:, s], x3[2 * i + s]).then_inc(x_loaded[s], 16)
                for s in range(2):
                    n = 2 * i + s
                    act.wait_ge(asks, 3 * n + 1)
                    nc.scalar.activation(d0[:], d0[:], ACT.Exp)
                    nc.scalar.activation(d1[:], d1[:], ACT.Exp).then_inc(exped, 1)
                    act.wait_ge(asks, 3 * n + 2)
                    nc.scalar.activation(var[:], var[:], ACT.Sqrt).then_inc(exped, 1)
                    act.wait_ge(asks, 3 * n + 3)
                    nc.scalar.activation(m2[:], m2[:], ACT.Exp).then_inc(exped, 1)
                    act.wait_ge(out_ready, STEPS * i + LT * (s + 1))
                    act.dma_start(y[2 * i + s], xo[:, s]).then_inc(stored[s], 16)
                for s in range(2):
                    act.wait_ge(stored[s], 16 * i + 16)
                    act.sem_inc(passed, 1)

        @block.vector
        def _(dve):
            tt, ts = nc.vector.tensor_tensor, nc.vector.tensor_scalar
            A4 = [P, TILES, NH]
            A16 = [P, TILES, HF]
            per_node = lambda a, s=A4: a[:].unsqueeze(2).broadcast_to(s)
            heads = lambda a: a.rearrange("p t (h e) -> p t h e", e=NE)
            bh = lambda a: a[:].unsqueeze(3).broadcast_to([P, TILES, NH, NE])
            by_feature = lambda k: par[:, k].unsqueeze(1).broadcast_to(A16)
            LINKS = 45

            def index(n, s):
                nc.vector.tensor_copy(lidx[s][:], last_i[:, bass.ts(n, TILES)]).then_inc(idx_ready, 1)

            dve.sem_inc(summed, RING)
            dve.sem_inc(nodes_done, 2)
            nc.vector.memset(last_i[:, NTL:], 0).then_inc(made, 1)
            index(0, 0)
            index(1, 1)
            dve.wait_ge(made, 2)
            dve.wait_ge(consts, 48)
            with dve.Fori(0, B // 2) as i:
                def share(r, e):
                    s, t = divmod(r, LT)
                    if e == 0:
                        dve.wait_ge(y_loaded[r % RING], 16 * (STEPS // RING) * i + 16 * (r // RING + 1))
                        if r >= 2:
                            dve.wait_ge(turned, STEPS * i + (r - 1))
                    else:
                        dve.wait_ge(added, (NE - 1) * STEPS * i + ((NE - 1) * r + e))
                    for k in range(K1):
                        gate = g[:, s, K1 * t + k, e:e + 1]
                        if e == 0:
                            last = nc.vector.tensor_scalar(acc[:, r % 2, k], ye[:, r % RING, k, e], gate, None,
                                                           ALU.mult)
                        else:
                            last = nc.vector.scalar_tensor_tensor(out=acc[:, r % 2, k], in0=ye[:, r % RING, k, e],
                                                                  scalar=gate, in1=acc[:, r % 2, k],
                                                                  op0=ALU.mult, op1=ALU.add)
                    last.then_inc(added if e < NE - 1 else summed, 1)

                def out(r):
                    s, t = divmod(r, LT)
                    if t == 0:
                        dve.wait_ge(x_loaded[s], 16 * i + 16)
                    dve.wait_ge(turned, STEPS * i + (r + 1))
                    c = slice(t * NT, (t + 1) * NT)
                    nc.vector.tensor_tensor(xo[:, s, c], xo[:, s, c], bank[r % 2][:], ALU.add).then_inc(out_ready, 1)

                def node_gates(s):
                    n = 2 * i + s
                    link = Chain(dve, chain, LINKS * n)
                    link(nc.vector.tensor_copy(hs[:], has[:, bass.ts(n, TILES)]))
                    dve.wait_ge(t_loaded[s], 32 * i + 32)
                    link(tt(es[:], tr[:, s, :, HF:], td[:, s], ALU.add))
                    link(nc.vector.scalar_tensor_tensor(out=es[:], in0=es[:], scalar=0.2, in1=es[:], op0=ALU.mult,
                                                        op1=ALU.max))
                    link(ts(hb[:], hs[:], BIG, -BIG, ALU.mult, ALU.add))
                    dve.wait_ge(got[s], 16 * TILES * i + 16 * TILES)
                    index(n + 2, s)
                    link(tt(mh[:], st[:, s, :, COMP:], per_node(hs), ALU.mult))
                    link(tt(mh[:], mh[:], per_node(hb), ALU.add))
                    link(tt(mn[:], mh[:], es[:], ALU.max))
                    link(tt(d0[:], mh[:], mn[:], ALU.subtract))
                    tt(d1[:], es[:], mn[:], ALU.subtract).then_inc(asks, 1)
                    dve.wait_ge(exped, 3 * n + 1)
                    link(tt(den[:], st[:, s, :, HF:COMP], d0[:], ALU.mult))
                    link(tt(den[:], den[:], d1[:], ALU.add))
                    link(ts(den[:], den[:], 1e-16, None, ALU.add))
                    link(nc.vector.reciprocal(den[:], den[:]))
                    link(tt(heads(agg[:]), heads(st[:, s, :, 0:HF]), bh(d0), ALU.mult))
                    link(tt(heads(tmp[:]), heads(tr[:, s, :, 0:HF]), bh(d1), ALU.mult))
                    link(tt(agg[:], agg[:], tmp[:], ALU.add))
                    link(tt(heads(agg[:]), heads(agg[:]), bh(den), ALU.mult))
                    link(tt(agg[:], agg[:], by_feature(0), ALU.add))
                    link(nc.vector.tensor_reduce(mean[:], agg[:], AX.X, ALU.add))
                    link(ts(mean[:], mean[:], 1.0 / HF, None, ALU.mult))
                    link(tt(agg[:], agg[:], per_node(mean, A16), ALU.subtract))
                    link(tt(tmp[:], agg[:], agg[:], ALU.mult))
                    link(nc.vector.tensor_reduce(var[:], tmp[:], AX.X, ALU.add))
                    ts(var[:], var[:], 1.0 / HF, 1e-5, ALU.mult, ALU.add).then_inc(asks, 1)
                    dve.wait_ge(exped, 3 * n + 2)
                    link(nc.vector.reciprocal(var[:], var[:]))
                    link(tt(agg[:], agg[:], per_node(var, A16), ALU.mult))
                    link(tt(agg[:], agg[:], by_feature(1), ALU.mult))
                    link(tt(agg[:], agg[:], by_feature(2), ALU.add))
                    link(nc.vector.tensor_reduce(es[:], agg[:].rearrange("p t (h e) -> p t e h", e=NE), AX.X, ALU.add))
                    link(ts(es[:], es[:], 1.0 / NH, None, ALU.mult))
                    be = e4[:].unsqueeze(1).broadcast_to(A4)

                    def pick(scores, top, hot):
                        link(nc.vector.tensor_reduce(top[:], scores[:], AX.X, ALU.max))
                        link(tt(hot[:], scores[:], per_node(top), ALU.is_equal))
                        link(tt(hot[:], hot[:], be, ALU.mult))
                        link(nc.vector.tensor_reduce(i1[:], hot[:], AX.X, ALU.min))
                        link(tt(hot[:], be, per_node(i1), ALU.is_equal))

                    pick(es, m1, d0)
                    link(nc.vector.scalar_tensor_tensor(out=mh[:], in0=d0[:], scalar=-BIG, in1=es[:], op0=ALU.mult,
                                                        op1=ALU.add))
                    pick(mh, m2, d1)
                    tt(m2[:], m2[:], m1[:], ALU.subtract).then_inc(asks, 1)
                    dve.wait_ge(exped, 3 * n + 3)
                    link(ts(m1[:], m2[:], 1.0, None, ALU.add))
                    link(nc.vector.reciprocal(m1[:], m1[:]))
                    link(tt(m2[:], m2[:], m1[:], ALU.mult))
                    link(tt(d0[:], d0[:], per_node(m1), ALU.mult))
                    link(tt(d1[:], d1[:], per_node(m2), ALU.mult))
                    link(tt(g[:, s], d0[:], d1[:], ALU.add))
                    assert link.n == LINKS, link.n
                    dve.sem_inc(nodes_done, 1)

                for s in range(2):
                    node_gates(s)
                    for r in range(s * LT, (s + 1) * LT):
                        for e in range(NE):
                            share(r, e)
                        if r % LT:
                            out(r - 1)
                    out((s + 1) * LT - 1)


def metaformer(nc, x, y, w):
    scratch = lambda n, s, d=F32: nc.dram_tensor(n, s, d, kind="Internal").ap()
    x1, x3 = scratch("x1_dram", (B + 1, P, HW)), scratch("x3_dram", (B, P, HW))
    hn = scratch("hn_dram", (B * LT, P, NT))
    ys = scratch("ys_dram", (B * LT, P, K1, NE, P))
    xb, yb = scratch("xb_dram", (SLOTS, P)), scratch("yb_dram", (SLOTS, P))
    rows, adst = scratch("rows_dram", (M, ROW)), scratch("adst_dram", (M, NH))
    srcs, dsts = scratch("srcs_dram", (P, FE), I32), scratch("dsts_dram", (P, FE), I32)
    cont = scratch("cont_dram", (P, FE))
    endtab = scratch("endtab_dram", (N, 1), I32)
    v = scratch("v_dram", (NEDGE, NH))
    res = scratch("res_dram", (NEDGE, RES))
    with ExitStack() as ctx:
        keep = lambda n, s, d: ctx.enter_context(nc.sbuf_tensor(f"keep_{n}", s, d))
        ln = LayerNorm(nc, keep, lambda n: ctx.enter_context(nc.semaphore(n)), "ln")
        made = ctx.enter_context(nc.semaphore("ident_made"))
        ident = keep("ident", [P, P], F32)
        with nc.Block() as block:
            @block.gpsimd
            def _(pool):
                nc.gpsimd.memset(ident[:], 0.0).then_inc(made, 1)
                pool.wait_ge(made, 1)
                nc.gpsimd.affine_select(out=ident[:], in_=ident[:], compare_op=ALU.not_equal, fill=1.0, base=0,
                                        pattern=[[-1, P]], channel_multiplier=1).then_inc(made, 1)
                pool.wait_ge(made, 2)
        slots = keep("slots", [P, NTL + 2 * TILES], I32)
        gates0 = keep("gates0", [P, NTL + TILES], F32)
        counts = keep("counts", [P, NTL], F32)
        passed = ctx.enter_context(nc.semaphore("passed"))
        sort_edges(nc, w["src"], w["dst"], srcs, dsts, cont, ident)
        involution_and_routing(nc, passed, x, x1, xb, (slots, gates0), (w["dst"], counts), ln, ident, w["involution"])
        experts(nc, passed, xb, yb, v, (w["dst"], counts), ident, w["experts"])
        last_i, first_i = keep("last_i", [P, NTL + 2 * TILES], I32), keep("first_i", [P, NTL], I32)
        has = keep("has", [P, NTL], F32)
        node_ranges(nc, counts, (last_i, first_i, has), endtab, ident)
        combine_and_conv(nc, passed, x1, yb, x3, hn, rows, adst, v, first_i, (slots, gates0), ln, ident,
                         w["conv"])
        partition_starts(nc, adst, dsts, v)
        edge_states(nc, passed, rows, srcs, cont, v, res, hn, ys, w["gelu"])
        join_partitions(nc, res, dsts, endtab, ident)
        gates_and_output(nc, passed, x3, ys, y, res, rows, adst, (last_i, first_i, has), ident, w["gates"])



def kernel(**inputs):
    import concourse.bacc as bacc
    from concourse.bass_utils import run_bass_kernel_spmd

    a = {n: np.asarray(v) for n, v in inputs.items()}
    l0, l1, f0, f1 = (lambda n, k=k: a[k + n] for k in ("L0_conv_", "L1_conv_", "L0_ffn_", "L1_ffn_"))
    row = lambda v: v.reshape(1, -1)
    weights = {
        "involution": {"w1t": l0("w1").T, "w2t": l0("w2").T, "b2": row(l0("b2")),
                       "bn": np.stack([l0(n) for n in ("b1", "bn_gamma", "bn_beta", "bn_mean", "bn_var")], axis=1),
                       "gate_w": f0("gate_w"), "gate_b": row(f0("gate_b"))},
        "experts": {"w1": f0("w1"), "w2": f0("w2"), "b1": f0("b1").reshape(E0, F0 // P, P).transpose(0, 2, 1),
                    "b2": f0("b2").reshape(E0, 1, P)},
        "conv": {"conv": l1("weight").transpose(1, 2, 3, 0).reshape(P, K3 * K3, P),
                 "conv_b": l1("bias").reshape(P, 1), "gat": f1("W_gat"),
                 "att_src": row(f1("att_src")), "att_dst": row(f1("att_dst"))},
        "gates": {n: row(f1(n)) for n in ("b_gat", "ln_gamma", "ln_beta")},
        "gelu": {"w1": f1("W1"), "w2": f1("W2"), "b1": f1("b1").reshape(NE, 2, P).transpose(2, 0, 1),
                 "b2": row(f1("b2"))},
    }
    nc = bacc.Bacc("TRN2", target_bir_lowering=False, num_devices=1)
    arrays = {}

    def put(name, v):
        arrays[name] = np.ascontiguousarray(v)
        return nc.dram_tensor(name, arrays[name].shape, mybir.dt.from_np(arrays[name].dtype),
                              kind="ExternalInput").ap()

    w = {stage: {n: put(f"in_{stage}_{n}", v) for n, v in group.items()} for stage, group in weights.items()}
    edges = f1("edge_index").astype(np.int32)
    w["src"], w["dst"] = put("in_src", edges[0].reshape(P, FE)), put("in_dst", edges[1].reshape(P, FE))
    x = put("in_x", a["x"].reshape(B, P, HW))
    y = nc.dram_tensor("out_y", (B, P, HW), F32, kind="ExternalOutput").ap()
    metaformer(nc, x, y, w)
    r = run_bass_kernel_spmd(nc, [arrays], core_ids=[0])
    return r.results[0]["out_y"].reshape(B, P, H, W)
```
